# Optimizing a Trainium2 kernel written in Bass

```python
import numpy as np
import jax
import jax.numpy as jnp

def _softmax(x, axis=-1):
    return jax.nn.softmax(x, axis=axis)

def _gelu(x):
    return jax.nn.gelu(x, approximate=True)

def _silu(x):
    return jax.nn.silu(x)

def _sigmoid(x):
    return jax.nn.sigmoid(x)

def _layernorm(x, axis=-1, eps=1e-05):
    m = jnp.mean(x, axis=axis, keepdims=True)
    v = jnp.var(x, axis=axis, keepdims=True)
    return (x - m) / jnp.sqrt(v + eps)

def _scatter_add(tgt, idx, src, axis=0):
    return tgt.at[idx].add(src)

def _segment_sum(src, seg, n):
    return jax.ops.segment_sum(src, seg, n)
kernel_name = 'mk_decoder_preln_d4_seqx_r4_86618c'

def setup_inputs(seed: int=0):
    np.random.seed(seed)
    _w = jnp.asarray

    def _rec_inputs():
        import jax
        import jax.numpy as jnp
        _rk = jax.random.key(seed)
        x = 0.0002279 + 0.9999 * jax.random.normal(jax.random.fold_in(_rk, 1), (2, 1024, 256), jnp.float32)
        _lenS = 1024 - jax.random.randint(jax.random.fold_in(_rk, 7), (2,), 0, max(1, 1024 // 4) + 1, jnp.int32)
        _lenS2 = 154 - jax.random.randint(jax.random.fold_in(_rk, 8), (2,), 0, max(1, 154 // 4) + 1, jnp.int32)
        _ctx_1024P = jax.random.normal(jax.random.fold_in(_rk, 11), (2, 16, 256), jnp.float32)
        _ctx_1024c = jax.random.dirichlet(jax.random.fold_in(_rk, 511), 0.3 * jnp.ones((16,), jnp.float32), (2, 154))
        _ctx_1024t = jnp.einsum('bsk,bkd->bsd', _ctx_1024c, _ctx_1024P)
        _ctx_1024t = _ctx_1024t * jax.lax.rsqrt(jnp.mean(jnp.square(_ctx_1024t)) + 1e-12) * 0.953939
        ctx_1024 = -7.10856e-05 + 0.999911 * (_ctx_1024t + 0.3 * jax.random.normal(jax.random.fold_in(_rk, 611), (2, 154, 256), jnp.float32))
        _validS = jnp.arange(1024)[None, :] < _lenS[:, None]
        _validS2 = jnp.arange(154)[None, :] < _lenS2[:, None]
        _causal = jnp.tril(jnp.ones((1024, 1024), dtype=bool))
        mask_BxS2_bf1 = jnp.ones((2, 154), dtype=bool)
        mask_Bx1xSxS2_if1 = jnp.where(jnp.ones((2, 1, 1024, 154), dtype=bool), 1, 0).astype(jnp.int32)
        return (x, ctx_1024, mask_BxS2_bf1, mask_Bx1xSxS2_if1)
    x, ctx_1024, mask_BxS2_bf1, mask_Bx1xSxS2_if1 = _rec_inputs()

    def _L0_attn_setup():
        import jax, jax.numpy as jnp
        import numpy as np
        DIM = 256
        N_HEADS = 16
        HEAD_DIM = DIM // N_HEADS
        D_LATENT = 64
        B, T = (1, 1024)
        key = jax.random.key(seed)
        ks = jax.random.split(key, 6)
        s = 0.02
        return {'x': jax.random.normal(ks[0], (B, T, DIM), dtype=jnp.float32), 'W_DKV': jax.random.normal(ks[1], (DIM, D_LATENT), dtype=jnp.float32) * s, 'W_UK': jax.random.normal(ks[2], (D_LATENT, DIM), dtype=jnp.float32) * s, 'W_UV': jax.random.normal(ks[3], (D_LATENT, DIM), dtype=jnp.float32) * s, 'W_UQ': jax.random.normal(ks[4], (DIM, DIM), dtype=jnp.float32) * s, 'W_O': jax.random.normal(ks[5], (DIM, DIM), dtype=jnp.float32) * s}
    _L0_attn_all = _L0_attn_setup()
    _L0_attn_in = {k: v for k, v in _L0_attn_all.items() if k in ('W_DKV', 'W_UK', 'W_UV', 'W_UQ', 'W_O')}
    del _L0_attn_all

    def _L0_xattn_setup():
        import jax, jax.numpy as jnp
        import numpy as np
        DIM = 256
        HEADS = 16
        DIM_HEAD = 64
        INNER = HEADS * DIM_HEAD
        B, F, Q = (16, 1024, 64)
        EPS = 1e-05
        SCALE = DIM_HEAD ** (-0.5)

        def _layernorm(x, gamma, beta):
            mu = jnp.mean(x, axis=-1, keepdims=True)
            var = jnp.var(x, axis=-1, keepdims=True)
            return (x - mu) * jax.lax.rsqrt(var + EPS) * gamma + beta
        key = jax.random.key(seed)
        ks = jax.random.split(key, 8)
        features = jax.random.normal(ks[0], (B, F, DIM), dtype=jnp.float32)
        masks = jnp.ones((B, F), dtype=bool)
        latents = jax.random.normal(ks[1], (B, Q, DIM), dtype=jnp.float32)
        Wq = jax.random.normal(ks[2], (DIM, INNER), dtype=jnp.float32) / np.sqrt(DIM)
        Wk = jax.random.normal(ks[3], (DIM, INNER), dtype=jnp.float32) / np.sqrt(DIM)
        Wv = jax.random.normal(ks[4], (DIM, INNER), dtype=jnp.float32) / np.sqrt(DIM)
        Wo = jax.random.normal(ks[5], (INNER, DIM), dtype=jnp.float32) / np.sqrt(INNER)
        gm = jnp.ones((DIM,), jnp.float32)
        bm = jnp.zeros((DIM,), jnp.float32)
        gl = jnp.ones((DIM,), jnp.float32)
        bl = jnp.zeros((DIM,), jnp.float32)
        return {'features': features, 'masks': masks, 'latents': latents, 'gm': gm, 'bm': bm, 'gl': gl, 'bl': bl, 'Wq': Wq, 'Wk': Wk, 'Wv': Wv, 'Wo': Wo}
    _L0_xattn_all = _L0_xattn_setup()
    _L0_xattn_in = {k: v for k, v in _L0_xattn_all.items() if k in ('gm', 'bm', 'gl', 'bl', 'Wq', 'Wk', 'Wv', 'Wo')}
    del _L0_xattn_all

    def _L0_ffn_setup():
        import jax, jax.numpy as jnp
        import numpy as np
        B, S, H, E = (4, 512, 256, 8)
        key = jax.random.key(seed)
        k1, k2, k3 = jax.random.split(key, 3)
        scale_w = 1.0 / np.sqrt(H)
        return {'x': jax.random.normal(k1, (B, S, H), dtype=jnp.float32), 'router_w': jax.random.normal(k2, (H, E), dtype=jnp.float32) * scale_w, 'router_b': jnp.zeros((E,), dtype=jnp.float32), 'expert_w': jax.random.normal(k3, (E, H, H), dtype=jnp.float32) * scale_w, 'expert_b': jnp.zeros((E, H), dtype=jnp.float32)}
    _L0_ffn_all = _L0_ffn_setup()
    _L0_ffn_in = {k: v for k, v in _L0_ffn_all.items() if k in ('router_w', 'router_b', 'expert_w', 'expert_b')}
    del _L0_ffn_all

    def _L1_attn_setup():
        import jax, jax.numpy as jnp
        import numpy as np
        N, B, C = (72, 64, 256)
        H = 16
        P_PER_TASK = 4
        NUM_TASKS = 7

        def _prompt_mask(n, p, num_tasks, dtype):
            P = (num_tasks + 1) * p
            r = jnp.arange(n)[:, None]
            c = jnp.arange(n)[None, :]
            blocked = (c < P) & ~((r < P) & (r >= c // p * p))
            return jnp.where(blocked, -jnp.inf, 0.0).astype(dtype)
        key = jax.random.key(seed)
        k1, k2, k3 = jax.random.split(key, 3)
        x = jax.random.normal(k1, (N, B, C), dtype=jnp.float32)
        Wqkv = jax.random.normal(k2, (3 * C, C), dtype=jnp.float32) * 0.02
        bqkv = jnp.zeros((3 * C,), dtype=jnp.float32)
        Wproj = jax.random.normal(k3, (C, C), dtype=jnp.float32) * 0.02
        bproj = jnp.zeros((C,), dtype=jnp.float32)
        return {'x': x, 'Wqkv': Wqkv, 'bqkv': bqkv, 'Wproj': Wproj, 'bproj': bproj}
    _L1_attn_all = _L1_attn_setup()
    _L1_attn_in = {k: v for k, v in _L1_attn_all.items() if k in ('Wqkv', 'bqkv', 'Wproj', 'bproj')}
    del _L1_attn_all

    def _L1_xattn_setup():
        import jax, jax.numpy as jnp
        import numpy as np
        D_MODEL = 256
        N_HEADS = 16
        key = jax.random.key(seed)
        ks = jax.random.split(key, 11)
        B, S = (4, 512)
        sc = 1.0 / np.sqrt(D_MODEL)
        inp = {'Q': jax.random.normal(ks[0], (B, S, D_MODEL), jnp.float32), 'K': jax.random.normal(ks[1], (B, S, D_MODEL), jnp.float32), 'V': jax.random.normal(ks[2], (B, S, D_MODEL), jnp.float32), 'Wq': jax.random.normal(ks[3], (D_MODEL, D_MODEL), jnp.float32) * sc, 'bq': jnp.zeros((D_MODEL,), jnp.float32), 'Wk': jax.random.normal(ks[4], (D_MODEL, D_MODEL), jnp.float32) * sc, 'bk': jnp.zeros((D_MODEL,), jnp.float32), 'Wv': jax.random.normal(ks[5], (D_MODEL, D_MODEL), jnp.float32) * sc, 'bv': jnp.zeros((D_MODEL,), jnp.float32), 'Wo': jax.random.normal(ks[6], (D_MODEL, D_MODEL), jnp.float32) * sc, 'bo': jnp.zeros((D_MODEL,), jnp.float32)}
        return inp
    _L1_xattn_all = _L1_xattn_setup()
    _L1_xattn_in = {k: v for k, v in _L1_xattn_all.items() if k in ('Wq', 'bq', 'Wk', 'bk', 'Wv', 'bv', 'Wo', 'bo')}
    del _L1_xattn_all

    def _L1_ffn_setup():
        import jax, jax.numpy as jnp
        import numpy as np
        DIM = 256
        HIDDEN = 768
        SCALE = 1.0 / 127.0

        def _dequant(w_int, dtype):
            return w_int.astype(dtype) * jnp.asarray(SCALE, dtype)
        key = jax.random.key(seed)
        k_x, k_g, k_u, k_d = jax.random.split(key, 4)
        x = jax.random.normal(k_x, (4, 512, DIM), dtype=jnp.float32)
        w_gate = jax.random.randint(k_g, (HIDDEN, DIM), -127, 128, dtype=jnp.int32)
        w_up = jax.random.randint(k_u, (HIDDEN, DIM), -127, 128, dtype=jnp.int32)
        w_down = jax.random.randint(k_d, (DIM, HIDDEN), -127, 128, dtype=jnp.int32)
        return {'x': x, 'w_gate': w_gate, 'w_up': w_up, 'w_down': w_down}
    _L1_ffn_all = _L1_ffn_setup()
    _L1_ffn_in = {k: v for k, v in _L1_ffn_all.items() if k in ('w_gate', 'w_up', 'w_down')}
    del _L1_ffn_all

    def _L2_attn_setup():
        import jax, jax.numpy as jnp
        import numpy as np
        D_MODEL = 256
        D_STATE = 16
        D_CONV = 4
        EXPAND = 2
        D_INNER = EXPAND * D_MODEL
        DT_RANK = (D_MODEL + 15) // 16
        BATCH = 2
        SEQ = 256

        def _mamba(x, in_proj_w, conv_w, conv_b, x_proj_w, dt_proj_w, dt_proj_b, A_log, D, out_proj_w):
            L = x.shape[1]
            xz = x @ in_proj_w
            xc, z = jnp.split(xz, 2, axis=-1)
            xp = jnp.pad(xc, ((0, 0), (D_CONV - 1, 0), (0, 0)))
            xc = sum((conv_w[:, i] * xp[:, i:i + L, :] for i in range(D_CONV))) + conv_b
            xc = jax.nn.silu(xc)
            dbl = xc @ x_proj_w
            dt = dbl[..., :DT_RANK]
            Bm = dbl[..., DT_RANK:DT_RANK + D_STATE]
            Cm = dbl[..., DT_RANK + D_STATE:]
            delta = jax.nn.softplus(dt @ dt_proj_w + dt_proj_b)
            A = -jnp.exp(A_log)

            def step(h, t):
                d_t, B_t, C_t, u_t = t
                h = h * jnp.exp(d_t[..., None] * A) + (d_t * u_t)[..., None] * B_t[:, None, :]
                return (h, jnp.einsum('bdn,bn->bd', h, C_t))
            h0 = jnp.zeros((x.shape[0], D_INNER, D_STATE), x.dtype)
            xs = (delta.transpose(1, 0, 2), Bm.transpose(1, 0, 2), Cm.transpose(1, 0, 2), xc.transpose(1, 0, 2))
            _, ys = jax.lax.scan(step, h0, xs)
            y = ys.transpose(1, 0, 2) + xc * D
            y = y * jax.nn.silu(z)
            return y @ out_proj_w
        key = jax.random.key(seed)
        k = jax.random.split(key, 12)
        s = 0.02
        f32 = jnp.float32
        return {'x': jax.random.normal(k[0], (BATCH, SEQ, D_MODEL), f32), 'in_proj_w': jax.random.normal(k[1], (D_MODEL, 2 * D_INNER), f32) * s, 'conv_w': jax.random.normal(k[2], (D_INNER, D_CONV), f32) * s, 'conv_b': jnp.zeros((D_INNER,), f32), 'x_proj_w': jax.random.normal(k[3], (D_INNER, DT_RANK + 2 * D_STATE), f32) * s, 'dt_proj_w': jax.random.normal(k[4], (DT_RANK, D_INNER), f32) * s, 'dt_proj_b': jax.random.uniform(k[5], (D_INNER,), f32, -4.6, -2.3), 'A_log': jnp.log(jnp.tile(jnp.arange(1, D_STATE + 1, dtype=f32), (D_INNER, 1))), 'D': jnp.ones((D_INNER,), f32), 'out_proj_w': jax.random.normal(k[6], (D_INNER, D_MODEL), f32) * s, 'ln_g': jnp.ones((D_MODEL,), f32), 'ln_b': jnp.zeros((D_MODEL,), f32), 'ff_w1': jax.random.normal(k[7], (D_MODEL, 4 * D_MODEL), f32) * s, 'ff_b1': jnp.zeros((4 * D_MODEL,), f32), 'ff_w2': jax.random.normal(k[8], (4 * D_MODEL, D_MODEL), f32) * s, 'ff_b2': jnp.zeros((D_MODEL,), f32)}
    _L2_attn_all = _L2_attn_setup()
    _L2_attn_in = {k: v for k, v in _L2_attn_all.items() if k in ('in_proj_w', 'conv_w', 'conv_b', 'x_proj_w', 'dt_proj_w', 'dt_proj_b', 'A_log', 'D', 'out_proj_w', 'ln_g', 'ln_b', 'ff_w1', 'ff_b1', 'ff_w2', 'ff_b2')}
    del _L2_attn_all

    def _L2_xattn_setup():
        import jax, jax.numpy as jnp
        import numpy as np
        B, L_ENC, L_DEC, D = (16, 128, 128, 256)
        key = jax.random.key(seed)
        k1, k2, k3, k4, k5, k6 = jax.random.split(key, 6)
        encoder_hc = jax.random.normal(k1, (B, L_ENC, D), dtype=jnp.float32)
        decoder_hq = jax.random.normal(k2, (B, L_DEC, D), dtype=jnp.float32)
        w_sim = jax.random.normal(k3, (3 * D,), dtype=jnp.float32) * 0.02
        b_sim = jax.random.normal(k4, (1,), dtype=jnp.float32) * 0.02
        W_qv = jax.random.normal(k5, (4 * D, D), dtype=jnp.float32) * 0.02
        b_qv = jax.random.normal(k6, (D,), dtype=jnp.float32) * 0.02
        return {'encoder_hc': encoder_hc, 'decoder_hq': decoder_hq, 'w_sim': w_sim, 'b_sim': b_sim, 'W_qv': W_qv, 'b_qv': b_qv}
    _L2_xattn_all = _L2_xattn_setup()
    _L2_xattn_in = {k: v for k, v in _L2_xattn_all.items() if k in ('w_sim', 'b_sim', 'W_qv', 'b_qv')}
    del _L2_xattn_all

    def _L2_ffn_setup():
        import jax, jax.numpy as jnp
        import numpy as np
        EPS = 1e-05
        TOP_K = 2

        def _rmsnorm(x, w):
            xf = x.astype(jnp.float32)
            rms = jax.lax.rsqrt(jnp.mean(xf * xf, axis=-1, keepdims=True) + EPS)
            return (xf * rms).astype(x.dtype) * w

        def _attention(x, wq, wk, wv, wo, num_heads=16):
            B, S, H = x.shape
            D = H // num_heads
            q = (x @ wq.T).reshape(B, S, num_heads, D)
            k = (x @ wk.T).reshape(B, S, num_heads, D)
            v = (x @ wv.T).reshape(B, S, num_heads, D)
            scale = 1.0 / jnp.sqrt(jnp.float32(D)).astype(x.dtype)
            scores = jnp.einsum('bqhd,bkhd->bhqk', q, k) * scale
            probs = jax.nn.softmax(scores, axis=-1)
            out = jnp.einsum('bhqk,bkhd->bqhd', probs, v).reshape(B, S, H)
            return out @ wo.T

        def _moe(x, gate_w, w1, w2, w3):
            B, S, H = x.shape
            xf = x.reshape(-1, H)
            logits = xf @ gate_w.T
            rw, sel = jax.lax.top_k(logits, TOP_K)
            rw = jax.nn.softmax(rw.astype(jnp.float32), axis=-1).astype(x.dtype)
            E = gate_w.shape[0]
            out = jnp.zeros_like(xf)
            for e in range(E):
                we = jnp.sum(jnp.where(sel == e, rw, 0.0), axis=-1)
                h = jax.nn.silu(xf @ w1[e].T) * (xf @ w3[e].T)
                out = out + h @ w2[e].T * we[:, None]
            return out.reshape(B, S, H)
        key = jax.random.key(seed)
        ks = jax.random.split(key, 10)
        H, I, E, NH = (256, 512, 8, 16)
        B, S = (2, 512)
        s = 0.02
        return {'x': jax.random.normal(ks[0], (B, S, H), jnp.float32), 'ln1_w': jnp.ones((H,), jnp.float32), 'ln2_w': jnp.ones((H,), jnp.float32), 'wq': jax.random.normal(ks[1], (H, H), jnp.float32) * s, 'wk': jax.random.normal(ks[2], (H, H), jnp.float32) * s, 'wv': jax.random.normal(ks[3], (H, H), jnp.float32) * s, 'wo': jax.random.normal(ks[4], (H, H), jnp.float32) * s, 'gate_w': jax.random.normal(ks[5], (E, H), jnp.float32) * s, 'w1': jax.random.normal(ks[6], (E, I, H), jnp.float32) * s, 'w2': jax.random.normal(ks[7], (E, H, I), jnp.float32) * s, 'w3': jax.random.normal(ks[8], (E, I, H), jnp.float32) * s}
    _L2_ffn_all = _L2_ffn_setup()
    _L2_ffn_in = {k: v for k, v in _L2_ffn_all.items() if k in ('ln1_w', 'ln2_w', 'wq', 'wk', 'wv', 'wo', 'gate_w', 'w1', 'w2', 'w3')}
    del _L2_ffn_all

    def _L3_attn_setup():
        import jax, jax.numpy as jnp
        import numpy as np
        B, T, D = (2, 512, 256)
        H = 16
        HD = D // H
        DL = 128
        NR = 64
        EPS = 1.1920929e-07

        def _rms_norm(x, w):
            ms = jnp.mean(jnp.square(x), axis=-1, keepdims=True)
            return x * jax.lax.rsqrt(ms + EPS) * w
        key = jax.random.key(seed)
        ks = jax.random.split(key, 10)
        s = 0.02
        return {'x': jax.random.normal(ks[0], (B, T, D), dtype=jnp.float32), 'W_DQ': jax.random.normal(ks[1], (DL, HD), dtype=jnp.float32) * s, 'W_UQ': jax.random.normal(ks[2], (HD, DL), dtype=jnp.float32) * s, 'W_DKV': jax.random.normal(ks[3], (2 * DL, HD), dtype=jnp.float32) * s, 'W_UKV': jax.random.normal(ks[4], (2 * HD, 2 * DL), dtype=jnp.float32) * s, 'W_QR': jax.random.normal(ks[5], (NR, HD), dtype=jnp.float32) * s, 'W_KR': jax.random.normal(ks[6], (NR, HD), dtype=jnp.float32) * s, 'W_O': jax.random.normal(ks[7], (HD, HD), dtype=jnp.float32) * s, 'q_norm_w': jnp.ones((HD,), dtype=jnp.float32), 'k_norm_w': jnp.ones((HD,), dtype=jnp.float32)}
    _L3_attn_all = _L3_attn_setup()
    _L3_attn_in = {k: v for k, v in _L3_attn_all.items() if k in ('W_DQ', 'W_UQ', 'W_DKV', 'W_UKV', 'W_QR', 'W_KR', 'W_O', 'q_norm_w', 'k_norm_w')}
    del _L3_attn_all

    def _L3_xattn_setup():
        import jax, jax.numpy as jnp
        import numpy as np
        from math import sqrt
        H = 16
        key = jax.random.key(seed)
        ks = jax.random.split(key, 8)
        B, Sq, Skv, Dq, Dkv, Dall = (2, 512, 512, 256, 256, 256)
        x = jax.random.normal(ks[0], (B, Sq, Dq), dtype=jnp.float32)
        y = jax.random.normal(ks[1], (B, Skv, Dkv), dtype=jnp.float32)
        attention_mask = jnp.ones((B, 1, Sq, Skv), dtype=jnp.int32)
        Wq = jax.random.normal(ks[2], (Dall, Dq), dtype=jnp.float32) * 0.02
        Wk = jax.random.normal(ks[3], (Dall, Dkv), dtype=jnp.float32) * 0.02
        Wv = jax.random.normal(ks[4], (Dall, Dkv), dtype=jnp.float32) * 0.02
        Wo = jax.random.normal(ks[5], (Dq, Dall), dtype=jnp.float32) * 0.02
        bo = jnp.zeros((Dq,), dtype=jnp.float32)
        return {'x': x, 'y': y, 'attention_mask': attention_mask, 'Wq': Wq, 'Wk': Wk, 'Wv': Wv, 'Wo': Wo, 'bo': bo}
    _L3_xattn_all = _L3_xattn_setup()
    _L3_xattn_in = {k: v for k, v in _L3_xattn_all.items() if k in ('Wq', 'Wk', 'Wv', 'Wo', 'bo')}
    del _L3_xattn_all

    def _L3_ffn_setup():
        import jax, jax.numpy as jnp
        import numpy as np
        D_MODEL = 256
        N_HEADS = 16
        HEAD_DIM = D_MODEL // N_HEADS
        FFN_DIM = 1024
        N_EXPERTS = 8
        CAP_FRAC = 0.25
        MOE_TOKEN_DROPOUT = 0.2
        LN_EPS = 1e-05
        B, S = (4, 128)

        def _layer_norm(x, g, b):
            mu = x.mean(-1, keepdims=True)
            var = ((x - mu) ** 2).mean(-1, keepdims=True)
            return (x - mu) * jax.lax.rsqrt(var + LN_EPS) * g + b

        def _self_attention(x, wq, bq, wk, bk, wv, bv, wo, bo):
            b, s, d = x.shape
            q = ((x @ wq + bq) * HEAD_DIM ** (-0.5)).reshape(b, s, N_HEADS, HEAD_DIM)
            k = (x @ wk + bk).reshape(b, s, N_HEADS, HEAD_DIM)
            v = (x @ wv + bv).reshape(b, s, N_HEADS, HEAD_DIM)
            scores = jnp.einsum('bqhd,bkhd->bhqk', q, k)
            p = jax.nn.softmax(scores, axis=-1)
            o = jnp.einsum('bhqk,bkhd->bqhd', p, v).reshape(b, s, d)
            return o @ wo + bo

        def _moe_ffn(x, wr, w1, b1, w2, b2):
            T, D = x.shape
            C = int(np.ceil(CAP_FRAC * T))
            logits = x @ wr
            probs = jax.nn.softmax(logits, axis=-1)
            top1 = jnp.argmax(probs, axis=-1)
            m1 = jax.nn.one_hot(top1, N_EXPERTS, dtype=x.dtype)
            top2 = jnp.argmax(jnp.where(m1 > 0, -jnp.inf, logits), axis=-1)
            m2 = jax.nn.one_hot(top2, N_EXPERTS, dtype=x.dtype)
            loc1 = jnp.cumsum(m1, axis=0) - 1.0
            loc2 = jnp.cumsum(m2, axis=0) - 1.0 + m1.sum(0, keepdims=True)
            m1 = m1 * (loc1 < C)
            m2 = m2 * (loc2 < C)
            t1 = (probs * m1).sum(-1)
            t2 = (probs * m2).sum(-1)
            denom = jnp.maximum(t1 + t2, jnp.finfo(x.dtype).eps)
            t1, t2 = (t1 / denom, t2 / denom)
            tok = jnp.arange(T)
            s1 = loc1[tok, top1].astype(jnp.int32)
            s2 = loc2[tok, top2].astype(jnp.int32)
            v1 = m1[tok, top1] > 0
            v2 = m2[tok, top2] > 0
            s1 = jnp.where(v1, s1, C)
            s2 = jnp.where(v2, s2, C)
            buf = jnp.zeros((N_EXPERTS, C, D), x.dtype)
            buf = buf.at[top1, s1].set(x, mode='drop')
            buf = buf.at[top2, s2].set(x, mode='drop')
            h = jax.nn.relu(jnp.einsum('ecd,edf->ecf', buf, w1) + b1[:, None, :])
            y = (jnp.einsum('ecf,efd->ecd', h, w2) + b2[:, None, :]) * (1.0 - MOE_TOKEN_DROPOUT)
            y1 = y[top1, jnp.minimum(s1, C - 1)]
            y2 = y[top2, jnp.minimum(s2, C - 1)]
            g1 = t1 * v1
            g2 = t2 * v2
            return g1[:, None] * y1 + g2[:, None] * y2
        key = jax.random.key(seed)
        ks = jax.random.split(key, 20)

        def w(k, shape, scale=0.02):
            return jax.random.normal(k, shape, jnp.float32) * scale
        return {'x': jax.random.normal(ks[0], (B, S, D_MODEL), jnp.float32), 'wq': w(ks[1], (D_MODEL, D_MODEL)), 'bq': w(ks[2], (D_MODEL,)), 'wk': w(ks[3], (D_MODEL, D_MODEL)), 'bk': w(ks[4], (D_MODEL,)), 'wv': w(ks[5], (D_MODEL, D_MODEL)), 'bv': w(ks[6], (D_MODEL,)), 'wo': w(ks[7], (D_MODEL, D_MODEL)), 'bo': w(ks[8], (D_MODEL,)), 'ln1_g': 1.0 + w(ks[9], (D_MODEL,)), 'ln1_b': w(ks[10], (D_MODEL,)), 'ln2_g': 1.0 + w(ks[11], (D_MODEL,)), 'ln2_b': w(ks[12], (D_MODEL,)), 'wr': w(ks[13], (D_MODEL, N_EXPERTS)), 'w1': w(ks[14], (N_EXPERTS, D_MODEL, FFN_DIM)), 'b1': w(ks[15], (N_EXPERTS, FFN_DIM)), 'w2': w(ks[16], (N_EXPERTS, FFN_DIM, D_MODEL)), 'b2': w(ks[17], (N_EXPERTS, D_MODEL))}
    _L3_ffn_all = _L3_ffn_setup()
    _L3_ffn_in = {k: v for k, v in _L3_ffn_all.items() if k in ('wq', 'bq', 'wk', 'bk', 'wv', 'bv', 'wo', 'bo', 'ln1_g', 'ln1_b', 'ln2_g', 'ln2_b', 'wr', 'w1', 'b1', 'w2', 'b2')}
    del _L3_ffn_all
    return {'x': x, 'ctx_1024': ctx_1024, 'mask_BxS2_bf1': mask_BxS2_bf1, 'mask_Bx1xSxS2_if1': mask_Bx1xSxS2_if1, 'L0_attn_W_DKV': _L0_attn_in['W_DKV'], 'L0_attn_W_UK': _L0_attn_in['W_UK'], 'L0_attn_W_UV': _L0_attn_in['W_UV'], 'L0_attn_W_UQ': _L0_attn_in['W_UQ'], 'L0_attn_W_O': _L0_attn_in['W_O'], 'L0_xattn_gm': _L0_xattn_in['gm'], 'L0_xattn_bm': _L0_xattn_in['bm'], 'L0_xattn_gl': _L0_xattn_in['gl'], 'L0_xattn_bl': _L0_xattn_in['bl'], 'L0_xattn_Wq': _L0_xattn_in['Wq'], 'L0_xattn_Wk': _L0_xattn_in['Wk'], 'L0_xattn_Wv': _L0_xattn_in['Wv'], 'L0_xattn_Wo': _L0_xattn_in['Wo'], 'L0_ffn_router_w': _L0_ffn_in['router_w'], 'L0_ffn_router_b': _L0_ffn_in['router_b'], 'L0_ffn_expert_w': _L0_ffn_in['expert_w'], 'L0_ffn_expert_b': _L0_ffn_in['expert_b'], 'L1_attn_Wqkv': _L1_attn_in['Wqkv'], 'L1_attn_bqkv': _L1_attn_in['bqkv'], 'L1_attn_Wproj': _L1_attn_in['Wproj'], 'L1_attn_bproj': _L1_attn_in['bproj'], 'L1_xattn_Wq': _L1_xattn_in['Wq'], 'L1_xattn_bq': _L1_xattn_in['bq'], 'L1_xattn_Wk': _L1_xattn_in['Wk'], 'L1_xattn_bk': _L1_xattn_in['bk'], 'L1_xattn_Wv': _L1_xattn_in['Wv'], 'L1_xattn_bv': _L1_xattn_in['bv'], 'L1_xattn_Wo': _L1_xattn_in['Wo'], 'L1_xattn_bo': _L1_xattn_in['bo'], 'L1_ffn_w_gate': _L1_ffn_in['w_gate'], 'L1_ffn_w_up': _L1_ffn_in['w_up'], 'L1_ffn_w_down': _L1_ffn_in['w_down'], 'L2_attn_in_proj_w': _L2_attn_in['in_proj_w'], 'L2_attn_conv_w': _L2_attn_in['conv_w'], 'L2_attn_conv_b': _L2_attn_in['conv_b'], 'L2_attn_x_proj_w': _L2_attn_in['x_proj_w'], 'L2_attn_dt_proj_w': _L2_attn_in['dt_proj_w'], 'L2_attn_dt_proj_b': _L2_attn_in['dt_proj_b'], 'L2_attn_A_log': _L2_attn_in['A_log'], 'L2_attn_D': _L2_attn_in['D'], 'L2_attn_out_proj_w': _L2_attn_in['out_proj_w'], 'L2_attn_ln_g': _L2_attn_in['ln_g'], 'L2_attn_ln_b': _L2_attn_in['ln_b'], 'L2_attn_ff_w1': _L2_attn_in['ff_w1'], 'L2_attn_ff_b1': _L2_attn_in['ff_b1'], 'L2_attn_ff_w2': _L2_attn_in['ff_w2'], 'L2_attn_ff_b2': _L2_attn_in['ff_b2'], 'L2_xattn_w_sim': _L2_xattn_in['w_sim'], 'L2_xattn_b_sim': _L2_xattn_in['b_sim'], 'L2_xattn_W_qv': _L2_xattn_in['W_qv'], 'L2_xattn_b_qv': _L2_xattn_in['b_qv'], 'L2_ffn_ln1_w': _L2_ffn_in['ln1_w'], 'L2_ffn_ln2_w': _L2_ffn_in['ln2_w'], 'L2_ffn_wq': _L2_ffn_in['wq'], 'L2_ffn_wk': _L2_ffn_in['wk'], 'L2_ffn_wv': _L2_ffn_in['wv'], 'L2_ffn_wo': _L2_ffn_in['wo'], 'L2_ffn_gate_w': _L2_ffn_in['gate_w'], 'L2_ffn_w1': _L2_ffn_in['w1'], 'L2_ffn_w2': _L2_ffn_in['w2'], 'L2_ffn_w3': _L2_ffn_in['w3'], 'L3_attn_W_DQ': _L3_attn_in['W_DQ'], 'L3_attn_W_UQ': _L3_attn_in['W_UQ'], 'L3_attn_W_DKV': _L3_attn_in['W_DKV'], 'L3_attn_W_UKV': _L3_attn_in['W_UKV'], 'L3_attn_W_QR': _L3_attn_in['W_QR'], 'L3_attn_W_KR': _L3_attn_in['W_KR'], 'L3_attn_W_O': _L3_attn_in['W_O'], 'L3_attn_q_norm_w': _L3_attn_in['q_norm_w'], 'L3_attn_k_norm_w': _L3_attn_in['k_norm_w'], 'L3_xattn_Wq': _L3_xattn_in['Wq'], 'L3_xattn_Wk': _L3_xattn_in['Wk'], 'L3_xattn_Wv': _L3_xattn_in['Wv'], 'L3_xattn_Wo': _L3_xattn_in['Wo'], 'L3_xattn_bo': _L3_xattn_in['bo'], 'L3_ffn_wq': _L3_ffn_in['wq'], 'L3_ffn_bq': _L3_ffn_in['bq'], 'L3_ffn_wk': _L3_ffn_in['wk'], 'L3_ffn_bk': _L3_ffn_in['bk'], 'L3_ffn_wv': _L3_ffn_in['wv'], 'L3_ffn_bv': _L3_ffn_in['bv'], 'L3_ffn_wo': _L3_ffn_in['wo'], 'L3_ffn_bo': _L3_ffn_in['bo'], 'L3_ffn_ln1_g': _L3_ffn_in['ln1_g'], 'L3_ffn_ln1_b': _L3_ffn_in['ln1_b'], 'L3_ffn_ln2_g': _L3_ffn_in['ln2_g'], 'L3_ffn_ln2_b': _L3_ffn_in['ln2_b'], 'L3_ffn_wr': _L3_ffn_in['wr'], 'L3_ffn_w1': _L3_ffn_in['w1'], 'L3_ffn_b1': _L3_ffn_in['b1'], 'L3_ffn_w2': _L3_ffn_in['w2'], 'L3_ffn_b2': _L3_ffn_in['b2']}

def reference(x, ctx_1024, mask_BxS2_bf1, mask_Bx1xSxS2_if1, L0_attn_W_DKV, L0_attn_W_UK, L0_attn_W_UV, L0_attn_W_UQ, L0_attn_W_O, L0_xattn_gm, L0_xattn_bm, L0_xattn_gl, L0_xattn_bl, L0_xattn_Wq, L0_xattn_Wk, L0_xattn_Wv, L0_xattn_Wo, L0_ffn_router_w, L0_ffn_router_b, L0_ffn_expert_w, L0_ffn_expert_b, L1_attn_Wqkv, L1_attn_bqkv, L1_attn_Wproj, L1_attn_bproj, L1_xattn_Wq, L1_xattn_bq, L1_xattn_Wk, L1_xattn_bk, L1_xattn_Wv, L1_xattn_bv, L1_xattn_Wo, L1_xattn_bo, L1_ffn_w_gate, L1_ffn_w_up, L1_ffn_w_down, L2_attn_in_proj_w, L2_attn_conv_w, L2_attn_conv_b, L2_attn_x_proj_w, L2_attn_dt_proj_w, L2_attn_dt_proj_b, L2_attn_A_log, L2_attn_D, L2_attn_out_proj_w, L2_attn_ln_g, L2_attn_ln_b, L2_attn_ff_w1, L2_attn_ff_b1, L2_attn_ff_w2, L2_attn_ff_b2, L2_xattn_w_sim, L2_xattn_b_sim, L2_xattn_W_qv, L2_xattn_b_qv, L2_ffn_ln1_w, L2_ffn_ln2_w, L2_ffn_wq, L2_ffn_wk, L2_ffn_wv, L2_ffn_wo, L2_ffn_gate_w, L2_ffn_w1, L2_ffn_w2, L2_ffn_w3, L3_attn_W_DQ, L3_attn_W_UQ, L3_attn_W_DKV, L3_attn_W_UKV, L3_attn_W_QR, L3_attn_W_KR, L3_attn_W_O, L3_attn_q_norm_w, L3_attn_k_norm_w, L3_xattn_Wq, L3_xattn_Wk, L3_xattn_Wv, L3_xattn_Wo, L3_xattn_bo, L3_ffn_wq, L3_ffn_bq, L3_ffn_wk, L3_ffn_bk, L3_ffn_wv, L3_ffn_bv, L3_ffn_wo, L3_ffn_bo, L3_ffn_ln1_g, L3_ffn_ln1_b, L3_ffn_ln2_g, L3_ffn_ln2_b, L3_ffn_wr, L3_ffn_w1, L3_ffn_b1, L3_ffn_w2, L3_ffn_b2):
    import jax
    import jax.numpy as jnp

    def _L0_attn_ref(x, W_DKV, W_UK, W_UV, W_UQ, W_O):
        import jax, jax.numpy as jnp
        import numpy as np
        DIM = 256
        N_HEADS = 16
        HEAD_DIM = DIM // N_HEADS
        D_LATENT = 64
        B, T = (1, 1024)
        b, t, d = x.shape
        h, hd = (N_HEADS, HEAD_DIM)
        c_kv = x @ W_DKV
        k = (c_kv @ W_UK).reshape(b, t, h, hd)
        v = (c_kv @ W_UV).reshape(b, t, h, hd)
        q = (x @ W_UQ).reshape(b, t, h, hd)
        scale = 1.0 / jnp.sqrt(jnp.asarray(hd, x.dtype))
        scores = jnp.einsum('bqhd,bkhd->bhqk', q, k) * scale
        causal = jnp.tril(jnp.ones((t, t), dtype=bool))
        scores = jnp.where(causal, scores, jnp.asarray(-jnp.inf, scores.dtype))
        probs = jax.nn.softmax(scores, axis=-1)
        ctx = jnp.einsum('bhqk,bkhd->bqhd', probs, v).reshape(b, t, d)
        return ctx @ W_O

    def _L0_xattn_ref(features, masks, latents, gm, bm, gl, bl, Wq, Wk, Wv, Wo):
        import jax, jax.numpy as jnp
        import numpy as np
        DIM = 256
        HEADS = 16
        DIM_HEAD = 64
        INNER = HEADS * DIM_HEAD
        B, F, Q = (16, 1024, 64)
        EPS = 1e-05
        SCALE = DIM_HEAD ** (-0.5)

        def _layernorm(x, gamma, beta):
            mu = jnp.mean(x, axis=-1, keepdims=True)
            var = jnp.var(x, axis=-1, keepdims=True)
            return (x - mu) * jax.lax.rsqrt(var + EPS) * gamma + beta
        b, f, d = features.shape
        q_len = latents.shape[1]
        x = _layernorm(features, gm, bm)
        lat = _layernorm(latents, gl, bl)
        q = (lat @ Wq).reshape(b, q_len, HEADS, DIM_HEAD).transpose(0, 2, 1, 3)
        kv_input = jnp.concatenate([x, lat], axis=1)
        kv_mask = jnp.concatenate([masks, jnp.ones((b, q_len), dtype=bool)], axis=1)
        kv_mask = kv_mask[:, None, None, :]
        k = (kv_input @ Wk).reshape(b, f + q_len, HEADS, DIM_HEAD).transpose(0, 2, 1, 3)
        v = (kv_input @ Wv).reshape(b, f + q_len, HEADS, DIM_HEAD).transpose(0, 2, 1, 3)
        q = q * SCALE
        sim = jnp.einsum('bhqd,bhfd->bhqf', q, k)
        sim = sim - jax.lax.stop_gradient(jnp.max(sim, axis=-1, keepdims=True))
        sim = jnp.where(kv_mask, sim, -jnp.inf)
        alphas = jax.nn.softmax(sim, axis=-1)
        out = jnp.einsum('bhqf,bhfd->bhqd', alphas, v)
        out = out.transpose(0, 2, 1, 3).reshape(b, q_len, INNER)
        return out @ Wo

    def _L0_ffn_ref(x, router_w, router_b, expert_w, expert_b):
        import jax, jax.numpy as jnp
        import numpy as np
        B, S, H, E = (4, 512, 256, 8)
        b, s, h = x.shape
        xt = x.reshape(b * s, h)
        logits = xt @ router_w + router_b
        probs = jax.nn.softmax(logits, axis=-1)
        gate = jnp.max(probs, axis=-1)
        idx = jnp.argmax(probs, axis=-1)
        out_all = jnp.einsum('th,ehd->ted', xt, expert_w) + expert_b[None, :, :]
        e_out = jnp.take_along_axis(out_all, idx[:, None, None], axis=1)[:, 0, :]
        y = gate[:, None] * e_out
        return y.reshape(b, s, h)

    def _L1_attn_ref(x, Wqkv, bqkv, Wproj, bproj):
        import jax, jax.numpy as jnp
        import numpy as np
        N, B, C = (72, 64, 256)
        H = 16
        P_PER_TASK = 4
        NUM_TASKS = 7

        def _prompt_mask(n, p, num_tasks, dtype):
            P = (num_tasks + 1) * p
            r = jnp.arange(n)[:, None]
            c = jnp.arange(n)[None, :]
            blocked = (c < P) & ~((r < P) & (r >= c // p * p))
            return jnp.where(blocked, -jnp.inf, 0.0).astype(dtype)
        n, b, ch = x.shape
        hd = ch // H
        scale = hd ** (-0.5)
        qkv = x @ Wqkv.T + bqkv
        q, k, v = jnp.split(qkv, 3, axis=-1)
        to_heads = lambda t: t.reshape(n, b * H, hd).transpose(1, 0, 2)
        q, k, v = (to_heads(q), to_heads(k), to_heads(v))
        mask = _prompt_mask(n, P_PER_TASK, NUM_TASKS, x.dtype)
        scores = mask + scale * jnp.einsum('bnd,bmd->bnm', q, k)
        attn = jax.nn.softmax(scores, axis=-1)
        out = jnp.einsum('bnm,bmd->bnd', attn, v)
        out = out.transpose(1, 0, 2).reshape(n, b, ch)
        return out @ Wproj.T + bproj

    def _L1_xattn_ref(Q, K, V, Wq, bq, Wk, bk, Wv, bv, Wo, bo):
        import jax, jax.numpy as jnp
        import numpy as np
        D_MODEL = 256
        N_HEADS = 16
        B, Sq, d_model = Q.shape
        h = N_HEADS
        d_k = d_model // h

        def split_heads(x, W, b):
            y = x @ W.T + b
            return y.reshape(B, x.shape[1], h, d_k).transpose(0, 2, 1, 3)
        q = split_heads(Q, Wq, bq)
        k = split_heads(K, Wk, bk)
        v = split_heads(V, Wv, bv)
        scores = jnp.einsum('bhqd,bhkd->bhqk', q, k) / jnp.sqrt(jnp.asarray(d_k, q.dtype))
        attn = jax.nn.softmax(scores.astype(jnp.float32), axis=-1).astype(q.dtype)
        out = jnp.einsum('bhqk,bhkd->bhqd', attn, v)
        out = out.transpose(0, 2, 1, 3).reshape(B, Sq, d_model)
        return out @ Wo.T + bo

    def _L1_ffn_ref(x, w_gate, w_up, w_down):
        import jax, jax.numpy as jnp
        import numpy as np
        DIM = 256
        HIDDEN = 768
        SCALE = 1.0 / 127.0

        def _dequant(w_int, dtype):
            return w_int.astype(dtype) * jnp.asarray(SCALE, dtype)
        wg = _dequant(w_gate, x.dtype)
        wu = _dequant(w_up, x.dtype)
        wd = _dequant(w_down, x.dtype)
        gate = jnp.einsum('bsd,hd->bsh', x, wg)
        up = jnp.einsum('bsd,hd->bsh', x, wu)
        h = jax.nn.silu(gate) * up
        return jnp.einsum('bsh,dh->bsd', h, wd)

    def _L2_attn_ref(x, in_proj_w, conv_w, conv_b, x_proj_w, dt_proj_w, dt_proj_b, A_log, D, out_proj_w, ln_g, ln_b, ff_w1, ff_b1, ff_w2, ff_b2):
        import jax, jax.numpy as jnp
        import numpy as np
        D_MODEL = 256
        D_STATE = 16
        D_CONV = 4
        EXPAND = 2
        D_INNER = EXPAND * D_MODEL
        DT_RANK = (D_MODEL + 15) // 16
        BATCH = 2
        SEQ = 256

        def _mamba(x, in_proj_w, conv_w, conv_b, x_proj_w, dt_proj_w, dt_proj_b, A_log, D, out_proj_w):
            L = x.shape[1]
            xz = x @ in_proj_w
            xc, z = jnp.split(xz, 2, axis=-1)
            xp = jnp.pad(xc, ((0, 0), (D_CONV - 1, 0), (0, 0)))
            xc = sum((conv_w[:, i] * xp[:, i:i + L, :] for i in range(D_CONV))) + conv_b
            xc = jax.nn.silu(xc)
            dbl = xc @ x_proj_w
            dt = dbl[..., :DT_RANK]
            Bm = dbl[..., DT_RANK:DT_RANK + D_STATE]
            Cm = dbl[..., DT_RANK + D_STATE:]
            delta = jax.nn.softplus(dt @ dt_proj_w + dt_proj_b)
            A = -jnp.exp(A_log)

            def step(h, t):
                d_t, B_t, C_t, u_t = t
                h = h * jnp.exp(d_t[..., None] * A) + (d_t * u_t)[..., None] * B_t[:, None, :]
                return (h, jnp.einsum('bdn,bn->bd', h, C_t))
            h0 = jnp.zeros((x.shape[0], D_INNER, D_STATE), x.dtype)
            xs = (delta.transpose(1, 0, 2), Bm.transpose(1, 0, 2), Cm.transpose(1, 0, 2), xc.transpose(1, 0, 2))
            _, ys = jax.lax.scan(step, h0, xs)
            y = ys.transpose(1, 0, 2) + xc * D
            y = y * jax.nn.silu(z)
            return y @ out_proj_w
        b = x.shape[0]
        xx = jnp.concatenate([x, jnp.flip(x, axis=1)], axis=0)
        m = _mamba(xx, in_proj_w, conv_w, conv_b, x_proj_w, dt_proj_w, dt_proj_b, A_log, D, out_proj_w)
        mo = m[:b] + jnp.flip(m[b:], axis=1)
        mu = mo.mean(-1, keepdims=True)
        var = mo.var(-1, keepdims=True)
        h = (mo - mu) / jnp.sqrt(var + 1e-05) * ln_g + ln_b
        return jax.nn.gelu(h @ ff_w1 + ff_b1, approximate=False) @ ff_w2 + ff_b2

    def _L2_xattn_ref(encoder_hc, decoder_hq, w_sim, b_sim, W_qv, b_qv):
        import jax, jax.numpy as jnp
        import numpy as np
        B, L_ENC, L_DEC, D = (16, 128, 128, 256)
        d = encoder_hc.shape[-1]
        w1, w2, w3 = (w_sim[:d], w_sim[d:2 * d], w_sim[2 * d:])
        Sim = (encoder_hc @ w1)[:, :, None] + (decoder_hq @ w2)[:, None, :] + jnp.einsum('bid,bjd->bij', encoder_hc * w3, decoder_hq) + b_sim[0]
        A = jax.nn.softmax(Sim, axis=2)
        hq_hat = jnp.einsum('bij,bjd->bid', A, decoder_hq)
        Batt = jax.nn.softmax(jnp.max(Sim, axis=2), axis=1)
        hc_bar = jnp.einsum('bi,bid->bd', Batt, encoder_hc)[:, None, :]
        hc_hat = jnp.broadcast_to(hc_bar, encoder_hc.shape)
        feats = jnp.concatenate([encoder_hc, hq_hat, encoder_hc * hq_hat, encoder_hc * hc_hat], axis=-1)
        hcq = feats @ W_qv + b_qv
        return hcq

    def _L2_ffn_ref(x, ln1_w, ln2_w, wq, wk, wv, wo, gate_w, w1, w2, w3):
        import jax, jax.numpy as jnp
        import numpy as np
        EPS = 1e-05
        TOP_K = 2

        def _rmsnorm(x, w):
            xf = x.astype(jnp.float32)
            rms = jax.lax.rsqrt(jnp.mean(xf * xf, axis=-1, keepdims=True) + EPS)
            return (xf * rms).astype(x.dtype) * w

        def _attention(x, wq, wk, wv, wo, num_heads=16):
            B, S, H = x.shape
            D = H // num_heads
            q = (x @ wq.T).reshape(B, S, num_heads, D)
            k = (x @ wk.T).reshape(B, S, num_heads, D)
            v = (x @ wv.T).reshape(B, S, num_heads, D)
            scale = 1.0 / jnp.sqrt(jnp.float32(D)).astype(x.dtype)
            scores = jnp.einsum('bqhd,bkhd->bhqk', q, k) * scale
            probs = jax.nn.softmax(scores, axis=-1)
            out = jnp.einsum('bhqk,bkhd->bqhd', probs, v).reshape(B, S, H)
            return out @ wo.T

        def _moe(x, gate_w, w1, w2, w3):
            B, S, H = x.shape
            xf = x.reshape(-1, H)
            logits = xf @ gate_w.T
            rw, sel = jax.lax.top_k(logits, TOP_K)
            rw = jax.nn.softmax(rw.astype(jnp.float32), axis=-1).astype(x.dtype)
            E = gate_w.shape[0]
            out = jnp.zeros_like(xf)
            for e in range(E):
                we = jnp.sum(jnp.where(sel == e, rw, 0.0), axis=-1)
                h = jax.nn.silu(xf @ w1[e].T) * (xf @ w3[e].T)
                out = out + h @ w2[e].T * we[:, None]
            return out.reshape(B, S, H)
        h = x + _attention(_rmsnorm(x, ln1_w), wq, wk, wv, wo)
        h = h + _moe(_rmsnorm(h, ln2_w), gate_w, w1, w2, w3)
        return h

    def _L3_attn_ref(x, W_DQ, W_UQ, W_DKV, W_UKV, W_QR, W_KR, W_O, q_norm_w, k_norm_w):
        import jax, jax.numpy as jnp
        import numpy as np
        B, T, D = (2, 512, 256)
        H = 16
        HD = D // H
        DL = 128
        NR = 64
        EPS = 1.1920929e-07

        def _rms_norm(x, w):
            ms = jnp.mean(jnp.square(x), axis=-1, keepdims=True)
            return x * jax.lax.rsqrt(ms + EPS) * w
        b, t, d = x.shape
        scale = HD ** (-0.5)
        xh = x.reshape(b, t, H, HD).transpose(0, 2, 1, 3)
        c_q = jnp.einsum('bhtd,ld->bhtl', xh, W_DQ)
        q_c = jnp.einsum('bhtl,dl->bhtd', c_q, W_UQ)
        q_c_norm = _rms_norm(q_c, q_norm_w)
        q_r = jnp.einsum('bhtd,rd->bhtr', q_c_norm, W_QR)
        q = jnp.concatenate([q_c_norm, q_r], axis=-1)
        c_kv = jnp.einsum('bhtd,ld->bhtl', xh, W_DKV)
        kv = jnp.einsum('bhtl,dl->bhtd', c_kv, W_UKV)
        k_c, v_c = (kv[..., :HD], kv[..., HD:])
        k_c_norm = _rms_norm(k_c, k_norm_w)
        k_r = jnp.einsum('bhtd,rd->bhtr', xh, W_KR)
        k = jnp.concatenate([k_c_norm, k_r], axis=-1)
        scores = jnp.einsum('bhqd,bhkd->bhqk', q, k) * scale
        causal = jnp.triu(jnp.full((t, t), -jnp.inf, dtype=scores.dtype), k=1)
        attn = jax.nn.softmax(scores + causal, axis=-1)
        ctx = jnp.einsum('bhqk,bhkd->bhqd', attn, v_c)
        out = jnp.einsum('bhtd,od->bhto', ctx, W_O)
        return out.transpose(0, 2, 1, 3).reshape(b, t, d)

    def _L3_xattn_ref(x, y, attention_mask, Wq, Wk, Wv, Wo, bo):
        import jax, jax.numpy as jnp
        import numpy as np
        from math import sqrt
        H = 16
        B, Sq, _ = x.shape
        Dall = Wq.shape[0]
        Dh = Dall // H
        q = (x @ Wq.T).reshape(B, Sq, H, Dh).transpose(0, 2, 1, 3)
        k = (y @ Wk.T).reshape(B, -1, H, Dh).transpose(0, 2, 1, 3)
        v = (y @ Wv.T).reshape(B, -1, H, Dh).transpose(0, 2, 1, 3)
        scores = jnp.einsum('bhqd,bhkd->bhqk', q, k)
        mask = attention_mask == 0
        scores = jnp.where(mask, jnp.float32(-1000000000.0), scores)
        attn = jax.nn.softmax(scores / sqrt(Dh), axis=-1)
        out = jnp.einsum('bhqk,bhkd->bhqd', attn, v)
        out = out.transpose(0, 2, 1, 3).reshape(B, Sq, Dall)
        return out @ Wo.T + bo

    def _L3_ffn_ref(x, wq, bq, wk, bk, wv, bv, wo, bo, ln1_g, ln1_b, ln2_g, ln2_b, wr, w1, b1, w2, b2):
        import jax, jax.numpy as jnp
        import numpy as np
        D_MODEL = 256
        N_HEADS = 16
        HEAD_DIM = D_MODEL // N_HEADS
        FFN_DIM = 1024
        N_EXPERTS = 8
        CAP_FRAC = 0.25
        MOE_TOKEN_DROPOUT = 0.2
        LN_EPS = 1e-05
        B, S = (4, 128)

        def _layer_norm(x, g, b):
            mu = x.mean(-1, keepdims=True)
            var = ((x - mu) ** 2).mean(-1, keepdims=True)
            return (x - mu) * jax.lax.rsqrt(var + LN_EPS) * g + b

        def _self_attention(x, wq, bq, wk, bk, wv, bv, wo, bo):
            b, s, d = x.shape
            q = ((x @ wq + bq) * HEAD_DIM ** (-0.5)).reshape(b, s, N_HEADS, HEAD_DIM)
            k = (x @ wk + bk).reshape(b, s, N_HEADS, HEAD_DIM)
            v = (x @ wv + bv).reshape(b, s, N_HEADS, HEAD_DIM)
            scores = jnp.einsum('bqhd,bkhd->bhqk', q, k)
            p = jax.nn.softmax(scores, axis=-1)
            o = jnp.einsum('bhqk,bkhd->bqhd', p, v).reshape(b, s, d)
            return o @ wo + bo

        def _moe_ffn(x, wr, w1, b1, w2, b2):
            T, D = x.shape
            C = int(np.ceil(CAP_FRAC * T))
            logits = x @ wr
            probs = jax.nn.softmax(logits, axis=-1)
            top1 = jnp.argmax(probs, axis=-1)
            m1 = jax.nn.one_hot(top1, N_EXPERTS, dtype=x.dtype)
            top2 = jnp.argmax(jnp.where(m1 > 0, -jnp.inf, logits), axis=-1)
            m2 = jax.nn.one_hot(top2, N_EXPERTS, dtype=x.dtype)
            loc1 = jnp.cumsum(m1, axis=0) - 1.0
            loc2 = jnp.cumsum(m2, axis=0) - 1.0 + m1.sum(0, keepdims=True)
            m1 = m1 * (loc1 < C)
            m2 = m2 * (loc2 < C)
            t1 = (probs * m1).sum(-1)
            t2 = (probs * m2).sum(-1)
            denom = jnp.maximum(t1 + t2, jnp.finfo(x.dtype).eps)
            t1, t2 = (t1 / denom, t2 / denom)
            tok = jnp.arange(T)
            s1 = loc1[tok, top1].astype(jnp.int32)
            s2 = loc2[tok, top2].astype(jnp.int32)
            v1 = m1[tok, top1] > 0
            v2 = m2[tok, top2] > 0
            s1 = jnp.where(v1, s1, C)
            s2 = jnp.where(v2, s2, C)
            buf = jnp.zeros((N_EXPERTS, C, D), x.dtype)
            buf = buf.at[top1, s1].set(x, mode='drop')
            buf = buf.at[top2, s2].set(x, mode='drop')
            h = jax.nn.relu(jnp.einsum('ecd,edf->ecf', buf, w1) + b1[:, None, :])
            y = (jnp.einsum('ecf,efd->ecd', h, w2) + b2[:, None, :]) * (1.0 - MOE_TOKEN_DROPOUT)
            y1 = y[top1, jnp.minimum(s1, C - 1)]
            y2 = y[top2, jnp.minimum(s2, C - 1)]
            g1 = t1 * v1
            g2 = t2 * v2
            return g1[:, None] * y1 + g2[:, None] * y2
        h = _layer_norm(x, ln1_g, ln1_b)
        h = _self_attention(h, wq, bq, wk, bk, wv, bv, wo, bo)
        x = x + h
        h = _layer_norm(x, ln2_g, ln2_b)
        b, s, d = h.shape
        moe = _moe_ffn(h.reshape(b * s, d), wr, w1, b1, w2, b2).reshape(b, s, d)
        return x + moe
    x = x + _L0_attn_ref(_layernorm(x, axis=-1), L0_attn_W_DKV, L0_attn_W_UK, L0_attn_W_UV, L0_attn_W_UQ, L0_attn_W_O)
    x = x + _L0_xattn_ref(ctx_1024, mask_BxS2_bf1, _layernorm(x, axis=-1), L0_xattn_gm, L0_xattn_bm, L0_xattn_gl, L0_xattn_bl, L0_xattn_Wq, L0_xattn_Wk, L0_xattn_Wv, L0_xattn_Wo)
    x = x + _L0_ffn_ref(_layernorm(x, axis=-1), L0_ffn_router_w, L0_ffn_router_b, L0_ffn_expert_w, L0_ffn_expert_b)
    x = x + _L1_attn_ref(_layernorm(x, axis=-1), L1_attn_Wqkv, L1_attn_bqkv, L1_attn_Wproj, L1_attn_bproj)
    x = x + _L1_xattn_ref(_layernorm(x, axis=-1), ctx_1024, ctx_1024, L1_xattn_Wq, L1_xattn_bq, L1_xattn_Wk, L1_xattn_bk, L1_xattn_Wv, L1_xattn_bv, L1_xattn_Wo, L1_xattn_bo)
    x = x + _L1_ffn_ref(_layernorm(x, axis=-1), L1_ffn_w_gate, L1_ffn_w_up, L1_ffn_w_down)
    x = x + _L2_attn_ref(_layernorm(x, axis=-1), L2_attn_in_proj_w, L2_attn_conv_w, L2_attn_conv_b, L2_attn_x_proj_w, L2_attn_dt_proj_w, L2_attn_dt_proj_b, L2_attn_A_log, L2_attn_D, L2_attn_out_proj_w, L2_attn_ln_g, L2_attn_ln_b, L2_attn_ff_w1, L2_attn_ff_b1, L2_attn_ff_w2, L2_attn_ff_b2)
    x = x + _L2_xattn_ref(_layernorm(x, axis=-1), ctx_1024, L2_xattn_w_sim, L2_xattn_b_sim, L2_xattn_W_qv, L2_xattn_b_qv)
    x = x + _L2_ffn_ref(_layernorm(x, axis=-1), L2_ffn_ln1_w, L2_ffn_ln2_w, L2_ffn_wq, L2_ffn_wk, L2_ffn_wv, L2_ffn_wo, L2_ffn_gate_w, L2_ffn_w1, L2_ffn_w2, L2_ffn_w3)
    x = x + _L3_attn_ref(_layernorm(x, axis=-1), L3_attn_W_DQ, L3_attn_W_UQ, L3_attn_W_DKV, L3_attn_W_UKV, L3_attn_W_QR, L3_attn_W_KR, L3_attn_W_O, L3_attn_q_norm_w, L3_attn_k_norm_w)
    x = x + _L3_xattn_ref(_layernorm(x, axis=-1), ctx_1024, mask_Bx1xSxS2_if1, L3_xattn_Wq, L3_xattn_Wk, L3_xattn_Wv, L3_xattn_Wo, L3_xattn_bo)
    x = x + _L3_ffn_ref(_layernorm(x, axis=-1), L3_ffn_wq, L3_ffn_bq, L3_ffn_wk, L3_ffn_bk, L3_ffn_wv, L3_ffn_bv, L3_ffn_wo, L3_ffn_bo, L3_ffn_ln1_g, L3_ffn_ln1_b, L3_ffn_ln2_g, L3_ffn_ln2_b, L3_ffn_wr, L3_ffn_w1, L3_ffn_b1, L3_ffn_w2, L3_ffn_b2)
    return x

_drawn_inputs = setup_inputs


def setup_inputs(seed=0):
    import zlib

    import numpy as np

    out = dict(_drawn_inputs(seed))
    spreads = {'L0_xattn_gm': (1.0, 0.2),
     'L0_xattn_bm': (0.0, 0.1),
     'L0_xattn_gl': (1.0, 0.2),
     'L0_xattn_bl': (0.0, 0.1),
     'L0_ffn_router_b': (0.0, 0.1),
     'L0_ffn_expert_b': (0.0, 0.1),
     'L1_attn_bqkv': (0.0, 0.1),
     'L1_attn_bproj': (0.0, 0.1),
     'L1_xattn_bq': (0.0, 0.32),
     'L1_xattn_bk': (0.0, 0.8),
     'L1_xattn_bv': (0.0, 0.1),
     'L1_xattn_bo': (0.0, 0.1),
     'L2_attn_conv_b': (0.0, 0.8),
     'L2_attn_D': (1.0, 0.6),
     'L2_attn_ln_g': (1.0, 0.6),
     'L2_attn_ln_b': (0.0, 0.8),
     'L2_attn_ff_b1': (0.0, 0.8),
     'L2_attn_ff_b2': (0.0, 0.8),
     'L2_ffn_ln1_w': (1.0, 0.6),
     'L2_ffn_ln2_w': (1.0, 0.6),
     'L3_attn_q_norm_w': (1.0, 0.6),
     'L3_attn_k_norm_w': (1.0, 0.6),
     'L3_xattn_bo': (0.0, 0.8)}
    factors = {'L0_attn_W_DKV': 8.0,
     'L0_attn_W_UK': 8.0,
     'L0_attn_W_UV': 8.0,
     'L0_attn_W_UQ': 8.0,
     'L0_attn_W_O': 5.816,
     'L2_attn_in_proj_w': 8.0,
     'L2_attn_conv_w': 8.0,
     'L2_attn_x_proj_w': 8.0,
     'L2_attn_dt_proj_w': 8.0,
     'L2_attn_dt_proj_b': 8.0,
     'L2_attn_A_log': 8.0,
     'L2_attn_out_proj_w': 8.0,
     'L2_attn_ff_w1': 8.0,
     'L2_attn_ff_w2': 8.0,
     'L2_xattn_w_sim': 8.0,
     'L2_xattn_W_qv': 8.0,
     'L2_xattn_b_qv': 8.0,
     'L2_ffn_wq': 8.0,
     'L2_ffn_wk': 8.0,
     'L2_ffn_wv': 8.0,
     'L2_ffn_wo': 8.0,
     'L2_ffn_gate_w': 8.0,
     'L2_ffn_w1': 8.0,
     'L2_ffn_w2': 8.0,
     'L2_ffn_w3': 8.0,
     'L3_attn_W_DQ': 8.0,
     'L3_attn_W_UQ': 8.0,
     'L3_attn_W_DKV': 8.0,
     'L3_attn_W_UKV': 8.0,
     'L3_attn_W_QR': 8.0,
     'L3_attn_W_KR': 8.0,
     'L3_attn_W_O': 8.0,
     'L3_xattn_Wq': 8.0,
     'L3_xattn_Wk': 8.0,
     'L3_xattn_Wv': 8.0,
     'L3_xattn_Wo': 8.0,
     'L3_ffn_wq': 8.0,
     'L3_ffn_bq': 8.0,
     'L3_ffn_wk': 8.0,
     'L3_ffn_wv': 8.0,
     'L3_ffn_bv': 8.0,
     'L3_ffn_wo': 8.0,
     'L3_ffn_bo': 8.0,
     'L3_ffn_ln1_g': 8.0,
     'L3_ffn_ln1_b': 8.0,
     'L3_ffn_ln2_g': 8.0,
     'L3_ffn_ln2_b': 8.0,
     'L3_ffn_wr': 8.0,
     'L3_ffn_w1': 8.0,
     'L3_ffn_b1': 8.0,
     'L3_ffn_w2': 8.0,
     'L3_ffn_b2': 8.0}
    for name, (base, spread) in spreads.items():
        noise = np.random.default_rng([zlib.crc32(name.encode()), seed]).standard_normal(out[name].shape)
        drawn = base * np.exp(spread * noise) if base else spread * noise
        out[name] = jnp.asarray(drawn.astype(out[name].dtype))
    for name, factor in factors.items():
        out[name] = (out[name] * factor).astype(out[name].dtype)
    return out
```

```python
from contextlib import ExitStack

import numpy as np
import concourse.bass as bass
from concourse import mybir

F32 = mybir.dt.float32
BF16 = mybir.dt.bfloat16
I32 = mybir.dt.int32
U8 = mybir.dt.uint8
ALU = mybir.AluOpType
ACT = mybir.ActivationFunctionType
AX = mybir.AxisListType
NEG = -1e30
BIG = 1e30
S = 1024
NT = 16
KC = 154
D = 256
QH = 96
QM = 98


class Lane:

    def __init__(self, sem):
        self.sem = sem
        self.items = []
        self.count = 0
        self.seen = {}

    def after(self, toks):
        for sem, value in toks:
            if self.seen.get(sem.name, 0) < value:
                self.seen[sem.name] = value
                self.items.append(waiter(sem, value))

    def put(self, fn, toks=(), inc=True):
        self.after(toks)
        if inc:
            self.count += 1
            self.items.append(counted(fn, self.sem))
        else:
            self.items.append(fn)
        return (self.sem, self.count)

    @property
    def now(self):
        return (self.sem, self.count)


def waiter(sem, value):
    return lambda e: e.wait_ge(sem, value)


def counted(fn, sem):
    return lambda e: fn(e).then_inc(sem, 1)


def bc(ap, shape):
    return ap.broadcast_to(list(shape))


def build(nc, ins, out, phases):
    ctx = ExitStack()
    with ctx:
        def sem(name):
            return ctx.enter_context(nc.semaphore(name))

        pe = Lane(sem("s_pe"))
        ac = Lane(sem("s_act"))
        dv = Lane(sem("s_dve"))
        gp = Lane(sem("s_pool"))
        sp = Lane(sem("s_sp"))
        lanes = [pe, ac, dv, gp]

        TOT = 53200
        AR = ctx.enter_context(nc.sbuf_tensor("AR", [128, TOT], F32))
        PS = ctx.enter_context(nc.psum_tensor("PS", [128, 8, 512], F32))

        def view(off, dims, dt=F32, p0=0, p1=128):
            n = int(np.prod(dims))
            words = n if dt in (F32, I32) else n // 2
            ap = AR[p0:p1, off:off + words]
            if dt != F32:
                ap = ap.bitcast(dt)
            if len(dims) == 1:
                return ap
            names = "abcd"[:len(dims)]
            return ap.rearrange(f"p ({' '.join(names)}) -> p {' '.join(names)}",
                                **{k: v for k, v in zip(names, dims)})

        class Heap:
            def __init__(self, lo, hi):
                self.lo, self.hi, self.at = lo, hi, lo

            def take(self, dims, dt=F32, p0=0, p1=128):
                n = int(np.prod(dims))
                words = n if dt in (F32, I32) else (n + 1) // 2
                off = self.at
                self.at += words
                assert self.at <= self.hi, (self.at, self.hi)
                return view(off, dims, dt, p0, p1)

            def clear(self):
                self.at = self.lo

        fixed = Heap(0, 10000)
        WA = Heap(10000, 16300)
        WB = [Heap(16300, 18400), Heap(18400, 20500)]
        scr = Heap(20500, TOT)

        X = fixed.take([NT, D])
        XNT = fixed.take([2, 2048])
        consts = fixed.take([840])
        ident = consts[:, 0:128]
        anti = consts[:, 128:256]
        rep16 = consts[0:16, 256:384]
        maskS_f = consts[:, 384:512]
        maskT_f = consts[:, 512:640]
        upper = consts[:, 640:768]
        bdm = consts[:, 768:776]
        rev = consts[:, 776:784]
        kb64 = consts[:, 784:785]
        kb65 = consts[:, 785:786]
        ctxT = fixed.take([2, 308])
        ones = fixed.take([128])
        identb = fixed.take([128], BF16)
        maskS = fixed.take([128], BF16)
        maskT = fixed.take([128], BF16)

        def mm(o, l, r, start, stop, w=(), inc=False, tile=None):
            if tile is None:
                return pe.put(lambda e: e.matmul(o, l, r, start=start, stop=stop), w, inc)
            return pe.put(lambda e: e.matmul(o, l, r, start=start, stop=stop, tile_position=tile), w, inc)

        def tr(o, i, idn, w=(), inc=False):
            return pe.put(lambda e: e.transpose(o, i, idn), w, inc)

        def act(o, i, f, w=(), bias=None, scale=None, acc=None):
            kw = {}
            if bias is not None:
                kw["bias"] = bias
            if scale is not None:
                kw["scale"] = scale
            if acc is not None:
                kw["accum_out"] = acc
            return ac.put(lambda e: e.activation(o, i, f, **kw), w)

        def tt(q, o, a, b, op, w=()):
            return q.put(lambda e: e.tensor_tensor(o, a, b, op), w)

        def ts(q, o, a, s1, s2, op0, op1, w=()):
            if op1 is None:
                return q.put(lambda e: e.tensor_scalar(o, a, s1, None, op0), w)
            return q.put(lambda e: e.tensor_scalar(o, a, s1, s2, op0, op1), w)

        def stt(o, a, s, b, op0, op1, w=()):
            return dv.put(lambda e: e.scalar_tensor_tensor(out=o, in0=a, scalar=s, in1=b, op0=op0, op1=op1), w)

        def red(o, a, op, w=(), neg=False):
            if neg:
                return dv.put(lambda e: e.tensor_reduce(o, a, AX.X, op, negate=True), w)
            return dv.put(lambda e: e.tensor_reduce(o, a, AX.X, op), w)

        def cp(q, o, i, w=()):
            if q is ac:
                return act(o, i, ACT.Copy, w)
            return q.put(lambda e: e.tensor_copy(o, i), w)

        def fill(q, o, v, w=()):
            return q.put(lambda e: e.memset(o, v), w)

        def recip(o, i, w=()):
            return dv.put(lambda e: e.reciprocal(o, i), w)

        def dma(o, i, s, w=()):
            sp.after(w)
            sp.items.append(lambda e: e.dma_start(o, i).then_inc(s, 16))

        def barrier():
            toks = [q.now for q in lanes]
            for q in lanes + [sp]:
                q.after(toks)
            for b in range(8):
                pf[b] = []

        pf = {b: [] for b in range(8)}
        turn = [0]

        def evac_lane():
            turn[0] += 1
            return ac if turn[0] % 2 else dv

        class Load:

            def __init__(self, name):
                self.sem = sem(name)
                self.n = 0

            def add(self, o, i, w=()):
                dma(o, i, self.sem, w)
                self.n += 16

            @property
            def ready(self):
                return (self.sem, self.n)

        l0 = Load("d_const")
        l0.add(consts[:, 0:840], ins["consts"])
        lx = Load("d_x")
        for i in range(4):
            lx.add(X[:, 4 * i:4 * i + 4, :],
                   ins["x"].rearrange("b (t p) c -> p (b t) c", p=128)[:, 4 * i:4 * i + 4, :])
        lc = Load("d_ctx")
        lc.add(ctxT, ins["ctxT"].rearrange("p (c n) -> p c n", c=2))
        fill(dv, ones, 1.0)
        cp(dv, identb, ident, [l0.ready])
        cp(dv, maskS, maskS_f)
        cp(dv, maskT, maskT_f)
        dv.after([lx.ready, lc.ready])
        ac.after([lx.ready, lc.ready])
        pe.after([l0.ready, lc.ready])
        gp.after([l0.ready, lc.ready, lx.ready])
        barrier()

        def load_w(heap, name, parts=128, width=None, dt=F32):
            heap_ap = heap.take([ins[name].shape[1]], dt, 0, parts)
            l = Load(f"d_{name}")
            n = ins[name].shape[1]
            half = (n + 1) // 2
            if n > 1024:
                l.add(heap_ap[:, 0:half], ins[name][:, 0:half], [])
                l.add(heap_ap[:, half:n], ins[name][:, half:n], [])
            else:
                l.add(heap_ap, ins[name], [])
            return heap_ap, l.ready

        def stats(src, n, heap, eps, rows=128, w=()):
            st = heap.take([n, 6])
            mv = heap.take([n, 2])
            ve = heap.take([n])
            sd = heap.take([n])
            rs = heap.take([n])
            dv.after(w)
            for i in range(n):
                dv.put(lambda e, i=i: e.bn_stats(st[0:rows, i, :], src(i)))
            t = dv.now
            for i in range(n):
                dv.put(lambda e, i=i: e.bn_aggr(mv[0:rows, i, :], st[0:rows, i, :]), [t])
            t = ts(dv, ve[0:rows], mv[0:rows, :, 1], eps, None, ALU.add, None, [dv.now])
            t = act(sd[0:rows], ve[0:rows], ACT.Sqrt, [t])
            t = recip(rs[0:rows], sd[0:rows], [t])
            dv.after([t])
            return mv, rs

        def normalise(dst, src, mv, rs, i, rows=128, w=()):
            return ts(dv, dst, src, mv[0:rows, i, 0:1], rs[0:rows, i:i + 1], ALU.subtract, ALU.mult, w)

        def to_T(src, dst, chunks, ready, idn=None, mul=None, add=None, banks=range(8), groups=4, order=None):
            idn = ident if idn is None else idn
            toks = []
            nb = len(banks)
            n = 0
            for k in range(groups):
                for c in range(chunks):
                    b = banks[n % nb]
                    n += 1
                    for j in range(4):
                        i = 4 * k + j
                        t = tr(PS[:, b, 128 * j:128 * j + 128], src(i if order is None else order[i], c), idn,
                               pf[b] + ready(i if order is None else order[i]), inc=(j == 3))
                    q = evac_lane()
                    if mul is None:
                        t = cp(q, dst(c, k), PS[:, b, :], [t])
                    else:
                        a = 0.0 if add is None else add(c)
                        t = ts(dv, dst(c, k), PS[:, b, :], mul(c), a, ALU.mult, ALU.add, [t])
                    pf[b] = [t]
                    toks.append(t)
            return toks

        def layer_norm_T(keep=None, mul=None, add=None, idn=None, order=None, src=None, eps=1e-5, twice=False):
            mark = scr.at
            src = X if src is None else src
            mv, rs = stats(lambda i: src[:, i, :], NT, scr, eps)
            xn = keep if keep is not None else scr.take([NT, D])
            done = []
            for i in range(NT):
                done.append(normalise(xn[:, i, :], src[:, i, :], mv, rs, i))
            if twice:
                mv, rs = stats(lambda i: xn[:, i, :], NT, scr, eps, w=[dv.now])
                done = []
                for i in range(NT):
                    done.append(normalise(xn[:, i, :], xn[:, i, :], mv, rs, i))
            toks = to_T(lambda i, c: xn[:, i, 128 * c:128 * c + 128],
                        lambda c, k: XNT[:, c, 512 * k:512 * k + 512], 2, lambda i: [done[i]],
                        idn=idn, mul=mul, add=add, order=order)
            scr.at = mark
            for q in lanes + [sp]:
                q.after(toks + [dv.now])
            return toks

        def rms_T(src, wcol, eps):
            mark = scr.at
            sq = scr.take([2, D])
            ms = scr.take([NT])
            sd = scr.take([NT])
            rs = scr.take([NT])
            xn = scr.take([NT, D])
            last = [(), ()]
            for i in range(NT):
                act(sq[:, i % 2, :], src[:, i, :], ACT.Square, [ac.now], acc=ms[:, i:i + 1])
            t = ts(dv, sd, ms, 1.0 / D, eps, ALU.mult, ALU.add, [ac.now])
            t = act(sd, sd, ACT.Sqrt, [t])
            t = recip(rs, sd, [t])
            done = []
            for i in range(NT):
                done.append(ts(dv, xn[:, i, :], src[:, i, :], rs[:, i:i + 1], None, ALU.mult, None, [t]))
            toks = to_T(lambda i, c: xn[:, i, 128 * c:128 * c + 128],
                        lambda c, k: XNT[:, c, 512 * k:512 * k + 512], 2, lambda i: [done[i]], mul=wcol)
            scr.at = mark
            for q in lanes + [sp]:
                q.after(toks + [dv.now])

        def add_proj(dst, lhs, nchunks, rhs, bias=None, tiles=range(NT), w=(), banks=range(8)):
            pe.after(w)
            n = 0
            toks = []
            for g in range(0, len(tiles), 2):
                b = banks[n % len(banks)]
                n += 1
                for k in range(2):
                    i = tiles[g + k]
                    o = PS[:, b, 256 * k:256 * k + 256]
                    for c in range(nchunks):
                        last = (c == nchunks - 1) and bias is None
                        t = mm(o, lhs(c, i), rhs(c), c == 0, last, pf[b], inc=(last and k == 1))
                    if bias is not None:
                        t = mm(o, ones[0:1, 0:128], bias, False, True, (), inc=(k == 1))
                i = tiles[g]
                v = dst[:, i:i + 2, :]
                t = tt(dv, v, PS[:, b, :].rearrange("p (k c) -> p k c", k=2), v, ALU.add, [t])
                pf[b] = [t]
                toks.append(t)
            return toks

        class Attention:

            def __init__(self, KV, causal, qkv, post=None, bound=None):
                self.KV, self.causal, self.qkv, self.post, self.bound = KV, causal, qkv, post, bound
                self.qS = [scr.take([8, S], BF16) for _ in range(2)]
                kn = S if KV == S else 160
                self.kS = [scr.take([8, kn], BF16) for _ in range(2)]
                self.nk = (KV + 127) // 128
                self.vE = [scr.take([self.nk, 8, 32]) for _ in range(2)]
                self.P = [scr.take([2, 512]) for _ in range(2)]
                self.O = scr.take([NT, D])
                self.ST = [scr.take([2, 8, 128], BF16) for _ in range(2)]
                self.R = [scr.take([2, 8, 16]) for _ in range(2)]
                self.Oc = scr.take([512])
                self.Mst = scr.take([4, 4, 32], BF16)
                self.m2 = scr.take([4, 4, 2])
                self.mr = scr.take([4, 4])
                self.nm = scr.take([4, 4])
                self.ri = scr.take([4, 4, 1])
                for v in self.vE:
                    fill(gp, v, 0.0)
                for v in self.ST:
                    fill(gp, v, 0.0)
                fill(gp, self.Mst, 0.0)
                g = gp.now
                for v in self.vE:
                    fill(gp, v[:, :, :, 16:17], 1.0, [g])
                for v in self.ST:
                    fill(gp, v[:, 1, :, QH:QM], 1.0, [g])
                self.ready0 = gp.now
                for q in (ac, dv, pe):
                    q.after([self.ready0])
                self.st_free = [[], []]
                self.r_free = [[], []]
                self.seg_free = [[], []]
                self.seg_ready = [[], []]
                self.p_free = [[], []]
                self.n_prep = 0

            def prep(self, s):
                b, hh, par = s // 2, s % 2, s % 2
                pieces = []
                self.seg_ready[par] = []
                if self.KV == S:
                    work = [(t, 128, True, True) for t in range(8)]
                else:
                    work = [(t, 128 if t == 0 else 26, False, True) for t in range(2)]
                    work += [(t, 128, True, False) for t in range(8)]
                for t, rows, hq, hk in work:
                    st = {}
                    pieces.append(lambda t=t, rows=rows, hq=hq, hk=hk, st=st: self.split(b, hh, par, t, rows, hq, hk, st))
                    if hq:
                        pieces.append(lambda t=t, rows=rows, st=st: self.turn(par, t, rows, 0, st))
                    if hk:
                        pieces.append(lambda t=t, rows=rows, st=st: self.turn(par, t, rows, 1, st))
                return pieces

            def split(self, b, hh, par, t, rows, hq, hk, st):
                bank = 7
                x = self.n_prep % 2
                self.n_prep += 1
                st["x"] = x
                ps = PS[0:rows, bank, :]
                tok = self.qkv(b, hh, t, rows, hq, hk, ps, pf[bank])
                lo, hi = (0 if hq else 1), (2 if hk else 1)
                ST, R = self.ST[x], self.R[x]
                a = ps[:, 0:256].rearrange("p (z h d) -> p z h d", z=2, h=8)
                rd = []
                if hk:
                    rd.append(act(self.vE[par][0:rows, t, :, 0:16], ps[:, 256:384].rearrange("p (h d) -> p h d", h=8),
                                  ACT.Copy, [tok] + self.seg_free[par]))
                    self.seg_ready[par].append(rd[-1])
                if self.post is not None:
                    dv.after(rd)
                    a, tok, more = self.post(b, hh, t, ps, tok, x)
                    rd += more
                w = [tok] + self.st_free[x]
                def slots(z, js, n):
                    v = ST[0:rows, z, :, 0:96].rearrange("p h (j d) -> p h j d", d=16)
                    if len(js) == 1:
                        return v[:, :, js[0], :]
                    step = js[1] - js[0]
                    return v[:, :, js[0]:js[-1] + 1:step, :]
                def dup(v, n):
                    return bc(v.unsqueeze(2), [rows, 8, n, 16])
                firsts = []
                if hq:
                    firsts.append(act(slots(0, [0, 1, 2], 3), dup(a[:, 0], 3), ACT.Copy, w))
                if hk:
                    firsts.append(act(slots(1, [0, 3], 2), dup(a[:, 1], 2), ACT.Copy, w))
                    firsts.append(act(slots(1, [5], 1), a[:, 1], ACT.Copy, w))
                first = ST[0:rows, lo:hi, :, 0:16]
                r = R[0:rows, lo:hi]
                t1 = tt(dv, r, a[:, lo:hi], first, ALU.subtract, firsts + self.r_free[x])
                rd += [t1] + firsts
                pf[bank] = rd
                done = list(firsts)
                if hq:
                    done.append(cp(gp, slots(0, [3, 4], 2), dup(R[0:rows, 0], 2), [t1]))
                if hk:
                    done.append(cp(gp, slots(1, [1, 4], 2), dup(R[0:rows, 1], 2), [t1]))
                g = gp.now
                if hq:
                    done.append(tt(gp, slots(0, [5], 1), R[0:rows, 0], slots(0, [3], 1), ALU.subtract, [g]))
                if hk:
                    done.append(tt(gp, slots(1, [2], 1), R[0:rows, 1], slots(1, [1], 1), ALU.subtract, [g]))
                self.r_free[x] = [gp.now]
                st["done"] = done
                self.st_free[x] = []

            def turn(self, par, t, rows, z, st):
                bank = 7
                x = st["x"]
                pb = PS[:, bank, :].bitcast(BF16).rearrange("p (h n) -> p h n", h=8)
                for h in range(8):
                    tok = tr(pb[:, h, 0:rows], self.ST[x][0:rows, z, h, :], identb[0:rows, 0:rows],
                             st["done"] + pf[bank], inc=(h == 7))
                self.st_free[x] = self.st_free[x] + [tok]
                dst = (self.qS if z == 0 else self.kS)[par]
                e = cp(evac_lane(), dst[0:QM, :, 128 * t:128 * t + rows], pb[0:QM, :, 0:rows],
                       [tok] + self.seg_free[par])
                pf[bank] = [e]
                self.seg_ready[par].append(e)

            def max_pieces(self, s, g, qb, u):
                par = s % 2
                qS, kS = self.qS[par], self.kS[par]
                b = s // 2
                pieces = []
                KV = self.KV
                st = {"toks": []}
                slot = [0]
                if KV == S:
                    nh = (qb + 1) if self.causal else 2
                    for qt in range(4):
                        for j in range(4):
                            def piece(qt=qt, j=j):
                                h = 4 * g + j
                                q0 = 512 * qb + 128 * qt
                                for half in range(nh):
                                    bank = 4 + slot[0] % 2
                                    slot[0] += 1
                                    n = 512
                                    diag = False
                                    if self.causal and half == nh - 1:
                                        n = 128 * (qt + 1)
                                        diag = True
                                    o = PS[:, bank, 0:n]
                                    tok = mm(o, qS[0:QH, h, q0:q0 + 128], kS[0:QH, h, 512 * half:512 * half + n],
                                             True, not diag, pf[bank] + self.seg_ready[par], inc=not diag)
                                    if diag:
                                        tok = mm(PS[:, bank, n - 128:n], identb, maskS, False, True, (), inc=True)
                                    e = red(self.m2[:, qt, j, half:half + 1], o, ALU.max, [tok] + st.get("w", []))
                                    pf[bank] = [e]
                            pieces.append(piece)
                else:
                    nh = 1
                    for qt in range(4):
                        for jj in range(2):
                            def piece(qt=qt, jj=jj):
                                bank = 4 + slot[0] % 2
                                slot[0] += 1
                                q0 = 512 * qb + 128 * qt
                                for k in range(2):
                                    h = 4 * g + 2 * jj + k
                                    tok = mm(PS[:, bank, KC * k:KC * k + KC], qS[0:QH, h, q0:q0 + 128], kS[0:QH, h, 0:KC],
                                             True, True, pf[bank] + self.seg_ready[par], inc=(k == 1))
                                v = PS[:, bank, 0:2 * KC].rearrange("p (k n) -> p k n", k=2)
                                if self.bound is not None:
                                    bd = self.bound[0][:, 8 * b + 4 * qb + qt, :]
                                    tok = tt(dv, v, v, bc(bd.unsqueeze(1), [128, 2, KC]), ALU.min, [tok])
                                e = red(self.m2[:, qt, 2 * jj:2 * jj + 2, 0], v, ALU.max, [tok])
                                pf[bank] = [e]
                            pieces.append(piece)

                def fin1():
                    t = dv.now
                    if nh == 2:
                        t = red(self.nm, self.m2, ALU.max, [t], neg=True)
                    else:
                        t = ts(dv, self.nm, self.m2[:, :, :, 0], -1.0, None, ALU.mult, None, [t])
                    t = cp(dv, self.Mst[:, :, :, 0], self.nm, [t] + st_m["free"])
                    t = tt(dv, self.Mst[:, :, :, 1], self.nm, self.Mst[:, :, :, 0], ALU.subtract, [t])
                    st["m"] = t

                def fin2():
                    pb = PS[:, 7, :].bitcast(BF16)
                    for qt in range(4):
                        tok = tr(pb[:, 128 * qt:128 * qt + 128], self.Mst[:, qt].rearrange("p j r -> p (j r)"), identb,
                                 [st["m"]] + pf[7], inc=(qt == 3))
                    st_m["free"] = [tok]
                    es = []
                    for j in range(4):
                        es.append(cp(dv, qS[QH:QM, 4 * g + j, 512 * qb:512 * qb + 512], pb[32 * j:32 * j + 2, 0:512],
                                     [tok] + self.seg_ready[par]))
                    pf[7] = es
                    self.m_ready[u] = es
                st_m = self.st_m
                pieces.append(fin1)
                pieces.append(fin2)
                return pieces

            def exp_unit(self, s, g, qb, u, side):
                par, b, hh = s % 2, s // 2, s % 2
                qS, kS, vE = self.qS[par], self.kS[par], self.vE[par]
                nk = 4 * (qb + 1) if self.causal else self.nk
                q0 = 512 * qb
                steps = [(t, jj) for t in range(nk) for jj in range(2)]
                pend = None
                mw = self.m_ready[u]

                def pv(item):
                    t, jj, rows, lo, par2, tok = item
                    for k in range(2):
                        j = 2 * jj + k
                        x = mm(PS[32 * j:32 * j + 32, 6, lo:512], vE[0:rows, t, 4 * g + j, :],
                               self.P[par2][0:rows, k, lo:512], t == 0, t == nk - 1, [tok] + (pf[6] if t == 0 else []),
                               inc=(k == 1), tile=(0, 32 * j))
                    self.p_free[par2] = [x]
                    return x
                last = None
                for n, (t, jj) in enumerate(steps):
                    rows = min(128, self.KV - 128 * t)
                    lo = 0
                    diag = self.causal and t >= 4 * qb
                    if diag:
                        lo = 128 * (t - 4 * qb)
                    pr = n % 2
                    for k in range(2):
                        h = 4 * g + 2 * jj + k
                        bank = 2 * pr + k
                        tok = mm(PS[0:rows, bank, lo:512], kS[0:QM, h, 128 * t:128 * t + rows], qS[0:QM, h, q0 + lo:q0 + 512],
                                 True, not diag, pf[bank] + mw, inc=(k == 1 and not diag))
                        if diag:
                            tok = mm(PS[0:rows, bank, lo:lo + 128], identb, maskT, False, True, (), inc=(k == 1))
                    v = PS[0:rows, 2 * pr:2 * pr + 2, lo:512]
                    if self.bound is not None:
                        bt = self.bound[1][0:rows, t, b * S + q0:b * S + q0 + 512]
                        tok = tt(dv, v, v, bc(bt.unsqueeze(1), [rows, 2, 512]), ALU.min, [tok])
                    e = act(self.P[pr][0:rows, :, lo:512], v, ACT.Exp, [tok] + self.p_free[pr], scale=0.25)
                    pf[2 * pr] = [e]
                    pf[2 * pr + 1] = [e]
                    if pend is not None:
                        pv(pend)
                    pend = (t, jj, rows, lo, pr, e)
                    side(n, len(steps))
                last = pv(pend)
                w = cp(dv, self.Oc, PS[:, 6, :], [last] + self.oc_free)
                pf[6] = [w]
                for qt in range(4):
                    tok = tr(PS[:, 7, 128 * qt:128 * qt + 128], self.Oc[:, 128 * qt:128 * qt + 128], ident,
                             [w] + pf[7], inc=(qt == 3))
                self.oc_free = [tok]
                pv4 = PS[:, 7, :].rearrange("p (t j d) -> p t j d", t=4, j=4)
                r = recip(self.ri, pv4[:, :, :, 16:17], [tok, dv.now])
                i0 = 8 * b + 4 * qb
                c0 = 128 * hh + 64 * g
                o = self.O[:, i0:i0 + 4, c0:c0 + 64].rearrange("p t (j d) -> p t j d", j=4)
                e = tt(dv, o, pv4[:, :, :, 0:16], bc(self.ri, [128, 4, 4, 16]), ALU.mult, [r])
                pf[7] = [e]
                return [last, e]

            def run(self):
                self.m_ready = {}
                self.st_m = {"free": []}
                self.oc_free = []
                units = [(s, g, qb) for s in range(4) for g in range(2) for qb in range(2)]
                for p in self.prep(0):
                    p()
                for p in self.max_pieces(*units[0], 0):
                    p()
                pre = []
                users = {0: [], 1: []}
                for u, (s, g, qb) in enumerate(units):
                    if u % 4 == 0:
                        for p in pre:
                            p()
                        pre = []
                        if s + 1 < 4:
                            self.seg_free[(s + 1) % 2] = users[(s + 1) % 2]
                            users[(s + 1) % 2] = []
                            pre = self.prep(s + 1)
                    nxt = []
                    if u + 1 < len(units):
                        if (u + 1) % 4 == 0:
                            nxt = pre + self.max_pieces(*units[u + 1], u + 1)
                            pre = []
                        else:
                            k = (len(pre) + 3 - u % 4 - 1) // max(1, 4 - u % 4 - 1 + 0) if u % 4 < 3 else len(pre)
                            k = min(k, len(pre))
                            mx = self.max_pieces(*units[u + 1], u + 1)
                            own, pre = pre[:k], pre[k:]
                            nxt = []
                            body, tail = mx[:-2], mx[-2:]
                            tot = len(body) + len(own)
                            bi = oi = 0
                            for z in range(tot):
                                if oi < len(own) and oi * tot <= z * len(own):
                                    nxt.append(own[oi])
                                    oi += 1
                                elif bi < len(body):
                                    nxt.append(body[bi])
                                    bi += 1
                                else:
                                    nxt.append(own[oi])
                                    oi += 1
                            nxt += tail
                    at = [0]

                    def side(n, of, nxt=nxt, at=at):
                        want = (n + 1) * len(nxt) // of
                        while at[0] < want:
                            nxt[at[0]]()
                            at[0] += 1
                    users[s % 2] = users[s % 2] + self.exp_unit(s, g, qb, u, side)
                    users[s % 2] = users[s % 2][-4:] + [pe.now]

        def out_proj(att, wo, bias, dst, wtok):
            barrier()
            toks = to_T(lambda i, c: att.O[:, i, 128 * c:128 * c + 128],
                        lambda c, k: XNT[:, c, 512 * k:512 * k + 512], 2, lambda i: [])
            pe.after(toks + [wtok])
            add_proj(dst, lambda c, i: XNT[:, c, 128 * i:128 * i + 128], 2, wo, bias)

        def plain_qkv(wq, wkv, bias, wtok, kvT=None):
            def f(b, hh, t, rows, hq, hk, ps, w):
                pe.after([wtok])
                r0 = b * S + 128 * t
                tok = None
                if hq and hk:
                    for c in range(2):
                        tok = mm(ps[:, 0:384], XNT[:, c, r0:r0 + 128], wq(c, hh, 0, 384), c == 0, c == 1 and bias is None, w,
                                 inc=(c == 1 and bias is None))
                    if bias is not None:
                        tok = mm(ps[:, 0:384], ones[0:1, 0:128], bias[:, hh, 0:384], False, True, (), inc=True)
                    return tok
                if hq:
                    src, lo, hi = (lambda c: XNT[:, c, r0:r0 + 128]), 0, 128
                else:
                    k0 = KC * b + 128 * t
                    src, lo, hi = (lambda c: ctxT[:, c, k0:k0 + rows]), 128, 384
                for c in range(2):
                    tok = mm(ps[:, lo:hi], src(c), wq(c, hh, lo, hi), c == 0, c == 1 and bias is None, w,
                             inc=(c == 1 and bias is None))
                if bias is not None:
                    tok = mm(ps[:, lo:hi], ones[0:1, 0:rows], bias[:, hh, lo:hi], False, True, (), inc=True)
                return tok
            return f

        def w_seg(wap):
            v = wap.rearrange("p (c s n) -> p c s n", c=2, s=2)
            return lambda c, hh, lo, hi: v[:, c, hh, lo:hi]

        def w_rows(wap, n=256):
            v = wap.rearrange("p (c n) -> p c n", n=n)
            return lambda c: v[:, c, :]

        W = {}

        def load_0():
            WB[0].clear()
            W[0] = load_w(WB[0], "pk0")

        def phase_0():
            w, wt = W[0]
            dkv = w[:, 0:128].rearrange("p (c n) -> p c n", c=2)
            ukv = w[0:64, 128:640].rearrange("p (s n) -> p s n", s=2)
            uq = w[:, 640:1152].rearrange("p (c n) -> p c n", c=2)
            wo = w_rows(w[:, 1152:1664])
            layer_norm_T()
            ckv = scr.take([2048])
            pe.after([wt])
            for k in range(4):
                for c in range(2):
                    t = mm(PS[0:64, k, :], dkv[:, c, :], XNT[:, c, 512 * k:512 * k + 512], c == 0, c == 1, pf[k], inc=(c == 1))
                t = cp(evac_lane(), ckv[0:64, 512 * k:512 * k + 512], PS[0:64, k, :], [t])
                pf[k] = [t]
            barrier()

            def qkv(b, hh, t, rows, hq, hk, ps, w):
                r0 = b * S + 128 * t
                for c in range(2):
                    mm(ps[:, 0:128], XNT[:, c, r0:r0 + 128], uq[:, c, 128 * hh:128 * hh + 128], c == 0, c == 1, w)
                return mm(ps[:, 128:384], ckv[0:64, r0:r0 + 128], ukv[:, hh, :], True, True, (), inc=True)
            att = Attention(S, True, qkv)
            att.run()
            out_proj(att, wo, None, X, wt)

        def load_1():
            WA.clear()
            WB[1].clear()
            W[1] = [load_w(WA, "pk1"), load_w(WB[1], "pk1o"), (scr_mask(), None)]

        def scr_mask():
            return None

        def phase_1():
            (wa, ta), (wb, tb), _ = W[1]
            wq = wa[:, 0:2112].rearrange("p (c h n) -> p c h n", c=2, h=16)
            wk = wa[:, 2112:4224].rearrange("p (c h n) -> p c h n", c=2, h=16)
            wv = wa[:, 4224:6272].rearrange("p (c n) -> p c n", c=2)
            g = wa[:, 6272:6280].rearrange("p (z c) -> p z c", z=4)
            wo = wb[:, 0:2048].rearrange("p (k n) -> p k n", k=8)
            for q in lanes:
                q.after([ta, tb])
            layer_norm_T(mul=lambda c: g[:, 0, c:c + 1], add=lambda c: g[:, 1, c:c + 1], twice=True)
            fT = scr.take([2, 308])
            mk = scr.take([308])
            onh = scr.take([66])
            onhz = scr.take([66])
            lm = Load("d_mask")
            mk8 = scr.take([308 // 4 + 1])
            ct = scr.take([4, D])
            m8 = mk8.bitcast(U8)[0:1, 0:308]
            lm.add(m8, ins["mask8"])
            for b in range(2):
                lm.add(ct[:, 2 * b, :], ins["ctx"][b, 0:128, :])
                lm.add(ct[0:26, 2 * b + 1, :], ins["ctx"][b, 128:154, :])
            dv.after([lm.ready])
            mk_t = ts(dv, mk[0:1, 0:308], m8, -1.0, -NEG, ALU.add, ALU.mult)
            for b in range(2):
                for z in range(2):
                    rows = 128 if z == 0 else 26
                    i = 2 * b + z
                    mv, rs = stats(lambda _, i=i, rows=rows: ct[0:rows, i, :], 1, scr, 1e-5, rows=rows)
                    t = normalise(ct[0:rows, i, :], ct[0:rows, i, :], mv, rs, 0, rows)
                    for c in range(2):
                        p = tr(PS[:, 0, 128 * c:128 * c + rows], ct[0:rows, i, 128 * c:128 * c + 128], ident[0:rows, 0:rows],
                               [t] + pf[0], inc=(c == 1))
                    for c in range(2):
                        t = ts(dv, fT[:, c, KC * b + 128 * z:KC * b + 128 * z + rows], PS[:, 0, 128 * c:128 * c + rows],
                               g[:, 2, c:c + 1], g[:, 3, c:c + 1], ALU.mult, ALU.add, [p])
                    pf[0] = [t]
            t = fill(dv, onh[0:1, :], 0.0)
            fill(dv, onh[0:1, 65:66], 1.0, [t])
            KV = S + KC
            vE = scr.take([10, 8, 65])
            qT = [scr.take([S]) for _ in range(2)]
            kT = [scr.take([KV]) for _ in range(2)]
            qB = [scr.take([S], BF16) for _ in range(2)]
            kB = [scr.take([KV], BF16) for _ in range(2)]
            P = [scr.take([2, 512]) for _ in range(2)]
            O = scr.take([8, 512])
            OT = scr.take([2, 4, 128])
            Mst = scr.take([8, 66])
            m2 = scr.take([8, 3])
            nm = scr.take([8])
            Oc = scr.take([512])
            ri = scr.take([4, 1])
            fill(gp, vE[:, :, :, 64:65], 1.0)
            fill(gp, Mst, 0.0)
            barrier()

            def kvsrc(b, t, c):
                if t < 8:
                    return XNT[:, c, b * S + 128 * t:b * S + 128 * t + 128]
                lo = KC * b + 128 * (t - 8)
                return fT[:, c, lo:lo + (128 if t == 8 else 26)]
            kvrows = [128] * 9 + [26]
            st = {"p": [[], []], "oc": [], "qk_free": [[], []], "mst": [], "o_free": [], "slot": 0}

            def prep(b, h, x, hd):
                pcs = []
                hd["rdy"] = []
                for k in range(2):
                    def pq(k=k):
                        for c in range(2):
                            tok = mm(PS[0:66, 7, :], wq[:, c, h, :], XNT[:, c, b * S + 512 * k:b * S + 512 * k + 512],
                                     c == 0, c == 1, pf[7], inc=(c == 1))
                        a = ts(dv, qT[x][0:66, 512 * k:512 * k + 512], PS[0:66, 7, :], kb65[0:66], None, ALU.add, None,
                               [tok] + st["qk_free"][x])
                        e = cp(gp, qB[x][0:66, 512 * k:512 * k + 512], qT[x][0:66, 512 * k:512 * k + 512], [a])
                        pf[7] = [a]
                        hd["rdy"] += [a, e]
                    pcs.append(pq)
                for k in range(3):
                    def pk(k=k):
                        n = 512 if k < 2 else KC
                        for c in range(2):
                            src = XNT[:, c, b * S + 512 * k:b * S + 512 * k + 512] if k < 2 else fT[:, c, KC * b:KC * b + KC]
                            tok = mm(PS[0:66, 7, 0:n], wk[:, c, h, :], src, c == 0, c == 1 and k < 2, pf[7], inc=(c == 1 and k < 2))
                        if k == 2:
                            tok = mm(PS[0:66, 7, 0:n], onh[0:1, 0:66], mk[0:1, KC * b:KC * b + KC], False, True, (), inc=True)
                        a = ts(dv, kT[x][0:66, 512 * k:512 * k + n], PS[0:66, 7, 0:n], kb64[0:66], None, ALU.add, None,
                               [tok] + st["qk_free"][x])
                        e = cp(gp, kB[x][0:66, 512 * k:512 * k + n], kT[x][0:66, 512 * k:512 * k + n], [a])
                        pf[7] = [a]
                        hd["rdy"] += [a, e]
                    pcs.append(pk)
                for qt in range(8):
                    def mx(qt=qt):
                        for k in range(3):
                            n = 512 if k < 2 else KC
                            bank = 4 + st["slot"] % 2
                            st["slot"] += 1
                            tok = mm(PS[:, bank, 0:n], qB[x][0:66, 128 * qt:128 * qt + 128], kB[x][0:66, 512 * k:512 * k + n],
                                     True, True, pf[bank] + hd["rdy"], inc=True)
                            e = red(m2[:, qt, k:k + 1], PS[:, bank, 0:n], ALU.max, [tok] + st["mst"])
                            pf[bank] = [e]
                    pcs.append(mx)

                def fin1():
                    t = red(nm, m2, ALU.max, [dv.now], neg=True)
                    t = cp(dv, Mst[:, :, 64], nm, [t] + st["mst"])
                    hd["m"] = t
                pcs.append(fin1)

                def fin2():
                    es = []
                    for k in range(2):
                        for j in range(4):
                            tok = tr(PS[0:66, 7, 128 * j:128 * j + 128], Mst[:, 4 * k + j, :], ident, [hd["m"]] + pf[7], inc=(j == 3))
                        e = cp(dv, qT[x][64:65, 512 * k:512 * k + 512], PS[64:65, 7, :], [tok] + hd["rdy"])
                        pf[7] = [e]
                        es.append(e)
                    st["mst"] = [tok]
                    hd["m_rdy"] = es
                pcs.append(fin2)
                return pcs

            def v_half(b, hh, w):
                for t in range(10):
                    bank = 4 + t % 3
                    rows = kvrows[t]
                    for c in range(2):
                        tok = mm(PS[0:rows, bank, :], kvsrc(b, t, c), wv[:, c, 512 * hh:512 * hh + 512], c == 0, c == 1,
                                 pf[bank], inc=(c == 1))
                    e = cp(evac_lane(), vE[0:rows, t, :, 0:64], PS[0:rows, bank, :].rearrange("p (h d) -> p h d", h=8), [tok] + w)
                    pf[bank] = [e]
                    v_rdy.append(e)
            v_rdy = []

            def exp_head(b, h, x, hd, side):
                hl = h % 8
                qk = hd["m_rdy"] + hd["rdy"]
                steps = []
                for qb in range(2):
                    for pr in range(5):
                        steps.append((qb, pr))
                pend = []

                def pv():
                    qb, pr, px, toks = pend.pop(0)
                    for k in range(2):
                        t = 2 * pr + k
                        rows = kvrows[t]
                        tok = mm(PS[0:65, 6, :], vE[0:rows, t, hl, :], P[px][0:rows, k, :], t == 0, t == 9,
                                 toks + v_rdy + (pf[6] if t == 0 else []), inc=(k == 1))
                    st["p"][px] = [tok]
                    if pr == 4:
                        w = cp(dv, Oc[0:65, :], PS[0:65, 6, :], [tok] + st["oc"])
                        pf[6] = [w]
                        for j in range(4):
                            tok = tr(PS[:, 7, 128 * j:128 * j + 65], Oc[0:65, 128 * j:128 * j + 128], ident[0:65, 0:65],
                                     [w] + pf[7], inc=(j == 3))
                        st["oc"] = [tok]
                        v4 = PS[:, 7, :].rearrange("p (t d) -> p t d", t=4)
                        r = recip(ri, v4[:, :, 64:65], [tok, dv.now])
                        e = tt(dv, O[:, 4 * qb:4 * qb + 4, 64 * hl:64 * hl + 64], v4[:, :, 0:64], bc(ri, [128, 4, 64]),
                               ALU.mult, [r] + st["o_free"])
                        pf[7] = [e]
                for n, (qb, pr) in enumerate(steps):
                    px = n % 2
                    for k in range(2):
                        t = 2 * pr + k
                        rows = kvrows[t]
                        tok = mm(PS[0:rows, 2 * px + k, :], kT[x][0:66, 128 * t:128 * t + rows],
                                 qT[x][0:66, 512 * qb:512 * qb + 512], True, True, pf[2 * px + k] + qk, inc=True)
                    if pr < 4:
                        e = [act(P[px], PS[:, 2 * px:2 * px + 2, :], ACT.Exp, [tok] + st["p"][px], scale=0.125)]
                    else:
                        e = [act(P[px][:, 0, :], PS[:, 2 * px, :], ACT.Exp, [tok] + st["p"][px], scale=0.125),
                             act(P[px][0:26, 1, :], PS[0:26, 2 * px + 1, :], ACT.Exp, [], scale=0.125)]
                    pf[2 * px] = e
                    pf[2 * px + 1] = e
                    if pend:
                        pv()
                    pend.append((qb, pr, px, e))
                    side(n, len(steps))
                pv()
                st["qk_free"][x] = [pe.now]

            order = [(b, hh, h) for b in range(2) for hh in range(2) for h in range(8 * hh, 8 * hh + 8)]
            hds = [{} for _ in order]
            for p in prep(order[0][0], order[0][2], 0, hds[0]):
                p()
            for n, (b, hh, h) in enumerate(order):
                if h % 8 == 0:
                    v_rdy.clear()
                    v_half(b, hh, [pe.now])
                nxt = []
                if n + 1 < len(order):
                    nxt = prep(order[n + 1][0], order[n + 1][2], (n + 1) % 2, hds[n + 1])
                at = [0]

                def side(i, of, nxt=nxt, at=at):
                    while at[0] < (i + 1) * len(nxt) // of:
                        nxt[at[0]]()
                        at[0] += 1
                exp_head(b, h, n % 2, hds[n], side)
                if h % 8 == 7:
                    ot_free = [[], []]
                    odone = dv.now
                    for i in range(8):
                        x = i % 2
                        for c in range(4):
                            tok = tr(PS[:, 4 + x, 128 * c:128 * c + 128], O[:, i, 128 * c:128 * c + 128], ident,
                                     pf[4 + x] + [odone], inc=(c == 3))
                        e = cp(evac_lane(), OT[:, x], PS[:, 4 + x, :].rearrange("p (c n) -> p c n", c=4), [tok] + ot_free[x])
                        pf[4 + x] = [e]
                        for c in range(4):
                            tok = mm(PS[:, 6, 0:256], OT[:, x, c, :], wo[:, 4 * hh + c, :], c == 0, c == 3, pf[6] + [e], inc=(c == 3))
                        ot_free[x] = [tok]
                        xv = X[:, 8 * b + i, :]
                        e = tt(dv, xv, PS[:, 6, 0:256], xv, ALU.add, [tok, dv.now])
                        pf[6] = [e]
                    st["o_free"] = [pe.now]

        def softmax8(l, heap, w=()):
            mx = heap.take([NT])
            p = heap.take([NT, 8])
            s = heap.take([NT])
            r = heap.take([NT])
            t = red(mx, l, ALU.max, w)
            t = tt(dv, p, l, bc(mx.unsqueeze(2), [128, NT, 8]), ALU.subtract, [t])
            t = act(p, p, ACT.Exp, [t])
            t = red(s, p, ALU.add, [t])
            t = recip(r, s, [t])
            return p, r, t

        def first_max(l, heap, w=()):
            mx = heap.take([NT])
            sc = heap.take([NT, 8])
            oh = heap.take([NT, 8])
            t = red(mx, l, ALU.max, w)
            t = tt(dv, sc, l, bc(mx.unsqueeze(2), [128, NT, 8]), ALU.is_equal, [t])
            t = tt(dv, sc, sc, bc(rev.unsqueeze(1), [128, NT, 8]), ALU.mult, [t])
            t = red(mx, sc, ALU.max, [t])
            t = tt(dv, oh, sc, bc(mx.unsqueeze(2), [128, NT, 8]), ALU.is_equal, [t])
            return oh, t

        def logits8(wr, bias, heap):
            for i in range(NT):
                o = PS[:, 0, 8 * i:8 * i + 8]
                for c in range(2):
                    t = mm(o, XNT[:, c, 128 * i:128 * i + 128], wr(c), c == 0, c == 1 and bias is None, pf[0], inc=(i == NT - 1 and c == 1))
                if bias is not None:
                    t = mm(o, ones[0:1, 0:128], bias, False, True, (), inc=(i == NT - 1))
            l = heap.take([NT, 8])
            t = cp(dv, l, PS[:, 0, 0:128].rearrange("p (i e) -> p i e", e=8), [t])
            pf[0] = [t]
            return l, t

        def load_2():
            WA.clear()
            W[2] = load_w(WA, "pk2")

        def phase_2():
            w, wt = W[2]
            ew = w[:, 0:4096].rearrange("p (c e n) -> p c e n", c=2, e=8)
            rw = w[:, 4096:4112].rearrange("p (c n) -> p c n", c=2)
            rb = w[0:1, 4112:4120]
            lb = Load("d_eb")
            eb = scr.take([2048], F32, 0, 1)
            lb.add(eb, ins["pk2e"])
            layer_norm_T()
            for q in lanes:
                q.after([wt, lb.ready])
            l, t = logits8(lambda c: rw[:, c, :], rb, scr)
            p, r, t = softmax8(l, scr, [t])
            t2 = tt(dv, p, p, bc(r.unsqueeze(2), [128, NT, 8]), ALU.mult, [t])
            oh, t = first_max(p, scr, [t2])
            G = scr.take([NT, 8])
            t = tt(dv, G, oh, p, ALU.mult, [t])
            last = t
            n = 0
            for i in range(NT):
                for e2 in range(4):
                    b = n % 8
                    n += 1
                    for c in range(2):
                        mm(PS[:, b, :], XNT[:, c, 128 * i:128 * i + 128], ew[:, c, 2 * e2:2 * e2 + 2, :].rearrange("p e n -> p (e n)"),
                           c == 0, False, pf[b])
                    t = mm(PS[:, b, :], ones[0:1, 0:128], eb[0:1, 512 * e2:512 * e2 + 512], False, True, (), inc=True)
                    for k in range(2):
                        t2 = stt(X[:, i, :], PS[:, b, 256 * k:256 * k + 256], G[:, i, 2 * e2 + k:2 * e2 + k + 1], X[:, i, :],
                                 ALU.mult, ALU.add, [t, last])
                        last = t2
                    pf[b] = [t2]

        def load_3():
            WB[0].clear()
            W[3] = load_w(WB[0], "pk3")

        def phase_3():
            w, wt = W[3]
            wqkv = w[:, 0:1536].rearrange("p (c n) -> p c n", c=2)
            wo = w_rows(w[:, 1536:2048])
            rows = scr.take([1024], F32, 0, 1)
            lr = Load("d_pk3r")
            lr.add(rows, ins["pk3r"])
            layer_norm_T()
            qk = [scr.take([2, 768]) for _ in range(2)]
            pr = [scr.take([2, 2, D]) for _ in range(2)]
            sc = [scr.take([2, 2, 16]) for _ in range(2)]
            mx = [scr.take([2, 16]) for _ in range(2)]
            O = scr.take([NT, D])
            ex = [scr.take([2, 2, 16]) for _ in range(2)]
            for q in lanes:
                q.after([wt, lr.ready])
            fr = [[], []]
            for i in range(8):
                x = i % 2
                ts_ = []
                for b in range(2):
                    for z in range(2):
                        bank = 4 * x + 2 * b + z
                        lo, hi = (0, 512) if z == 0 else (512, 768)
                        for c in range(2):
                            mm(PS[:, bank, 0:hi - lo], XNT[:, c, b * S + 128 * i:b * S + 128 * i + 128], wqkv[:, c, lo:hi], c == 0, False, pf[bank])
                        t = mm(PS[:, bank, 0:hi - lo], ones[0:1, 0:128], rows[0:1, lo:hi], False, True, (), inc=True)
                        t = cp(ac, qk[x][:, b, lo:hi], PS[:, bank, 0:hi - lo], [t] + fr[x])
                        pf[bank] = [t]
                Q, K, V = qk[x][:, :, 0:256], qk[x][:, :, 256:512], qk[x][:, :, 512:768]
                d0 = [t, dv.now]
                for r in range(2):
                    t = tt(dv, pr[x][:, r], bc(Q[:, r:r + 1, :], [128, 2, 256]), K, ALU.mult, d0)
                t = red(sc[x], pr[x].rearrange("p r c (h d) -> p (r c) h d", d=16), ALU.add, [t])
                t = tt(dv, mx[x], sc[x][:, :, 0, :], sc[x][:, :, 1, :], ALU.max, [t])
                t = tt(dv, sc[x], sc[x], bc(mx[x].unsqueeze(2), [128, 2, 2, 16]), ALU.subtract, [t])
                t = act(ex[x], sc[x], ACT.Exp, [t], scale=0.25)
                t = tt(dv, mx[x], ex[x][:, :, 0, :], ex[x][:, :, 1, :], ALU.add, [t])
                t = recip(mx[x], mx[x], [t])
                t = tt(dv, ex[x], ex[x], bc(mx[x].unsqueeze(2), [128, 2, 2, 16]), ALU.mult, [t])
                for r in range(2):
                    for c in range(2):
                        tt(dv, pr[x][:, r, c].rearrange("p (h d) -> p h d", d=16),
                           V[:, c].rearrange("p (h d) -> p h d", d=16), bc(ex[x][:, r, c].unsqueeze(2), [128, 16, 16]), ALU.mult, [t])
                t2 = dv.now
                for r in range(2):
                    t = tt(dv, O[:, 8 * r + i, :], pr[x][:, r, 0], pr[x][:, r, 1], ALU.add, [t2])
                fr[x] = [t]
            barrier()
            to_T(lambda i, c: O[:, i, 128 * c:128 * c + 128], lambda c, k: XNT[:, c, 512 * k:512 * k + 512], 2, lambda i: [])
            barrier()
            add_proj(X, lambda c, i: XNT[:, c, 128 * i:128 * i + 128], 2, wo, rows[0:1, 768:1024])

        def load_4():
            WB[1].clear()
            W[4] = load_w(WB[1], "pk4")

        def phase_4():
            w, wt = W[4]
            wq = w_seg(w[:, 0:1536])
            wo = w_rows(w[:, 1536:2048])
            rows = scr.take([1024], F32, 0, 1)
            lr = Load("d_pk4r")
            lr.add(rows, ins["pk4r"])
            layer_norm_T()
            pe.after([lr.ready])
            att = Attention(KC, False, plain_qkv(wq, None, rows[:, 0:768].rearrange("p (s n) -> p s n", s=2), wt))
            att.run()
            out_proj(att, wo, rows[0:1, 768:1024], X, wt)

        def load_5():
            WA.clear()
            W[5] = load_w(WA, "pk5", dt=I32)

        def phase_5():
            wi, wt = W[5]
            wf = wi.bitcast(F32)
            for q in lanes:
                q.after([wt])
            for k in range(3):
                ts([dv, gp, dv][k], wf[:, 1536 * k:1536 * k + 1536], wi[:, 1536 * k:1536 * k + 1536], 1.0 / 127.0, None, ALU.mult, None)
            wg = wf[:, 0:1536].rearrange("p (c n) -> p c n", c=2)
            wu = wf[:, 1536:3072].rearrange("p (c n) -> p c n", c=2)
            wd = wf[:, 3072:4608].rearrange("p (f n) -> p f n", f=6)
            layer_norm_T()
            for q in lanes:
                q.after([gp.now])
            hT = [scr.take([6, 512]) for _ in range(2)]
            sg = [scr.take([512]) for _ in range(2)]
            swiglu(4, 6, lambda f, c: wg[:, c, 128 * f:128 * f + 128], lambda f, c: wu[:, c, 128 * f:128 * f + 128], hT, sg,
                   lambda f: wd[:, f, :], None, X)

        swi = {"n": 0, "sgf": [[], []], "hf": [[], []], "pend": None, "last": {}}

        def swiglu_reset():
            swi.update({"n": 0, "sgf": [[], []], "hf": [[], []], "pend": None, "last": {}})

        def swiglu_down(item):
            hT, x, nf, wd, gate, dst, k, hr = item
            for i2 in range(2):
                b = 4 + (2 * k + i2) % 4
                for z in range(2):
                    i = 2 * i2 + z
                    for f in range(nf):
                        t = mm(PS[:, b, 256 * z:256 * z + 256], hT[x][:, f, 128 * i:128 * i + 128], wd(f), f == 0, f == nf - 1,
                               pf[b] + hr, inc=(f == nf - 1))
                i = 4 * k + 2 * i2
                if gate is None:
                    v = dst[:, i:i + 2, :]
                    e = tt(dv, v, PS[:, b, :].rearrange("p (k c) -> p k c", k=2), v, ALU.add, [t])
                else:
                    for z in range(2):
                        e = stt(dst[:, i + z, :], PS[:, b, 256 * z:256 * z + 256], gate(i + z), dst[:, i + z, :], ALU.mult, ALU.add,
                                [t] + swi["last"].get(i + z, []))
                        swi["last"][i + z] = [e]
                pf[b] = [e]
            swi["hf"][x] = [t]

        def swiglu(nblk, nf, wg, wu, hT, sg, wd, gate, dst, finish=True):
            for k in range(nblk):
                x = swi["n"] % 2
                swi["n"] += 1
                hr = []
                for f in range(nf):
                    y = f % 2
                    for z, w in ((0, wg), (1, wu)):
                        for c in range(2):
                            t = mm(PS[:, 2 * y + z, :], w(f, c), XNT[:, c, 512 * k:512 * k + 512], c == 0, c == 1, pf[2 * y + z], inc=(c == 1))
                        if z == 0:
                            a = act(sg[y], PS[:, 2 * y, :], ACT.Silu, [t] + swi["sgf"][y])
                            pf[2 * y] = [a]
                    e = tt(dv, hT[x][:, f, :], PS[:, 2 * y + 1, :], sg[y], ALU.mult, [t, a] + swi["hf"][x])
                    pf[2 * y + 1] = [e]
                    swi["sgf"][y] = [e]
                    hr.append(e)
                if swi["pend"] is not None:
                    swiglu_down(swi["pend"])
                swi["pend"] = (hT, x, nf, wd, gate, dst, k, hr)
            if finish:
                swiglu_down(swi["pend"])
                swi["pend"] = None

        def load_6():
            WB[0].clear()
            W[6] = [load_w(WB[0], "pk6b")]

        def phase_6():
            WA.clear()
            wa, ta = load_w(WA, "pk6")
            wb, tb = W[6][0]
            at = [0]

            def part(n):
                v = wa[:, at[0]:at[0] + n]
                at[0] += n
                return v
            inp = part(2048).rearrange("p (c n) -> p c n", c=2)
            xpw = part(192).rearrange("p (c n) -> p c n", c=4)
            opw = part(1024).rearrange("p (c n) -> p c n", c=4)
            fw1 = part(2048).rearrange("p (c n) -> p c n", c=2)
            dtw = part(512)
            cw = part(16).rearrange("p (c n) -> p c n", c=4)
            cb = part(4)
            dtb = part(4)
            alog = part(64).rearrange("p (c n) -> p c n", c=4)
            Dc = part(4)
            lg = part(2)
            lb = part(2)
            fb1 = part(8)
            fb2 = part(256)
            fw2 = wb.rearrange("p (c n) -> p c n", c=8)
            layer_norm_T()
            for q in lanes:
                q.after([ta, tb])
            u = scr.take([4, S])
            de = scr.take([4, S])
            du = scr.take([4, S])
            dbl = scr.take([S])
            MO = scr.take([NT, D])
            dA = [scr.take([4, 512]) for _ in range(2)]
            dB = [scr.take([4, 512]) for _ in range(2)]
            Cs = [scr.take([512]) for _ in range(3)]
            bcs = scr.take([S], BF16)
            eye3 = scr.take([32], BF16)
            PC = 4
            h = [scr.take([4, 512]) for _ in range(2)]
            xp = [h[k].rearrange("p a b -> p (a b)")[:, 0:1027] for k in range(2)]
            hl = scr.take([16, 4])
            An = scr.take([4, 16])
            rbc = dB[0][:, 0, :]
            mid = dB[0][:, 1, 0:256].bitcast(BF16)
            for k in range(3):
                cp(dv, eye3[32 * k:32 * k + 32, :], ident[0:32, 0:32])
            t = act(An, alog, ACT.Exp)
            ts(dv, An, An, -1.0, None, ALU.mult, None, [t])
            barrier()
            for sq in range(4):
                if sq == 2:
                    barrier()
                    flipped_T()
                    barrier()
                b = sq % 2
                rev_ = sq >= 2

                def xz(chunk, half, bank):
                    for c in range(2):
                        t = mm(PS[:, bank, :], inp[:, c, 128 * chunk:128 * chunk + 128],
                               XNT[:, c, b * S + 512 * half:b * S + 512 * half + 512], c == 0, c == 1, pf[bank], inc=(c == 1))
                    return t
                z0 = [fill(dv, v[:, 0:3], 0.0) for v in xp]
                xpf = [[], []]
                silu = []
                for c in range(4):
                    x = c % 2
                    for half in range(2):
                        bank = 2 * x + half
                        t = xz(c, half, bank)
                        t = act(xp[x][:, 3 + 512 * half:515 + 512 * half], PS[:, bank, :], ACT.Copy, [t] + xpf[x])
                        pf[bank] = [t]
                    t = ts(dv, u[:, c, :], xp[x][:, 0:S], cw[:, c, 0:1], cb[:, c:c + 1], ALU.mult, ALU.add, [t] + z0)
                    for i in range(1, 4):
                        t = stt(u[:, c, :], xp[x][:, i:i + S], cw[:, c, i:i + 1], u[:, c, :], ALU.mult, ALU.add, [t])
                    xpf[x] = [t]
                    silu.append(t)
                for c in range(4):
                    t = act(u[:, c, :], u[:, c, :], ACT.Silu, [silu[c]])
                for half in range(2):
                    for c in range(4):
                        p = mm(PS[0:48, 4 + half, :], xpw[:, c, :], u[:, c, 512 * half:512 * half + 512], c == 0, c == 3, pf[4 + half] + [t], inc=(c == 3))
                    s_ = slice(512 * half, 512 * half + 512)
                    e = cp(ac, dbl[32:48, s_], PS[32:48, 4 + half, :], [p])
                    src = PS[0:32, 4 + half, :]
                    t1 = cp(dv, bcs[0:32, s_], src, [p, e])
                    t1 = tt(dv, rbc[0:32, 0:512], src, bcs[0:32, s_], ALU.subtract, [t1])
                    pf[4 + half] = [e, t1]
                    t2 = cp(dv, bcs[32:64, s_], rbc[0:32, 0:512], [t1])
                    t2 = cp(dv, mid[0:32, 0:512], rbc[0:32, 0:512], [t1])
                    t2 = tt(dv, bcs[64:96, s_], rbc[0:32, 0:512], mid[0:32, 0:512], ALU.subtract, [t2])
                    pe.after([t2])
                    dv.after([t2])
                n = 0
                for c in range(4):
                    for half in range(2):
                        bank = n % 4
                        n += 1
                        p = mm(PS[:, bank, :], dtw[32:48, 128 * c:128 * c + 128], dbl[32:48, 512 * half:512 * half + 512], True, True, pf[bank] + [e], inc=True)
                        s_ = slice(512 * half, 512 * half + 512)
                        a = act(de[:, c, s_], PS[:, bank, :], ACT.Abs, [p], bias=dtb[:, c:c + 1])
                        m = ts(dv, du[:, c, s_], PS[:, bank, :], dtb[:, c:c + 1], 0.0, ALU.add, ALU.max, [p, a])
                        pf[bank] = [a, m]
                t = act(de, de, ACT.Exp, [ac.now], scale=-1.0)
                t = act(de, de, ACT.Ln, [t], bias=ones[:, 0:1])
                t = tt(dv, de, de, du, ALU.add, [t, dv.now])
                t = tt(dv, du, de, u, ALU.mult, [t])
                dv.after([t])
                ac.after([t])
                seq = [(half, n) for half in range(2) for n in range(16)]
                dAf, dBf, hf, cf, Bf = [[], []], [[], []], [[], []], [[], [], []], [[], []]
                made = {}

                def spread(k):
                    half, n = seq[k]
                    x = k % 2
                    s_ = slice(512 * half, 512 * half + 512)
                    pb = mm(PS[:, 4 + x, :], bc(eye3[0:96, n:n + 1], [96, 128]), bcs[0:96, s_], True, True, pf[4 + x], inc=True)
                    pc = mm(PS[:, 6 + x, :], bc(eye3[0:96, 16 + n:17 + n], [96, 128]), bcs[0:96, s_], True, True, pf[6 + x], inc=True)
                    for c in range(4):
                        a = act(dA[x][:, c, :], de[:, c, s_], ACT.Exp, dAf[x], scale=An[:, c, n:n + 1])
                    c_ = act(Cs[k % 3], PS[:, 6 + x, :], ACT.Copy, [pc] + cf[k % 3])
                    pf[6 + x] = [c_]
                    made[k] = (pb, a, c_)

                def bu(k):
                    half, n = seq[k]
                    x = k % 2
                    s_ = slice(512 * half, 512 * half + 512)
                    t = tt(dv, dB[x], du[:, :, s_], bc(PS[:, 4 + x, :].unsqueeze(1), [128, 4, 512]), ALU.mult, [made[k][0]] + dBf[x])
                    pf[4 + x] = [t]
                    Bf[x] = [t]
                yw = {}

                def ysum(k):
                    half, n = seq[k]
                    for c in range(4):
                        y = mm(PS[:, c, :], ident, h[k % 2][:, c, :], n == 0, n == 15, yw[k] + (pf[c] if n == 0 else []), inc=(c == 3))
                    return y

                def out_half(half, y):
                    s_ = slice(512 * half, 512 * half + 512)
                    for c in range(4):
                        t = stt(du[:, c, s_], u[:, c, s_], Dc[:, c:c + 1], PS[:, c, :], ALU.mult, ALU.add, [y, dv.now])
                        pf[c] = [t]
                spread(0)
                spread(1)
                bu(0)
                for k, (half, n) in enumerate(seq):
                    x = k % 2
                    if k == 16:
                        y = ysum(15)
                        hf[1] = [y]
                        out_half(0, y)
                        bu(16)
                    sc = []
                    for c in range(4):
                        ini = 0.0 if half == 0 else hl[:, n, c:c + 1]
                        t2 = dv.put(lambda e, c=c, x=x, ini=ini: e.tensor_tensor_scan(
                            out=h[x][:, c, :], data0=dA[x][:, c, :], data1=dB[x][:, c, :], initial=ini, op0=ALU.mult, op1=ALU.add),
                            [made[k][1]] + Bf[x] + hf[x])
                        sc.append(t2)
                    dAf[x] = [t2]
                    dBf[x] = [t2]
                    if k + 1 < 32 and k != 15:
                        bu(k + 1)
                    hw = []
                    if half == 0:
                        hw = [cp(gp, hl[:, n, :], h[x][:, :, 511], [t2])]
                    c3 = bc(Cs[k % 3].unsqueeze(1), [128, PC, 512])
                    g = [tt(gp, h[x][:, 0:PC, :], h[x][:, 0:PC, :], c3, ALU.mult, [made[k][2], t2] + hw)]
                    if PC < 4:
                        c3 = bc(Cs[k % 3].unsqueeze(1), [128, 4 - PC, 512])
                        g.append(tt(dv, h[x][:, PC:4, :], h[x][:, PC:4, :], c3, ALU.mult, [made[k][2], t2] + hw))
                    yw[k] = g
                    cf[k % 3] = g
                    if k + 2 < 32:
                        spread(k + 2)
                    if k > 0 and k != 16:
                        y = ysum(k - 1)
                        hf[1 - x] = [y]
                y = ysum(31)
                hf[1] = [y]
                out_half(1, y)
                t = dv.now
                n = 0
                szf = [[], [], [], []]
                for c in range(4):
                    for half in range(2):
                        bank = n % 4
                        p = xz(4 + c, half, bank)
                        a = act(dB[0][:, bank, :], PS[:, bank, :], ACT.Silu, [p, t] + szf[bank])
                        pf[bank] = [a]
                        s_ = slice(512 * half, 512 * half + 512)
                        e = tt(dv, du[:, c, s_], du[:, c, s_], dB[0][:, bank, :], ALU.mult, [a, t])
                        szf[bank] = [e]
                        n += 1
                tf = [[], []]
                for i in range(8):
                    bank = 4 + i % 2
                    for c in range(4):
                        p = mm(PS[:, bank, 0:256], du[:, c, 128 * i:128 * i + 128], opw[:, c, :], c == 0, c == 3, pf[bank] + [e], inc=(c == 3))
                    if not rev_:
                        t = cp(evac_lane(), MO[:, 8 * b + i, :], PS[:, bank, 0:256], [p])
                        pf[bank] = [t]
                    else:
                        tmp = dA[0][:, i % 2, 0:256]
                        t = cp(ac, tmp, PS[:, bank, 0:256], [p] + tf[i % 2])
                        pf[bank] = [t]
                        p = mm(PS[:, 6 + i % 2, 0:256], anti, tmp, True, True, pf[6 + i % 2] + [t], inc=True)
                        tf[i % 2] = [p]
                        o = MO[:, 8 * b + 7 - i, :]
                        t = tt(dv, o, o, PS[:, 6 + i % 2, 0:256], ALU.add, [p])
                        pf[6 + i % 2] = [t]
                if sq == 3:
                    barrier()
                else:
                    oproj = [pe.now, dv.now, ac.now, gp.now]
                    dv.after(oproj)
            scr.at = scr.lo
            xn = scr.take([NT, D])
            st_at = scr.at
            layer_norm_T(src=MO, keep=xn, mul=lambda c: lg[:, c:c + 1], add=lambda c: lb[:, c:c + 1])
            scr.at = st_at
            hT = [scr.take([8, 512]) for _ in range(2)]
            hTf = [[], []]
            n = 0
            for k in range(4):
                x = k % 2
                hr = []
                for f in range(8):
                    bank = n % 4
                    n += 1
                    for c in range(2):
                        t = mm(PS[:, bank, :], fw1[:, c, 128 * f:128 * f + 128], XNT[:, c, 512 * k:512 * k + 512], c == 0, c == 1, pf[bank], inc=(c == 1))
                    t = act(hT[x][:, f, :], PS[:, bank, :], ACT.Gelu, [t] + hTf[x], bias=fb1[:, f:f + 1])
                    pf[bank] = [t]
                    hr.append(t)
                add_proj(X, lambda c, i, x=x, k=k: hT[x][:, c, 128 * (i - 4 * k):128 * (i - 4 * k) + 128], 8, lambda c: fw2[:, c, :],
                         fb2[0:1, :], tiles=range(4 * k, 4 * k + 4), w=hr, banks=(4, 5, 6, 7))
                hTf[x] = [pe.now]

        def flipped_T():
            order = [7, 6, 5, 4, 3, 2, 1, 0, 15, 14, 13, 12, 11, 10, 9, 8]
            base = scr.lo + 4096 * 3 + 1024 + 4096
            hp = Heap(base, base + 4096 * 2)
            mv, rs = stats(lambda i: X[:, i, :], NT, hp, 1e-5)
            xn = hp.take([NT, D])
            done = [normalise(xn[:, i, :], X[:, i, :], mv, rs, i) for i in range(NT)]
            for k in range(4):
                for c in range(2):
                    bank = (2 * k + c) % 8
                    for j in range(4):
                        i = order[4 * k + j]
                        t = mm(PS[:, bank, 128 * j:128 * j + 128], xn[:, i, 128 * c:128 * c + 128], anti, True, True, pf[bank] + [done[i]], inc=(j == 3))
                    t = cp(evac_lane(), XNT[:, c, 512 * k:512 * k + 512], PS[:, bank, :], [t])
                    pf[bank] = [t]

        def load_7():
            WB[1].clear()
            W[7] = load_w(WB[1], "pk7")

        def phase_7():
            w, wt = W[7]
            wq = w[:, 0:2048].rearrange("p (k n) -> p k n", k=8)
            ws = w[:, 2048:2054].rearrange("p (z c) -> p z c", z=3)
            row = scr.take([260], F32, 0, 1)
            ct = scr.take([4, D])
            ld = Load("d_p7")
            ld.add(row[:, 0:257], ins["pk7r"])
            for b in range(2):
                ld.add(ct[:, 2 * b, :], ins["ctx"][b, 0:128, :])
                ld.add(ct[0:26, 2 * b + 1, :], ins["ctx"][b, 128:154, :])
            XN = scr.take([NT, D])
            layer_norm_T(keep=XN)
            HQ = scr.take([NT, D])
            hqT = scr.take([2, 2048])
            prod = scr.take([2, 2048])
            d3 = scr.take([2, 308])
            rr = scr.take([308])
            nm = scr.take([NT])
            sm = scr.take([NT])
            ri = scr.take([NT])
            Pm = [scr.take([KC]) for _ in range(2)]
            PT = [scr.take([2, 128]) for _ in range(2)]
            ml = scr.take([2])
            M = scr.take([2])
            e_ = scr.take([NT])
            hc = scr.take([2, 2])
            sr = scr.take([2])
            w4 = scr.take([2, 2, D])
            for q in lanes:
                q.after([wt, ld.ready])
            for c in range(2):
                t = ts(dv, d3[:, c, :], ctxT[:, c, :], ws[:, 2, c:c + 1], ws[:, 0, c:c + 1], ALU.mult, ALU.add)
            for c in range(2):
                p = mm(PS[0:1, 0, 0:308], ws[:, 1, c:c + 1], ctxT[:, c, :], c == 0, c == 1, pf[0], inc=(c == 1))
            t = ts(dv, rr[0:1, :], PS[0:1, 0, 0:308], row[0:1, 256:257], None, ALU.add, None, [p, t])
            pf[0] = [t]
            pe.after([t])
            pfree = [[], []]
            ptfree = [[], []]
            for i in range(NT):
                b, x = i // 8, i % 2
                bk = 4 * x
                for c in range(2):
                    mm(PS[:, bk, 0:KC], XNT[:, c, 128 * i:128 * i + 128], d3[:, c, KC * b:KC * b + KC], c == 0, False, pf[bk])
                p = mm(PS[:, bk, 0:KC], ones[0:1, 0:128], rr[0:1, KC * b:KC * b + KC], False, True, (), inc=True)
                t = red(nm[:, i:i + 1], PS[:, bk, 0:KC], ALU.max, [p], neg=True)
                t = act(Pm[x], PS[:, bk, 0:KC], ACT.Exp, [t] + pfree[x], bias=nm[:, i:i + 1], acc=sm[:, i:i + 1])
                pf[bk] = [t]
                r = recip(ri[:, i:i + 1], sm[:, i:i + 1], [t])
                tr(PS[:, bk + 1, 0:128], Pm[x][:, 0:128], ident, [t] + pf[bk + 1])
                p = tr(PS[0:26, bk + 1, 128:256], Pm[x][:, 128:154], ident, (), inc=True)
                pfree[x] = [p]
                e1 = cp(ac, PT[x][:, 0, :], PS[:, bk + 1, 0:128], [p] + ptfree[x])
                e2 = cp(ac, PT[x][0:26, 1, :], PS[0:26, bk + 1, 128:256], [])
                pf[bk + 1] = [e2]
                mm(PS[:, bk + 2, 0:256], PT[x][:, 0, :], ct[:, 2 * b, :], True, False, [e2] + pf[bk + 2])
                p = mm(PS[:, bk + 2, 0:256], PT[x][0:26, 1, :], ct[0:26, 2 * b + 1, :], False, True, (), inc=True)
                ptfree[x] = [p]
                t = ts(dv, HQ[:, i, :], PS[:, bk + 2, 0:256], ri[:, i:i + 1], None, ALU.mult, None, [p, r])
                pf[bk + 2] = [t]
            t = red(ml, nm.rearrange("p (b t) -> p b t", b=2), ALU.min, [dv.now], neg=True)
            t = gp.put(lambda e: e.partition_all_reduce(M, ml, 128, bass.bass_isa.ReduceOp.max), [t])
            t = ts(dv, M, M, -1.0, None, ALU.mult, None, [t])
            for b in range(2):
                t2 = act(e_[:, 8 * b:8 * b + 8], nm[:, 8 * b:8 * b + 8], ACT.Exp, [t], bias=M[:, b:b + 1], scale=-1.0)
            for b in range(2):
                for c in range(3):
                    o = PS[:, 3, 4 * b + c:4 * b + c + 1]
                    for k in range(8):
                        i = 8 * b + k
                        l = XN[:, i, 128 * c:128 * c + 128] if c < 2 else ones
                        p = mm(o, l, e_[:, i:i + 1], k == 0, k == 7, [t2] + pf[3], inc=(k == 7))
            v = PS[:, 3, 0:8].rearrange("p (b c) -> p b c", b=2)
            t = recip(sr, v[:, :, 2], [p])
            t = tt(dv, hc, v[:, :, 0:2], bc(sr.unsqueeze(2), [128, 2, 2]), ALU.mult, [t])
            pf[3] = [t]
            for b in range(2):
                for c in range(2):
                    t2 = stt(w4[:, b, c, :], wq[:, 6 + c, :], hc[:, b, c:c + 1], wq[:, c, :], ALU.mult, ALU.add, [t])
            barrier()
            to_T(lambda i, c: HQ[:, i, 128 * c:128 * c + 128], lambda c, k: hqT[:, c, 512 * k:512 * k + 512], 2, lambda i: [])
            barrier()
            tt(gp, prod[:, 0, :], XNT[:, 0, :], hqT[:, 0, :], ALU.mult)
            tt(dv, prod[:, 1, :], XNT[:, 1, :], hqT[:, 1, :], ALU.mult)
            barrier()

            def lhs(c, i):
                return [XNT, hqT, prod][c // 2][:, c % 2, 128 * i:128 * i + 128]
            for b in range(2):
                add_proj(X, lhs, 6, lambda c, b=b: w4[:, b, c, :] if c < 2 else wq[:, c, :], row[0:1, 0:256],
                         tiles=range(8 * b, 8 * b + 8))

        def top2(l, heap, t):
            oh1, t = first_max(l, heap, [t])
            l2 = heap.take([NT, 8])
            t = stt(l2, oh1, NEG, l, ALU.mult, ALU.add, [t])
            oh2, t = first_max(l2, heap, [t])
            return oh1, oh2, l2, t

        def load_8():
            WB[0].clear()
            W[8] = load_w(WB[0], "pk8")

        def add_H(H):
            for k in range(4):
                v = X[:, 4 * k:4 * k + 4, :]
                tt([dv, gp][k % 2], v, v, H[:, 4 * k:4 * k + 4, :], ALU.add, [q.now for q in (dv, gp)])

        def phase_8():
            w, wt = W[8]
            WA.clear()
            H = WA.take([NT, D])
            wo = w_rows(w[:, 1536:2048])
            l1 = w[:, 2048:2050]
            l2 = w[:, 2050:2052]
            gw = w[:, 2052:2068].rearrange("p (c n) -> p c n", c=2)
            for q in lanes:
                q.after([wt])
            layer_norm_T(keep=H)
            barrier()
            rms_T(H, lambda c: l1[:, c:c + 1], 1e-5)
            barrier()
            att = Attention(S, False, plain_qkv(w_seg(w[:, 0:1536]), None, None, wt))
            att.run()
            out_proj(att, wo, None, H, wt)
            barrier()
            scr.clear()
            ring = [scr.take([3072]) for _ in range(2)]
            lds = [Load("d_e8a"), Load("d_e8b")]
            for k in range(2):
                lds[k].add(ring[k], ins["pk8e"][k])
            rms_T(H, lambda c: l2[:, c:c + 1], 1e-5)
            barrier()
            l, t = logits8(lambda c: gw[:, c, :], None, scr)
            oh1, oh2, lm, t = top2(l, scr, t)
            m1 = scr.take([NT])
            m2 = scr.take([NT])
            ta = red(m1, l, ALU.max, [t])
            tb = red(m2, lm, ALU.max, [t])
            t = tt(dv, m2, m2, m1, ALU.subtract, [ta, tb])
            t = act(m2, m2, ACT.Exp, [t])
            t = ts(dv, m1, m2, 1.0, None, ALU.add, None, [t])
            t = recip(m1, m1, [t])
            t = tt(dv, m2, m2, m1, ALU.mult, [t])
            t = tt(dv, oh1, oh1, bc(m1.unsqueeze(2), [128, NT, 8]), ALU.mult, [t])
            t2 = tt(dv, oh2, oh2, bc(m2.unsqueeze(2), [128, NT, 8]), ALU.mult, [t])
            t = tt(dv, oh1, oh1, oh2, ALU.add, [t2])
            dv.after([t])
            G = oh1
            hT = [scr.take([4, 512]) for _ in range(2)]
            sg = [scr.take([512]) for _ in range(2)]
            swiglu_reset()
            for e in range(8):
                x = e % 2
                rg = ring[x]
                w1 = rg[:, 0:1024].rearrange("p (c n) -> p c n", c=2)
                w3 = rg[:, 1024:2048].rearrange("p (c n) -> p c n", c=2)
                w2 = rg[:, 2048:3072].rearrange("p (f n) -> p f n", f=4)
                pe.after([lds[x].ready])
                swiglu(4, 4, lambda f, c, w1=w1: w1[:, c, 128 * f:128 * f + 128], lambda f, c, w3=w3: w3[:, c, 128 * f:128 * f + 128], hT, sg,
                       lambda f, w2=w2: w2[:, f, :], lambda i, e=e: G[:, i, e:e + 1], H, finish=True)
                if e + 2 < 8:
                    lds[x].add(ring[x], ins["pk8e"][e + 2], [pe.now])
            barrier()
            add_H(H)

        def load_9():
            WB[1].clear()
            W[9] = load_w(WB[1], "pk9")

        def phase_9():
            w, wt = W[9]
            dq, uqT = w[:, 0:16], w[:, 16:32]
            dkv = w[:, 32:64].rearrange("p (c n) -> p c n", c=2)
            ukvT = w[:, 64:128].rearrange("p (c n) -> p c n", c=2)
            kr, qr = w[0:64, 128:144], w[0:64, 144:160]
            woT = w[0:16, 160:176]
            nw = w[:, 176:208].rearrange("p (z d) -> p z d", z=2)
            for q in lanes:
                q.after([wt])
            layer_norm_T()
            sm = scr.take([80])
            BD = scr.take([5, 8, 16])
            RQ = scr.take([NT, 2, 16])
            A2 = [scr.take([2, 8, 16]) for _ in range(2)]
            mark = scr.at
            sq = [scr.take([2, 256]) for _ in range(2)]
            sd = scr.take([NT * 32])
            mm(PS[0:16, 0, 0:16], dq, uqT, True, True)
            for c in range(2):
                mm(PS[0:16, 0, 16:48], dkv[:, c, :], ukvT[:, c, :], c == 0, c == 1)
            p = mm(PS[0:16, 0, 48:64], kr, qr, True, True, (), inc=True)
            t1 = cp(dv, sm[0:16, 0:64], PS[0:16, 0, 0:64], [p])
            t2 = cp(dv, sm[0:16, 64:80], woT)
            p = mm(PS[:, 1, 0:80], rep16, sm[0:16, :], True, True, [t1, t2], inc=True)
            t = tt(dv, BD, bc(PS[:, 1, 0:80].rearrange("p (z d) -> p z d", z=5).unsqueeze(2), [128, 5, 8, 16]),
                   bc(bdm.unsqueeze(1).unsqueeze(3), [128, 5, 8, 16]), ALU.mult, [p])
            pe.after([t])
            for q in (pe,):
                q.after([t])
            flat = BD.rearrange("p z h d -> p (z h d)")
            fr = [[], []]
            pf[0] = []
            for i in range(NT):
                x = i % 2
                for hh in range(2):
                    p = mm(PS[:, 2 + x, 256 * hh:256 * hh + 256], XNT[:, hh, 128 * i:128 * i + 128], flat[:, 0:256], True, True, pf[2 + x], inc=(hh == 1))
                a = act(sq[x], PS[:, 2 + x, :].rearrange("p (s n) -> p s n", s=2), ACT.Square, [p] + fr[x])
                pf[2 + x] = [a]
                t = red(RQ[:, i], sq[x].rearrange("p s (h d) -> p s h d", d=16), ALU.add, [a])
                fr[x] = [t]
            rq = RQ.rearrange("p i s h -> p (i s h)")
            t = ts(dv, rq, rq, 1.0 / 16, 1.1920929e-07, ALU.mult, ALU.add, [dv.now])
            t = act(sd, rq, ACT.Sqrt, [t])
            t = recip(rq, sd, [t])
            barrier()
            scr.at = mark

            def qkv(b, hh, t, rows, hq, hk, ps, w):
                r0 = b * S + 128 * t
                return mm(ps[:, 0:512], XNT[:, hh, r0:r0 + 128], flat[:, 0:512], True, True, w, inc=True)

            def post(b, hh, t, ps, tok, x):
                a = A2[x]
                t1 = tt(dv, a.rearrange("p z h d -> p (z h) d"), ps[:, 0:256].rearrange("p (h d) -> p h d", d=16),
                        bc(RQ[:, 8 * b + t, hh, :].unsqueeze(2), [128, 16, 16]), ALU.mult, [tok])
                t2 = tt(dv, a, a, bc(nw.unsqueeze(2), [128, 2, 8, 16]), ALU.mult, [t1])
                t3 = tt(dv, a[:, 1], a[:, 1], ps[:, 384:512].rearrange("p (h d) -> p h d", d=16), ALU.add, [t2])
                return a, t3, [t3]
            att = Attention(S, True, qkv, post=post)
            att.run()
            barrier()
            to_T(lambda i, c: att.O[:, i, 128 * c:128 * c + 128], lambda c, k: XNT[:, c, 512 * k:512 * k + 512], 2, lambda i: [])
            barrier()
            for i in range(0, NT, 2):
                bk = (i // 2) % 8
                for z in range(2):
                    for c in range(2):
                        p = mm(PS[:, bk, 256 * z + 128 * c:256 * z + 128 * c + 128], XNT[:, c, 128 * (i + z):128 * (i + z) + 128], flat[:, 512:640],
                               True, True, pf[bk], inc=(z == 1 and c == 1))
                v = X[:, i:i + 2, :]
                t = tt(dv, v, PS[:, bk, :].rearrange("p (k c) -> p k c", k=2), v, ALU.add, [p])
                pf[bk] = [t]

        def load_10():
            WB[0].clear()
            W[10] = load_w(WB[0], "pk10")

        def phase_10():
            w, wt = W[10]
            b1 = scr.take([NT, KC])
            bT = scr.take([2, 2048])
            row = scr.take([256], F32, 0, 1)
            ld = Load("d_p10")
            ld.add(row, ins["pk10r"])
            mi = b1.bitcast(I32)
            for b in range(2):
                ld.add(mi[:, 8 * b:8 * b + 8, :], ins["mask32"][b, 0].rearrange("(t p) k -> p t k", p=128))
            layer_norm_T()
            mark = scr.at
            b2 = scr.take([NT, KC])
            an = scr.take([NT])
            for q in lanes:
                q.after([wt, ld.ready])
            t = ts(dv, b1, mi, 0.0, None, ALU.not_equal, None)
            t = red(an, b1, ALU.max, [t])
            t1 = ts(dv, an, an, BIG, None, ALU.mult, None, [t])
            t2 = ts(dv, b2, b1, 2 * BIG, None, ALU.mult, None, [t])
            t2 = tt(dv, b2, b2, bc(an.unsqueeze(2), [128, NT, KC]), ALU.subtract, [t1, t2])
            ts(dv, b1, b1, BIG, -1e9, ALU.mult, ALU.add, [t2])
            for k in range(4):
                for z in range(2):
                    rows = 128 if z == 0 else 26
                    bk = 2 * (k % 4) + z
                    for j in range(4):
                        p = tr(PS[0:rows, bk, 128 * j:128 * j + 128], b2[:, 4 * k + j, 128 * z:128 * z + rows], ident, [t2] + pf[bk], inc=(j == 3))
                    t = cp(evac_lane(), bT[0:rows, z, 512 * k:512 * k + 512], PS[0:rows, bk, :], [p])
                    pf[bk] = [t]
            barrier()
            scr.at = mark
            att = Attention(KC, False, plain_qkv(w_seg(w[:, 0:1536]), None, None, wt), bound=(b1, bT))
            att.run()
            out_proj(att, w_rows(w[:, 1536:2048]), row[0:1, 0:256], X, wt)

        def load_11():
            WB[1].clear()
            W[11] = load_w(WB[1], "pk11")

        def phase_11():
            w, wt = W[11]
            WA.clear()
            H = WA.take([NT, D])
            lw = w[:, 2048:2056].rearrange("p (z c) -> p z c", z=4)
            wr = w[:, 2056:2072].rearrange("p (c n) -> p c n", c=2)
            wo = w_rows(w[:, 1536:2048])
            row = scr.take([1024], F32, 0, 1)
            ld = Load("d_p11")
            ld.add(row, ins["pk11r"])
            for q in lanes:
                q.after([wt, ld.ready])
            layer_norm_T(keep=H)
            barrier()
            layer_norm_T(src=H, mul=lambda c: lw[:, 0, c:c + 1], add=lambda c: lw[:, 1, c:c + 1])
            barrier()
            att = Attention(S, False, plain_qkv(w_seg(w[:, 0:1536]), None, row[:, 0:768].rearrange("p (s n) -> p s n", s=2), wt))
            att.run()
            out_proj(att, wo, row[0:1, 768:1024], H, wt)
            barrier()
            scr.clear()
            ring = [scr.take([4104]) for _ in range(2)]
            b2 = scr.take([2048], F32, 0, 1)
            lds = [Load("d_e11a"), Load("d_e11b")]
            lb = Load("d_b2")
            lb.add(b2, ins["pk11b"])
            for k in range(2):
                lds[k].add(ring[k], ins["pk11e"][k])
            layer_norm_T(src=H, mul=lambda c: lw[:, 2, c:c + 1], add=lambda c: lw[:, 3, c:c + 1])
            barrier()
            pe.after([lb.ready])
            l, t = logits8(lambda c: wr[:, c, :], None, scr)
            p, r, t2 = softmax8(l, scr, [t])
            t2 = tt(dv, p, p, bc(r.unsqueeze(2), [128, NT, 8]), ALU.mult, [t2])
            oh1, t = first_max(p, scr, [t2])
            l2 = scr.take([NT, 8])
            t = stt(l2, oh1, NEG, l, ALU.mult, ALU.add, [t])
            oh2, t = first_max(l2, scr, [t])
            loc = [scr.take([8, NT]) for _ in range(2)]
            tot = [scr.take([8, NT + 1]) for _ in range(2)]
            of = [scr.take([8, NT + 1]) for _ in range(2)]
            fill(dv, tot[0], 0.0)
            fill(dv, tot[1], 0.0)
            zz = fill(dv, of[0], 0.0)
            zz = fill(dv, of[1], 0.0)
            on = scr.take([NT + 1])
            zz = fill(dv, on, 1.0)
            for z, oh in ((0, oh1), (1, oh2)):
                f = oh.rearrange("p i e -> p (i e)")
                p1 = mm(PS[:, 2 * z + 1, 0:128], upper, f, True, True, [t], inc=True)
                p2 = mm(PS[:, 2 * z + 2, 0:128], ones, f, True, True, (), inc=True)
                t1 = cp(dv, tot[z][:, :, 1:NT + 1], PS[:, 2 * z + 2, 0:128].rearrange("p (i e) -> p e i", e=8), [p2, zz])
                if z == 1:
                    t1 = cp(dv, tot[1][:, :, 0], of[0][:, :, NT], [t1, dv.now])
                for e in range(8):
                    t2 = dv.put(lambda q, e=e, z=z: q.tensor_tensor_scan(out=of[z][:, e, :], data0=on, data1=tot[z][:, e, :],
                                                                        initial=0.0, op0=ALU.mult, op1=ALU.add), [t1])
                t2 = tt(dv, loc[z], PS[:, 2 * z + 1, 0:128].rearrange("p (i e) -> p e i", e=8), of[z][:, :, 0:NT], ALU.add, [p1, t2])
                t2 = ts(dv, loc[z], loc[z], -1.0, 512.0, ALU.add, ALU.is_lt, [t2])
                t2 = tt(dv, oh, oh, loc[z].rearrange("p e i -> p i e"), ALU.mult, [t2])
            G = scr.take([NT, 8])
            dn = scr.take([NT])
            t = tt(dv, G, oh1, oh2, ALU.add, [t2])
            t = tt(dv, G, G, p, ALU.mult, [t])
            t = red(dn, G, ALU.add, [t])
            t = ts(dv, dn, dn, 1.1920929e-07, None, ALU.max, None, [t])
            t = recip(dn, dn, [t])
            t = ts(dv, dn, dn, 0.8, None, ALU.mult, None, [t])
            t = tt(dv, G, G, bc(dn.unsqueeze(2), [128, NT, 8]), ALU.mult, [t])
            barrier()
            hT = [scr.take([8, 512]) for _ in range(2)]
            hf = [[], []]
            last = {}
            st = {"pend": None, "n": 0, "o": 0}

            def down(item):
                x, w2, e, k, hr = item
                for i2 in range(2):
                    bk = 4 + st["o"] % 4
                    st["o"] += 1
                    for z in range(2):
                        i = 2 * i2 + z
                        for f in range(8):
                            mm(PS[:, bk, 256 * z:256 * z + 256], hT[x][:, f, 128 * i:128 * i + 128], w2[:, f, :], f == 0, False, pf[bk] + hr)
                        t = mm(PS[:, bk, 256 * z:256 * z + 256], ones[0:1, 0:128], b2[0:1, 256 * e:256 * e + 256], False, True, (), inc=True)
                    for z in range(2):
                        i = 4 * k + 2 * i2 + z
                        t2 = stt(H[:, i, :], PS[:, bk, 256 * z:256 * z + 256], G[:, i, e:e + 1], H[:, i, :], ALU.mult, ALU.add,
                                 [t] + last.get(i, []))
                        last[i] = [t2]
                    pf[bk] = [t2]
                hf[x] = [t]
            for e in range(8):
                y = e % 2
                w1 = ring[y][:, 0:2048].rearrange("p (c n) -> p c n", c=2)
                w2 = ring[y][:, 2048:4096].rearrange("p (f n) -> p f n", f=8)
                bb = ring[y][:, 4096:4104]
                for q in (pe, ac, dv):
                    q.after([lds[y].ready])
                for k in range(4):
                    x = st["n"] % 2
                    st["n"] += 1
                    hr = []
                    for f in range(8):
                        bk = f % 4
                        for c in range(2):
                            t = mm(PS[:, bk, :], w1[:, c, 128 * f:128 * f + 128], XNT[:, c, 512 * k:512 * k + 512], c == 0, c == 1, pf[bk], inc=(c == 1))
                        if f % 2:
                            t = act(hT[x][:, f, :], PS[:, bk, :], ACT.Relu, [t] + hf[x], bias=bb[:, f:f + 1])
                        else:
                            t = ts(dv, hT[x][:, f, :], PS[:, bk, :], bb[:, f:f + 1], 0.0, ALU.add, ALU.max, [t] + hf[x])
                        pf[bk] = [t]
                        hr.append(t)
                    if st["pend"] is not None:
                        down(st["pend"])
                    st["pend"] = (x, w2, e, k, hr)
                down(st["pend"])
                st["pend"] = None
                if e + 2 < 8:
                    lds[y].add(ring[y], ins["pk11e"][e + 2], [pe.now, ac.now, dv.now])
            barrier()
            add_H(H)

        LOADS = {0: load_0, 1: load_1, 2: load_2, 3: load_3, 4: load_4, 5: load_5, 6: load_6, 7: load_7, 8: load_8, 9: load_9,
                 10: load_10, 11: load_11}
        AHEAD = {1: 0, 3: 2, 4: 3, 5: 4, 6: 5, 7: 6, 8: 7, 9: 8, 10: 9, 11: 10}
        loaded = set()

        def load_for(p):
            if p not in loaded:
                loaded.add(p)
                LOADS[p]()

        FN = {0: phase_0, 1: phase_1, 2: phase_2, 3: phase_3, 4: phase_4, 5: phase_5, 6: phase_6, 7: phase_7,
              8: phase_8, 9: phase_9, 10: phase_10, 11: phase_11}
        for p in phases:
            scr.clear()
            load_for(p)
            for nxt, at in AHEAD.items():
                if at == p and nxt in phases:
                    load_for(nxt)
            FN[p]()
            barrier()
        lo = Load("d_out")
        for i in range(4):
            lo.add(out.rearrange("b (t p) c -> p (b t) c", p=128)[:, 4 * i:4 * i + 4, :], X[:, 4 * i:4 * i + 4, :],
                   [q.now for q in lanes])
        sp.after([lo.ready])

        block = ctx.enter_context(nc.Block())

        @block.sync
        def _(e):
            for f in sp.items:
                f(e)

        @block.tensor
        def _(e):
            for f in pe.items:
                f(e)

        @block.scalar
        def _(e):
            for f in ac.items:
                f(e)

        @block.vector
        def _(e):
            for f in dv.items:
                f(e)

        @block.gpsimd
        def _(e):
            for f in gp.items:
                f(e)


def ch(w):
    w = np.asarray(w)
    k, n = w.shape
    return w.reshape(k // 128, 128, n).transpose(1, 0, 2).reshape(128, (k // 128) * n)


def cols(v):
    return np.asarray(v).reshape(-1, 128).T


def pad_rows(w):
    w = np.asarray(w)
    return np.concatenate([w, np.zeros((128 - w.shape[0], w.shape[1]), w.dtype)], 0)


def every(v):
    v = np.asarray(v).reshape(1, -1)
    return np.broadcast_to(v, (128, v.shape[1]))


def seg(wq, wk, wv):
    k = wq.shape[0] // 128
    w = np.stack([np.asarray(a).reshape(k, 128, 2, 128) for a in (wq, wk, wv)], 3)
    return w.transpose(1, 0, 2, 3, 4).reshape(128, -1)


def seg_row(bq, bk, bv):
    return np.stack([np.asarray(a).reshape(2, 128) for a in (bq, bk, bv)], 1).reshape(1, 768)


def cat(*a):
    return np.ascontiguousarray(np.concatenate(a, axis=1))


def constants():
    p = np.arange(128)
    c = np.zeros((128, 840), np.float32)
    c[:, 0:128] = np.eye(128)
    c[:, 128:256] = np.eye(128)[::-1]
    c[0:16, 256:384] = np.tile(np.eye(16), (1, 8))
    c[:, 384:512] = np.where(p[None, :] > p[:, None], NEG, 0.0)
    c[:, 512:640] = np.where(p[:, None] > p[None, :], NEG, 0.0)
    c[:, 640:768] = p[:, None] <= p[None, :]
    c[:, 768:776] = (p[:, None] // 16) == np.arange(8)[None, :]
    c[:, 776:784] = 8.0 - np.arange(8)[None, :]
    c[64, 784] = 1.0
    c[65, 785] = 1.0
    return c


def layout(I):
    o = {}
    o["consts"] = constants()
    o["x"] = np.asarray(I["x"])
    ctx = np.asarray(I["ctx_1024"])
    o["ctx"] = ctx
    o["ctxT"] = ch(ctx.reshape(308, 256).T)
    o["mask8"] = np.ascontiguousarray(I["mask_BxS2_bf1"]).view(np.uint8).reshape(1, 308)
    o["mask32"] = np.asarray(I["mask_Bx1xSxS2_if1"])
    a = {k[8:]: np.asarray(v) for k, v in I.items() if k.startswith("L0_attn_")}
    ukv = np.stack([a["W_UK"].reshape(64, 2, 128), a["W_UV"].reshape(64, 2, 128)], 2).reshape(64, 512)
    o["pk0"] = cat(ch(a["W_DKV"]), pad_rows(ukv), ch(a["W_UQ"]), ch(a["W_O"]))
    a = {k[9:]: np.asarray(v) for k, v in I.items() if k.startswith("L0_xattn_")}

    def headpad(w):
        w = w.reshape(256, 16, 64)
        return ch(np.concatenate([w, np.zeros((256, 16, 2), w.dtype)], 2).reshape(256, 16 * 66))
    o["pk1"] = cat(headpad(a["Wq"]), headpad(a["Wk"]), ch(a["Wv"]), cols(a["gl"]), cols(a["bl"]), cols(a["gm"]), cols(a["bm"]))
    o["pk1o"] = ch(a["Wo"])
    a = {k[7:]: np.asarray(v) for k, v in I.items() if k.startswith("L0_ffn_")}
    o["pk2"] = cat(ch(a["expert_w"].transpose(1, 0, 2).reshape(256, 2048)), ch(a["router_w"]), every(a["router_b"]))
    o["pk2e"] = a["expert_b"].reshape(1, 2048)
    a = {k[8:]: np.asarray(v) for k, v in I.items() if k.startswith("L1_attn_")}
    o["pk3"] = cat(ch(a["Wqkv"].T), ch(a["Wproj"].T))
    o["pk3r"] = np.concatenate([a["bqkv"], a["bproj"]]).reshape(1, 1024)
    a = {k[9:]: np.asarray(v) for k, v in I.items() if k.startswith("L1_xattn_")}
    o["pk4"] = cat(seg(a["Wq"].T, a["Wk"].T, a["Wv"].T), ch(a["Wo"].T))
    o["pk4r"] = cat(seg_row(a["bq"], a["bk"], a["bv"]), a["bo"].reshape(1, 256))
    a = {k[7:]: np.asarray(v) for k, v in I.items() if k.startswith("L1_ffn_")}
    o["pk5"] = cat(ch(a["w_gate"].T), ch(a["w_up"].T), ch(a["w_down"].T))
    a = {k[8:]: np.asarray(v) for k, v in I.items() if k.startswith("L2_attn_")}
    o["pk6"] = cat(ch(a["in_proj_w"]), ch(np.concatenate([a["x_proj_w"][:, 16:48], a["x_proj_w"][:, 0:16]], 1)), ch(a["out_proj_w"]), ch(a["ff_w1"]), pad_rows(np.concatenate([np.zeros((32, 512), np.float32), a["dt_proj_w"]], 0)), ch(a["conv_w"]),
                   cols(a["conv_b"]), cols(a["dt_proj_b"]), ch(a["A_log"]), cols(a["D"]), cols(a["ln_g"]), cols(a["ln_b"]), cols(a["ff_b1"]),
                   every(a["ff_b2"]))
    o["pk6b"] = ch(a["ff_w2"])
    a = {k[9:]: np.asarray(v) for k, v in I.items() if k.startswith("L2_xattn_")}
    o["pk7"] = cat(ch(a["W_qv"]), cols(a["w_sim"]))
    o["pk7r"] = np.concatenate([a["b_qv"], a["b_sim"]]).reshape(1, 257)
    a = {k[7:]: np.asarray(v) for k, v in I.items() if k.startswith("L2_ffn_")}
    o["pk8"] = cat(seg(a["wq"].T, a["wk"].T, a["wv"].T), ch(a["wo"].T), cols(a["ln1_w"]), cols(a["ln2_w"]), ch(a["gate_w"].T))
    o["pk8e"] = np.stack([cat(ch(a["w1"][e].T), ch(a["w3"][e].T), ch(a["w2"][e].T)) for e in range(8)])
    a = {k[8:]: np.asarray(v) for k, v in I.items() if k.startswith("L3_attn_")}
    o["pk9"] = cat(a["W_DQ"], np.ascontiguousarray(a["W_UQ"].T), ch(a["W_DKV"]), ch(a["W_UKV"].T), pad_rows(a["W_KR"]), pad_rows(a["W_QR"]),
                   pad_rows(a["W_O"].T), every(a["q_norm_w"]), every(a["k_norm_w"]))
    a = {k[9:]: np.asarray(v) for k, v in I.items() if k.startswith("L3_xattn_")}
    o["pk10"] = cat(seg(a["Wq"].T, a["Wk"].T, a["Wv"].T), ch(a["Wo"].T))
    o["pk10r"] = a["bo"].reshape(1, 256)
    a = {k[7:]: np.asarray(v) for k, v in I.items() if k.startswith("L3_ffn_")}
    o["pk11"] = cat(seg(a["wq"], a["wk"], a["wv"]), ch(a["wo"]), cols(a["ln1_g"]), cols(a["ln1_b"]), cols(a["ln2_g"]), cols(a["ln2_b"]),
                    ch(a["wr"]))
    o["pk11r"] = cat(seg_row(a["bq"], a["bk"], a["bv"]), a["bo"].reshape(1, 256))
    o["pk11b"] = a["b2"].reshape(1, 2048)
    o["pk11e"] = np.stack([cat(ch(a["w1"][e]), ch(a["w2"][e]), cols(a["b1"][e])) for e in range(8)])
    return {k: np.ascontiguousarray(v) for k, v in o.items()}


def kernel(**inputs):
    import concourse.bacc as _bacc
    from concourse import mybir as _mybir
    from concourse.bass_utils import run_bass_kernel_spmd as _run

    nc = _bacc.Bacc("TRN2", target_bir_lowering=False, num_devices=1)
    arrays = layout(inputs)
    ins = {}
    for name, a in arrays.items():
        ins[name] = nc.dram_tensor(f"in_{name}", a.shape, _mybir.dt.from_np(a.dtype), kind="ExternalInput").ap()
    out = nc.dram_tensor("out_0", (2, 1024, 256), _mybir.dt.float32, kind="ExternalOutput").ap()
    build(nc, ins, out, range(12))
    r = _run(nc, [{f"in_{k}": v for k, v in arrays.items()}], core_ids=[0])
    return r.results[0]["out_0"]
```

```python
from contextlib import ExitStack

import numpy as np
import concourse.bass as bass
from concourse import mybir

F32 = mybir.dt.float32
BF16 = mybir.dt.bfloat16
I32 = mybir.dt.int32
U8 = mybir.dt.uint8
ALU = mybir.AluOpType
ACT = mybir.ActivationFunctionType
AX = mybir.AxisListType
NEG = -1e30
BIG = 1e30
S = 1024
NT = 16
KC = 154
D = 256
QH = 96
QM = 98


class Lane:

    def __init__(self, sem):
        self.sem = sem
        self.items = []
        self.count = 0
        self.seen = {}

    def after(self, toks):
        for sem, value in toks:
            if self.seen.get(sem.name, 0) < value:
                self.seen[sem.name] = value
                self.items.append(waiter(sem, value))

    def put(self, fn, toks=(), inc=True):
        self.after(toks)
        if inc:
            self.count += 1
            self.items.append(counted(fn, self.sem))
        else:
            self.items.append(fn)
        return (self.sem, self.count)

    @property
    def now(self):
        return (self.sem, self.count)


def waiter(sem, value):
    return lambda e: e.wait_ge(sem, value)


def counted(fn, sem):
    return lambda e: fn(e).then_inc(sem, 1)


def bc(ap, shape):
    return ap.broadcast_to(list(shape))


def build(nc, ins, out, phases):
    ctx = ExitStack()
    with ctx:
        def sem(name):
            return ctx.enter_context(nc.semaphore(name))

        pe = Lane(sem("s_pe"))
        ac = Lane(sem("s_act"))
        dv = Lane(sem("s_dve"))
        gp = Lane(sem("s_pool"))
        sp = Lane(sem("s_sp"))
        lanes = [pe, ac, dv, gp]

        TOT = 53200
        AR = ctx.enter_context(nc.sbuf_tensor("AR", [128, TOT], F32))
        PS = ctx.enter_context(nc.psum_tensor("PS", [128, 8, 512], F32))

        def view(off, dims, dt=F32, p0=0, p1=128):
            n = int(np.prod(dims))
            words = n if dt in (F32, I32) else n // 2
            ap = AR[p0:p1, off:off + words]
            if dt != F32:
                ap = ap.bitcast(dt)
            if len(dims) == 1:
                return ap
            names = "abcd"[:len(dims)]
            return ap.rearrange(f"p ({' '.join(names)}) -> p {' '.join(names)}",
                                **{k: v for k, v in zip(names, dims)})

        class Heap:
            def __init__(self, lo, hi):
                self.lo, self.hi, self.at = lo, hi, lo

            def take(self, dims, dt=F32, p0=0, p1=128):
                n = int(np.prod(dims))
                words = n if dt in (F32, I32) else (n + 1) // 2
                off = self.at
                self.at += words
                assert self.at <= self.hi, (self.at, self.hi)
                return view(off, dims, dt, p0, p1)

            def clear(self):
                self.at = self.lo

        fixed = Heap(0, 10000)
        WA = Heap(10000, 16300)
        WB = [Heap(16300, 18400), Heap(18400, 20500)]
        scr = Heap(20500, TOT)

        X = fixed.take([NT, D])
        XNT = fixed.take([2, 2048])
        consts = fixed.take([840])
        ident = consts[:, 0:128]
        anti = consts[:, 128:256]
        rep16 = consts[0:16, 256:384]
        maskS_f = consts[:, 384:512]
        maskT_f = consts[:, 512:640]
        upper = consts[:, 640:768]
        bdm = consts[:, 768:776]
        rev = consts[:, 776:784]
        el8 = consts[:, 786:794]
        iota24 = consts[:, 794:818]
        pcol = consts[:, 818:819]
        ctxT = fixed.take([2, 308])
        ones = fixed.take([128])
        identb = fixed.take([128], BF16)
        maskS = fixed.take([128], BF16)
        maskT = fixed.take([128], BF16)

        def mm(o, l, r, start, stop, w=(), inc=False, tile=None):
            if tile is None:
                return pe.put(lambda e: e.matmul(o, l, r, start=start, stop=stop), w, inc)
            return pe.put(lambda e: e.matmul(o, l, r, start=start, stop=stop, tile_position=tile), w, inc)

        def tr(o, i, idn, w=(), inc=False):
            return pe.put(lambda e: e.transpose(o, i, idn), w, inc)

        def act(o, i, f, w=(), bias=None, scale=None, acc=None):
            kw = {}
            if bias is not None:
                kw["bias"] = bias
            if scale is not None:
                kw["scale"] = scale
            if acc is not None:
                kw["accum_out"] = acc
            return ac.put(lambda e: e.activation(o, i, f, **kw), w)

        def tt(q, o, a, b, op, w=()):
            return q.put(lambda e: e.tensor_tensor(o, a, b, op), w)

        def ts(q, o, a, s1, s2, op0, op1, w=()):
            if op1 is None:
                return q.put(lambda e: e.tensor_scalar(o, a, s1, None, op0), w)
            return q.put(lambda e: e.tensor_scalar(o, a, s1, s2, op0, op1), w)

        def stt(o, a, s, b, op0, op1, w=()):
            return dv.put(lambda e: e.scalar_tensor_tensor(out=o, in0=a, scalar=s, in1=b, op0=op0, op1=op1), w)

        def red(o, a, op, w=(), neg=False):
            if neg:
                return dv.put(lambda e: e.tensor_reduce(o, a, AX.X, op, negate=True), w)
            return dv.put(lambda e: e.tensor_reduce(o, a, AX.X, op), w)

        def cp(q, o, i, w=()):
            if q is ac:
                return act(o, i, ACT.Copy, w)
            return q.put(lambda e: e.tensor_copy(o, i), w)

        def fill(q, o, v, w=()):
            return q.put(lambda e: e.memset(o, v), w)

        def recip(o, i, w=()):
            return dv.put(lambda e: e.reciprocal(o, i), w)

        def dma(o, i, s, w=()):
            sp.after(w)
            sp.items.append(lambda e: e.dma_start(o, i).then_inc(s, 16))

        def barrier():
            toks = [q.now for q in lanes]
            for q in lanes + [sp]:
                q.after(toks)
            for b in range(8):
                pf[b] = []

        pf = {b: [] for b in range(8)}
        turn = [0]

        def evac_lane():
            turn[0] += 1
            return ac if turn[0] % 2 else dv

        class Load:

            def __init__(self, name):
                self.sem = sem(name)
                self.n = 0

            def add(self, o, i, w=()):
                dma(o, i, self.sem, w)
                self.n += 16

            @property
            def ready(self):
                return (self.sem, self.n)

        l0 = Load("d_const")
        l0.add(consts[:, 0:840], ins["consts"])
        lx = Load("d_x")
        for i in range(4):
            lx.add(X[:, 4 * i:4 * i + 4, :],
                   ins["x"].rearrange("b (t p) c -> p (b t) c", p=128)[:, 4 * i:4 * i + 4, :])
        lc = Load("d_ctx")
        lc.add(ctxT, ins["ctxT"].rearrange("p (c n) -> p c n", c=2))
        fill(dv, ones, 1.0)
        cp(dv, identb, ident, [l0.ready])
        cp(dv, maskS, maskS_f)
        cp(dv, maskT, maskT_f)
        dv.after([lx.ready, lc.ready])
        ac.after([lx.ready, lc.ready])
        pe.after([l0.ready, lc.ready])
        gp.after([l0.ready, lc.ready, lx.ready])
        barrier()

        def load_w(heap, name, parts=128, width=None, dt=F32):
            heap_ap = heap.take([ins[name].shape[1]], dt, 0, parts)
            l = Load(f"d_{name}")
            n = ins[name].shape[1]
            half = (n + 1) // 2
            if n > 1024:
                l.add(heap_ap[:, 0:half], ins[name][:, 0:half], [])
                l.add(heap_ap[:, half:n], ins[name][:, half:n], [])
            else:
                l.add(heap_ap, ins[name], [])
            return heap_ap, l.ready

        def stats(src, n, heap, eps, rows=128, w=()):
            st = heap.take([n, 6])
            mv = heap.take([n, 2])
            ve = heap.take([n])
            sd = heap.take([n])
            rs = heap.take([n])
            dv.after(w)
            for i in range(n):
                dv.put(lambda e, i=i: e.bn_stats(st[0:rows, i, :], src(i)))
            t = dv.now
            for i in range(n):
                dv.put(lambda e, i=i: e.bn_aggr(mv[0:rows, i, :], st[0:rows, i, :]), [t])
            t = ts(dv, ve[0:rows], mv[0:rows, :, 1], eps, None, ALU.add, None, [dv.now])
            t = act(sd[0:rows], ve[0:rows], ACT.Sqrt, [t])
            t = recip(rs[0:rows], sd[0:rows], [t])
            dv.after([t])
            return mv, rs

        def normalise(dst, src, mv, rs, i, rows=128, w=()):
            return ts(dv, dst, src, mv[0:rows, i, 0:1], rs[0:rows, i:i + 1], ALU.subtract, ALU.mult, w)

        def to_T(src, dst, chunks, ready, idn=None, mul=None, add=None, banks=range(8), groups=4, order=None):
            idn = ident if idn is None else idn
            toks = []
            nb = len(banks)
            n = 0
            for k in range(groups):
                for c in range(chunks):
                    b = banks[n % nb]
                    n += 1
                    for j in range(4):
                        i = 4 * k + j
                        t = tr(PS[:, b, 128 * j:128 * j + 128], src(i if order is None else order[i], c), idn,
                               pf[b] + ready(i if order is None else order[i]), inc=(j == 3))
                    q = evac_lane()
                    if mul is None:
                        t = cp(q, dst(c, k), PS[:, b, :], [t])
                    else:
                        a = 0.0 if add is None else add(c)
                        t = ts(dv, dst(c, k), PS[:, b, :], mul(c), a, ALU.mult, ALU.add, [t])
                    pf[b] = [t]
                    toks.append(t)
            return toks

        def layer_norm_T(keep=None, mul=None, add=None, idn=None, order=None, src=None, eps=1e-5, twice=False):
            mark = scr.at
            src = X if src is None else src
            mv, rs = stats(lambda i: src[:, i, :], NT, scr, eps)
            xn = keep if keep is not None else scr.take([NT, D])
            done = []
            for i in range(NT):
                done.append(normalise(xn[:, i, :], src[:, i, :], mv, rs, i))
            if twice:
                mv, rs = stats(lambda i: xn[:, i, :], NT, scr, eps, w=[dv.now])
                done = []
                for i in range(NT):
                    done.append(normalise(xn[:, i, :], xn[:, i, :], mv, rs, i))
            toks = to_T(lambda i, c: xn[:, i, 128 * c:128 * c + 128],
                        lambda c, k: XNT[:, c, 512 * k:512 * k + 512], 2, lambda i: [done[i]],
                        idn=idn, mul=mul, add=add, order=order)
            scr.at = mark
            for q in lanes + [sp]:
                q.after(toks + [dv.now])
            return toks

        def rms_T(src, wcol, eps, keep=None):
            mark = scr.at
            sq = scr.take([2, D])
            ms = scr.take([NT])
            sd = scr.take([NT])
            rs = scr.take([NT])
            xn = keep if keep is not None else scr.take([NT, D])
            last = [(), ()]
            for i in range(NT):
                act(sq[:, i % 2, :], src[:, i, :], ACT.Square, [ac.now], acc=ms[:, i:i + 1])
            t = ts(dv, sd, ms, 1.0 / D, eps, ALU.mult, ALU.add, [ac.now])
            t = act(sd, sd, ACT.Sqrt, [t])
            t = recip(rs, sd, [t])
            done = []
            for i in range(NT):
                done.append(ts(dv, xn[:, i, :], src[:, i, :], rs[:, i:i + 1], None, ALU.mult, None, [t]))
            toks = to_T(lambda i, c: xn[:, i, 128 * c:128 * c + 128],
                        lambda c, k: XNT[:, c, 512 * k:512 * k + 512], 2, lambda i: [done[i]], mul=wcol)
            scr.at = mark
            for q in lanes + [sp]:
                q.after(toks + [dv.now])

        def add_proj(dst, lhs, nchunks, rhs, bias=None, tiles=range(NT), w=(), banks=range(8)):
            pe.after(w)
            n = 0
            toks = []
            for g in range(0, len(tiles), 2):
                b = banks[n % len(banks)]
                n += 1
                for k in range(2):
                    i = tiles[g + k]
                    o = PS[:, b, 256 * k:256 * k + 256]
                    for c in range(nchunks):
                        last = (c == nchunks - 1) and bias is None
                        t = mm(o, lhs(c, i), rhs(c), c == 0, last, pf[b], inc=(last and k == 1))
                    if bias is not None:
                        t = mm(o, ones[0:1, 0:128], bias, False, True, (), inc=(k == 1))
                i = tiles[g]
                v = dst[:, i:i + 2, :]
                t = tt(dv, v, PS[:, b, :].rearrange("p (k c) -> p k c", k=2), v, ALU.add, [t])
                pf[b] = [t]
                toks.append(t)
            return toks

        class Attention:

            def __init__(self, KV, causal, qkv, post=None, bound=None):
                self.KV, self.causal, self.qkv, self.post, self.bound = KV, causal, qkv, post, bound
                self.qS = [scr.take([8, S], BF16) for _ in range(2)]
                kn = S if KV == S else 160
                self.kS = [scr.take([8, kn], BF16) for _ in range(2)]
                self.nk = (KV + 127) // 128
                self.vE = [scr.take([self.nk, 152]) for _ in range(2)]
                self.vh = [v[:, :, 0:136].rearrange("p t (h e) -> p t h e", e=17) for v in self.vE]
                self.P = [scr.take([2, 512]) for _ in range(2)]
                self.O = scr.take([NT, D])
                self.ST = [scr.take([2, 8, 112], BF16) for _ in range(3)]
                self.R = [scr.take([2, 8, 16]) for _ in range(3)]
                self.A = [scr.take([2, 8, 16]) for _ in range(3)]
                self.Oc = scr.take([512])
                self.Mst = scr.take([4, 4, 32], BF16)
                self.m2 = scr.take([4, 4, 2])
                self.nm = scr.take([4, 4])
                self.ri = scr.take([4, 4, 1])
                for v in self.vE:
                    fill(gp, v, 0.0)
                for v in self.ST:
                    fill(gp, v, 0.0)
                fill(gp, self.Mst, 0.0)
                g = gp.now
                for v in self.vh:
                    fill(gp, v[:, :, :, 16:17], 1.0, [g])
                for v in self.ST:
                    fill(gp, v[:, 1, :, QH:QM], 1.0, [g])
                self.ready0 = gp.now
                for q in (ac, dv, pe):
                    q.after([self.ready0])
                self.st_free = [[], [], []]
                self.r_free = [[], [], []]
                self.banks = [0, 1, 2, 3, 4, 5, 7]
                self.n_bank = 0
                self.seg_free = [[], []]
                self.seg_ready = [[], []]
                self.p_free = [[], []]
                self.n_prep = 0

            def prep(self, s):
                b, hh, par = s // 2, s % 2, s % 2
                self.seg_ready[par] = []
                if self.KV == S:
                    work = [(t, 128, True, True) for t in range(8)]
                else:
                    work = [(t, 128 if t == 0 else 26, False, True) for t in range(2)]
                    work += [(t, 128, True, False) for t in range(8)]
                splits, turns = [], []
                for t, rows, hq, hk in work:
                    st = {}
                    splits.append(lambda t=t, rows=rows, hq=hq, hk=hk, st=st: self.split(b, hh, par, t, rows, hq, hk, st))
                    turns.append([lambda t=t, rows=rows, st=st, z=z: self.turn(par, t, rows, z, st)
                                  for z, on in ((0, hq), (1, hk)) if on])
                pieces = splits[0:2]
                for k in range(len(work)):
                    pieces += splits[k + 2:k + 3] + turns[k]
                return pieces

            def bank(self):
                self.n_bank += 1
                return self.banks[self.n_bank % len(self.banks)]

            def split(self, b, hh, par, t, rows, hq, hk, st):
                bank = self.bank()
                x = self.n_prep % 3
                self.n_prep += 1
                st["x"] = x
                ps = PS[0:rows, bank, :]
                tok = self.qkv(b, hh, t, rows, hq, hk, ps, pf[bank])
                lo, hi = (0 if hq else 1), (2 if hk else 1)
                ST, R, a = self.ST[x], self.R[x], self.A[x]
                rd = []
                w = [tok] + self.st_free[x] + self.r_free[x]
                if hk:
                    rd.append(act(self.vh[par][0:rows, t, :, 0:16], ps[:, 256:384].rearrange("p (h d) -> p h d", h=8),
                                  ACT.Copy, [tok] + self.seg_free[par]))
                    self.seg_ready[par].append(rd[-1])
                if self.post is not None:
                    dv.after(rd)
                    ta, more = self.post(b, hh, t, ps, w, a)
                    rd += more
                else:
                    ta = act(a[0:rows, lo:hi], ps[:, 128 * lo:128 * hi].rearrange("p (z h d) -> p z h d", h=8, d=16), ACT.Copy, w)
                    rd.append(ta)
                pf[bank] = rd

                def slots(z, js):
                    v = ST[0:rows, z, :, 0:96].rearrange("p h (j d) -> p h j d", d=16)
                    if len(js) == 1:
                        return v[:, :, js[0], :]
                    step = js[1] - js[0]
                    return v[:, :, js[0]:js[-1] + 1:step, :]

                def dup(v, n):
                    return bc(v[0:rows].unsqueeze(2), [rows, 8, n, 16])
                done = []
                w = [ta] + self.st_free[x]
                if hq:
                    done.append(act(slots(0, [0, 1, 2]), dup(a[:, 0], 3), ACT.Copy, w))
                if hk:
                    done.append(act(slots(1, [0, 3]), dup(a[:, 1], 2), ACT.Copy, w))
                    done.append(act(slots(1, [5]), a[0:rows, 1], ACT.Copy, w))
                first = ST[0:rows, lo:hi, :, 0:16]
                t1 = tt(dv, R[0:rows, lo:hi], a[0:rows, lo:hi], first, ALU.subtract, done + self.r_free[x])
                if hq:
                    t2 = cp(dv, slots(0, [3, 4]), dup(R[:, 0], 2), [t1])
                if hk:
                    t2 = cp(dv, slots(1, [1, 4]), dup(R[:, 1], 2), [t1])
                done.append(t2)
                if hq:
                    done.append(tt(gp, slots(0, [5]), R[0:rows, 0], slots(0, [3]), ALU.subtract, [t2]))
                if hk:
                    done.append(tt(gp, slots(1, [2]), R[0:rows, 1], slots(1, [1]), ALU.subtract, [t2]))
                self.r_free[x] = [gp.now]
                st["done"] = done
                self.st_free[x] = []

            def turn(self, par, t, rows, z, st):
                bank = self.bank()
                x = st["x"]
                pb = PS[:, bank, :].bitcast(BF16).rearrange("p (h n) -> p h n", h=8)
                for h in range(8):
                    tok = tr(pb[0:112, h, 0:rows], self.ST[x][0:rows, z, h, :], identb[0:rows, 0:rows],
                             st["done"] + pf[bank], inc=(h == 7))
                self.st_free[x] = self.st_free[x] + [tok]
                dst = (self.qS if z == 0 else self.kS)[par]
                e = cp(evac_lane(), dst[0:QM, :, 128 * t:128 * t + rows], pb[0:QM, :, 0:rows],
                       [tok] + self.seg_free[par])
                pf[bank] = [e]
                self.seg_ready[par].append(e)

            def max_pieces(self, s, g, qb, u):
                par = s % 2
                qS, kS = self.qS[par], self.kS[par]
                b = s // 2
                pieces = []
                KV = self.KV
                st = {}
                if KV == S:
                    nh = (qb + 1) if self.causal else 2
                    for qt in range(4):
                        for j in range(4):
                            def piece(qt=qt, j=j):
                                h = 4 * g + j
                                q0 = 512 * qb + 128 * qt
                                for half in range(nh):
                                    bank = self.bank()
                                    n = 512
                                    diag = False
                                    if self.causal and half == nh - 1:
                                        n = 128 * (qt + 1)
                                        diag = True
                                    o = PS[:, bank, 0:n]
                                    tok = mm(o, qS[0:QH, h, q0:q0 + 128], kS[0:QH, h, 512 * half:512 * half + n],
                                             True, not diag, pf[bank] + self.seg_ready[par], inc=not diag)
                                    if diag:
                                        tok = mm(PS[:, bank, n - 128:n], identb, maskS, False, True, (), inc=True)
                                    e = red(self.m2[:, qt, j, half:half + 1], o, ALU.max, [tok] + st.get("w", []))
                                    pf[bank] = [e]
                            pieces.append(piece)
                else:
                    nh = 1
                    for qt in range(4):
                        for jj in range(2):
                            def piece(qt=qt, jj=jj):
                                bank = self.bank()
                                q0 = 512 * qb + 128 * qt
                                for k in range(2):
                                    h = 4 * g + 2 * jj + k
                                    tok = mm(PS[:, bank, KC * k:KC * k + KC], qS[0:QH, h, q0:q0 + 128], kS[0:QH, h, 0:KC],
                                             True, True, pf[bank] + self.seg_ready[par], inc=(k == 1))
                                v = PS[:, bank, 0:2 * KC].rearrange("p (k n) -> p k n", k=2)
                                if self.bound is not None:
                                    bd = self.bound[0][:, 8 * b + 4 * qb + qt, :]
                                    tok = tt(dv, v, v, bc(bd.unsqueeze(1), [128, 2, KC]), ALU.min, [tok])
                                e = red(self.m2[:, qt, 2 * jj:2 * jj + 2, 0], v, ALU.max, [tok])
                                pf[bank] = [e]
                            pieces.append(piece)

                def fin1():
                    t = dv.now
                    if nh == 2:
                        t = red(self.nm, self.m2, ALU.max, [t], neg=True)
                    else:
                        t = ts(dv, self.nm, self.m2[:, :, :, 0], -1.0, None, ALU.mult, None, [t])
                    t = cp(dv, self.Mst[:, :, :, 0], self.nm, [t] + st_m["free"])
                    t = tt(dv, self.Mst[:, :, :, 1], self.nm, self.Mst[:, :, :, 0], ALU.subtract, [t])
                    st["m"] = t

                def fin2():
                    bank = self.bank()
                    pb = PS[:, bank, :].bitcast(BF16)
                    for qt in range(4):
                        tok = tr(pb[:, 128 * qt:128 * qt + 128], self.Mst[:, qt].rearrange("p j r -> p (j r)"), identb,
                                 [st["m"]] + pf[bank], inc=(qt == 3))
                    st_m["free"] = [tok]
                    es = []
                    for j in range(4):
                        es.append(cp(dv, qS[QH:QM, 4 * g + j, 512 * qb:512 * qb + 512], pb[32 * j:32 * j + 2, 0:512],
                                     [tok] + self.seg_ready[par]))
                    pf[bank] = es
                    self.m_ready[u] = es
                st_m = self.st_m
                pieces.append(fin1)
                pieces.append(fin2)
                return pieces

            def exp_unit(self, s, g, qb, u, side):
                par, b, hh = s % 2, s // 2, s % 2
                qS, kS, vE = self.qS[par], self.kS[par], self.vE[par]
                nk = 4 * (qb + 1) if self.causal else self.nk
                q0 = 512 * qb
                steps = [(t, jj) for t in range(nk) for jj in range(2)]
                pend = None
                mw = self.m_ready[u]

                def pv(item):
                    t, jj, rows, lo, par2, tok = item
                    for k in range(2):
                        j = 2 * jj + k
                        x = mm(PS[32 * j:32 * j + 32, 6, lo:512], vE[0:rows, t, 17 * (4 * g + j):17 * (4 * g + j) + 32],
                               self.P[par2][0:rows, k, lo:512], t == 0, t == nk - 1, [tok] + (pf[6] if t == 0 else []),
                               inc=(k == 1), tile=(0, 32 * j))
                    self.p_free[par2] = [x]
                    return x
                last = None
                for n, (t, jj) in enumerate(steps):
                    rows = min(128, self.KV - 128 * t)
                    lo = 0
                    diag = self.causal and t >= 4 * qb
                    if diag:
                        lo = 128 * (t - 4 * qb)
                    pr = n % 2
                    for k in range(2):
                        h = 4 * g + 2 * jj + k
                        bank = 2 * pr + k
                        tok = mm(PS[0:rows, bank, lo:512], kS[0:QM, h, 128 * t:128 * t + rows], qS[0:QM, h, q0 + lo:q0 + 512],
                                 True, not diag, pf[bank] + mw, inc=(k == 1 and not diag))
                        if diag:
                            tok = mm(PS[0:rows, bank, lo:lo + 128], identb, maskT, False, True, (), inc=(k == 1))
                    v = PS[0:rows, 2 * pr:2 * pr + 2, lo:512]
                    if self.bound is not None:
                        bt = self.bound[1][0:rows, t, b * S + q0:b * S + q0 + 512]
                        tok = tt(dv, v, v, bc(bt.unsqueeze(1), [rows, 2, 512]), ALU.min, [tok])
                    e = act(self.P[pr][0:rows, :, lo:512], v, ACT.Exp, [tok] + self.p_free[pr], scale=0.25)
                    pf[2 * pr] = [e]
                    pf[2 * pr + 1] = [e]
                    side()
                    if pend is not None:
                        pv(pend)
                    pend = (t, jj, rows, lo, pr, e)
                    side()
                last = pv(pend)
                w = cp(ac, self.Oc, PS[:, 6, :], [last] + self.oc_free)
                pf[6] = [w]

                def finish():
                    bank = self.bank()
                    for qt in range(4):
                        tok = tr(PS[:, bank, 128 * qt:128 * qt + 128], self.Oc[:, 128 * qt:128 * qt + 128], ident,
                                 [w] + pf[bank], inc=(qt == 3))
                    self.oc_free = [tok]
                    pv4 = PS[:, bank, :].rearrange("p (t j d) -> p t j d", t=4, j=4)
                    r = recip(self.ri, pv4[:, :, :, 16:17], [tok, dv.now])
                    i0 = 8 * b + 4 * qb
                    c0 = 128 * hh + 64 * g
                    o = self.O[:, i0:i0 + 4, c0:c0 + 64].rearrange("p t (j d) -> p t j d", j=4)
                    e = tt(dv, o, pv4[:, :, :, 0:16], bc(self.ri, [128, 4, 4, 16]), ALU.mult, [r])
                    pf[bank] = [e]
                return finish

            def run(self):
                self.m_ready = {}
                self.st_m = {"free": []}
                self.oc_free = []
                units = [(s, g, qb) for s in range(4) for g in range(2) for qb in range(2)]
                for p in self.prep(0) + self.max_pieces(*units[0], 0):
                    p()
                self.banks = [4, 5, 7]
                pre = []
                fin = None
                users = {0: [], 1: []}
                for u, (s, g, qb) in enumerate(units):
                    if u % 4 == 0 and s + 1 < 4:
                        self.seg_free[(s + 1) % 2] = users[(s + 1) % 2]
                        pre = self.prep(s + 1)
                    nxt = []
                    if u + 1 < len(units):
                        k = -(-len(pre) // max(1, 3 - u % 4))
                        own, pre = pre[:k], pre[k:]
                        mx = self.max_pieces(*units[u + 1], u + 1)
                        body, (fin1, fin2) = mx[:-2], mx[-2:]
                        tail = own[max(0, k - 3):]
                        own = own[:max(0, k - 3)]
                        tot = len(body) + len(own)
                        bi = oi = 0
                        for z in range(tot):
                            if oi < len(own) and (oi * tot <= z * len(own) or bi == len(body)):
                                nxt.append(own[oi])
                                oi += 1
                            else:
                                nxt.append(body[bi])
                                bi += 1
                        nxt += [fin1] + (tail or [None, None]) + [fin2]
                    if fin is not None:
                        nxt = nxt[:1] + [fin] + nxt[1:]
                    nk = 4 * (qb + 1) if self.causal else self.nk
                    calls = 4 * nk - 1
                    at = [0, 0]

                    def side(nxt=nxt, at=at, calls=calls):
                        at[1] += 1
                        while at[0] < min(len(nxt), -(-at[1] * len(nxt) // calls)):
                            if nxt[at[0]] is not None:
                                nxt[at[0]]()
                            at[0] += 1
                    fin = self.exp_unit(s, g, qb, u, side)
                    users[s % 2] = [pe.now]
                fin()

        def out_proj(att, wo, bias, dst, wtok):
            barrier()
            toks = to_T(lambda i, c: att.O[:, i, 128 * c:128 * c + 128],
                        lambda c, k: XNT[:, c, 512 * k:512 * k + 512], 2, lambda i: [])
            pe.after(toks + [wtok])
            add_proj(dst, lambda c, i: XNT[:, c, 128 * i:128 * i + 128], 2, wo, bias)

        def plain_qkv(wq, wkv, bias, wtok, kvT=None):
            def f(b, hh, t, rows, hq, hk, ps, w):
                pe.after([wtok])
                r0 = b * S + 128 * t
                tok = None
                if hq and hk:
                    for c in range(2):
                        tok = mm(ps[:, 0:384], XNT[:, c, r0:r0 + 128], wq(c, hh, 0, 384), c == 0, c == 1 and bias is None, w,
                                 inc=(c == 1 and bias is None))
                    if bias is not None:
                        tok = mm(ps[:, 0:384], ones[0:1, 0:128], bias[:, hh, 0:384], False, True, (), inc=True)
                    return tok
                if hq:
                    src, lo, hi = (lambda c: XNT[:, c, r0:r0 + 128]), 0, 128
                else:
                    k0 = KC * b + 128 * t
                    src, lo, hi = (lambda c: ctxT[:, c, k0:k0 + rows]), 128, 384
                for c in range(2):
                    tok = mm(ps[:, lo:hi], src(c), wq(c, hh, lo, hi), c == 0, c == 1 and bias is None, w,
                             inc=(c == 1 and bias is None))
                if bias is not None:
                    tok = mm(ps[:, lo:hi], ones[0:1, 0:rows], bias[:, hh, lo:hi], False, True, (), inc=True)
                return tok
            return f

        def w_seg(wap):
            v = wap.rearrange("p (c s n) -> p c s n", c=2, s=2)
            return lambda c, hh, lo, hi: v[:, c, hh, lo:hi]

        def w_rows(wap, n=256):
            v = wap.rearrange("p (c n) -> p c n", n=n)
            return lambda c: v[:, c, :]

        W = {}

        def load_0():
            WB[0].clear()
            W[0] = load_w(WB[0], "pk0")

        def phase_0():
            w, wt = W[0]
            dkv = w[:, 0:128].rearrange("p (c n) -> p c n", c=2)
            ukv = w[0:64, 128:640].rearrange("p (s n) -> p s n", s=2)
            uq = w[:, 640:1152].rearrange("p (c n) -> p c n", c=2)
            wo = w_rows(w[:, 1152:1664])
            layer_norm_T()
            ckv = scr.take([2048])
            pe.after([wt])
            for k in range(4):
                for c in range(2):
                    t = mm(PS[0:64, k, :], dkv[:, c, :], XNT[:, c, 512 * k:512 * k + 512], c == 0, c == 1, pf[k], inc=(c == 1))
                t = cp(evac_lane(), ckv[0:64, 512 * k:512 * k + 512], PS[0:64, k, :], [t])
                pf[k] = [t]
            barrier()

            def qkv(b, hh, t, rows, hq, hk, ps, w):
                r0 = b * S + 128 * t
                for c in range(2):
                    mm(ps[:, 0:128], XNT[:, c, r0:r0 + 128], uq[:, c, 128 * hh:128 * hh + 128], c == 0, c == 1, w)
                return mm(ps[:, 128:384], ckv[0:64, r0:r0 + 128], ukv[:, hh, :], True, True, (), inc=True)
            att = Attention(S, True, qkv)
            att.run()
            out_proj(att, wo, None, X, wt)

        def load_1():
            WA.clear()
            WB[1].clear()
            W[1] = [load_w(WA, "pk1"), load_w(WB[1], "pk1o"), (scr_mask(), None)]

        def scr_mask():
            return None

        def phase_1():
            (wa, ta), (wb, tb), _ = W[1]
            wq = wa[:, 0:2048].rearrange("p (c n) -> p c n", c=2)
            wk = wa[:, 2048:4096].rearrange("p (c n) -> p c n", c=2)
            wv = wa[:, 4096:6144].rearrange("p (c n) -> p c n", c=2)
            g = wa[:, 6144:6152].rearrange("p (z c) -> p z c", z=4)
            wo = wb[:, 0:2048].rearrange("p (k n) -> p k n", k=8)
            for q in lanes:
                q.after([ta, tb])
            KV = S + KC
            KR = 97
            qT = [scr.take([S]) for _ in range(4)]
            kT = [scr.take([KV]) for _ in range(4)]
            qB = [scr.take([S], BF16) for _ in range(4)]
            kB = [scr.take([KV], BF16) for _ in range(4)]
            for y in range(4):
                for v, w_ in ((qT, 0.0), (qB, 0.0), (kT, 1.0), (kB, 1.0)):
                    fill(gp, v[y][64:128], w_, [gp.now])
            for y in range(4):
                for v, w_ in ((qT, 1.0), (qB, 1.0), (kT, 0.0), (kB, 0.0)):
                    fill(gp, v[y][96:97], w_, [gp.now])
            layer_norm_T(mul=lambda c: g[:, 0, c:c + 1], add=lambda c: g[:, 1, c:c + 1], twice=True)
            fT = scr.take([2, 308])
            mk = scr.take([308])
            lm = Load("d_mask")
            mk8 = scr.take([308 // 4 + 1])
            ct = scr.take([4, D])
            m8 = mk8.bitcast(U8)[0:1, 0:308]
            lm.add(m8, ins["mask8"])
            for b in range(2):
                lm.add(ct[:, 2 * b, :], ins["ctx"][b, 0:128, :])
                lm.add(ct[0:26, 2 * b + 1, :], ins["ctx"][b, 128:154, :])
            dv.after([lm.ready])
            ts(dv, mk[0:1, 0:308], m8, -1.0, -NEG, ALU.add, ALU.mult)
            for b in range(2):
                for z in range(2):
                    rows = 128 if z == 0 else 26
                    i = 2 * b + z
                    mv, rs = stats(lambda _, i=i, rows=rows: ct[0:rows, i, :], 1, scr, 1e-5, rows=rows)
                    t = normalise(ct[0:rows, i, :], ct[0:rows, i, :], mv, rs, 0, rows)
                    for c in range(2):
                        p = tr(PS[:, i, 128 * c:128 * c + rows], ct[0:rows, i, 128 * c:128 * c + 128], ident[0:rows, 0:rows],
                               [t] + pf[i], inc=(c == 1))
                    for c in range(2):
                        t = ts(dv, fT[:, c, KC * b + 128 * z:KC * b + 128 * z + rows], PS[:, i, 128 * c:128 * c + rows],
                               g[:, 2, c:c + 1], g[:, 3, c:c + 1], ALU.mult, ALU.add, [p])
                    pf[i] = [t]
            vE = scr.take([10, 8, 65])
            P = [scr.take([2, 512]) for _ in range(2)]
            O = scr.take([8, 512])
            OT = scr.take([2, 4, 128])
            Mst = scr.take([8, 65])
            m2 = scr.take([8, 3])
            nm = scr.take([8])
            Oc = scr.take([512])
            ri = scr.take([4, 1])
            fill(gp, vE[:, :, :, 64:65], 1.0, [gp.now])
            fill(gp, Mst, 0.0, [gp.now])
            barrier()

            def kvsrc(b, t, c):
                if t < 8:
                    return XNT[:, c, b * S + 128 * t:b * S + 128 * t + 128]
                lo = KC * b + 128 * (t - 8)
                return fT[:, c, lo:lo + (128 if t == 8 else 26)]
            kvrows = [128] * 9 + [26]
            st = {"p": [[], []], "oc": [], "free": [[], [], [], []], "mst": [], "o_free": [], "slot": 0}

            def proj(b, j, hds):
                pcs = []
                ys = [2 * (j % 2), 2 * (j % 2) + 1]
                for hd in hds:
                    hd["q"] = [[], []]
                    hd["k"] = [[], [], []]
                for z, k in ((0, 0), (1, 0), (1, 1), (1, 2), (0, 1)):
                    def piece(z=z, k=k):
                        n = 512 if k < 2 else KC
                        for c in range(2):
                            src = XNT[:, c, b * S + 512 * k:b * S + 512 * k + 512] if k < 2 else fT[:, c, KC * b:KC * b + KC]
                            tok = mm(PS[:, 7, 0:n], (wk if z else wq)[:, c, 128 * j:128 * j + 128], src, c == 0, c == 1, pf[7], inc=(c == 1))
                        F, H_ = (kT, kB) if z else (qT, qB)
                        for i in range(2):
                            y = ys[i]
                            s_ = slice(512 * k, 512 * k + n)
                            v = PS[64 * i:64 * i + 64, 7, 0:n]
                            ta = cp(dv, F[y][0:64, s_], v, [tok] + st["free"][y])
                            tb = cp(ac, H_[y][0:64, s_], F[y][0:64, s_], [ta] + st["free"][y])
                            w_ = [ta, tb]
                            if z == 1 and k == 2 and j < 2:
                                w_.append(cp(dv, F[y][96:97, s_], mk[0:1, KC * b:KC * b + KC], st["free"][y]))
                                w_.append(cp(dv, H_[y][96:97, s_], mk[0:1, KC * b:KC * b + KC], st["free"][y]))
                            hds[i]["k" if z else "q"][k] = w_
                        pf[7] = [ta]
                    pcs.append(piece)
                return pcs

            def maxes(y, hd):
                pcs = []
                for qt in range(8):
                    for k in range(3):
                        def mx(qt=qt, k=k):
                            n = 512 if k < 2 else KC
                            bank = 4 + st["slot"] % 2
                            st["slot"] += 1
                            tok = mm(PS[:, bank, 0:n], qB[y][0:KR, 128 * qt:128 * qt + 128], kB[y][0:KR, 512 * k:512 * k + n],
                                     True, True, pf[bank] + hd["q"][qt // 4] + hd["k"][k], inc=True)
                            e = red(m2[:, qt, k:k + 1], PS[:, bank, 0:n], ALU.max, [tok] + st["mst"])
                            pf[bank] = [e]
                        pcs.append(mx)

                def fin1():
                    t = red(nm, m2, ALU.max, [dv.now], neg=True)
                    hd["m"] = cp(dv, Mst[:, :, 64], nm, [t] + st["mst"])
                pcs.append(fin1)
                es = []
                for k in range(2):
                    def fin2(k=k):
                        for j in range(4):
                            tok = tr(PS[0:65, 7, 128 * j:128 * j + 128], Mst[:, 4 * k + j, :], ident, [hd["m"]] + pf[7], inc=(j == 3))
                        e = cp(dv, qT[y][64:65, 512 * k:512 * k + 512], PS[64:65, 7, :], [tok] + st["free"][y])
                        pf[7] = [e]
                        st["mst"] = [tok]
                        es.append(e)
                        hd["rdy"] = es + [x for v in hd["q"] + hd["k"] for x in v]
                    pcs.append(fin2)
                return pcs

            def v_half(b, hh, w):
                for t in range(10):
                    bank = 4 + t % 3
                    rows = kvrows[t]
                    for c in range(2):
                        tok = mm(PS[0:rows, bank, :], kvsrc(b, t, c), wv[:, c, 512 * hh:512 * hh + 512], c == 0, c == 1,
                                 pf[bank], inc=(c == 1))
                    e = cp(evac_lane(), vE[0:rows, t, :, 0:64], PS[0:rows, bank, :].rearrange("p (h d) -> p h d", h=8), [tok] + w)
                    pf[bank] = [e]
                    v_rdy.append(e)
            v_rdy = []

            def exp_head(h, y, hd, side):
                hl = h % 8
                steps = [(qb, pr) for qb in range(2) for pr in range(5)]
                pend = []
                late = []

                def pv():
                    qb, pr, px, toks = pend.pop(0)
                    for k in range(2):
                        t = 2 * pr + k
                        rows = kvrows[t]
                        tok = mm(PS[0:65, 6, :], vE[0:rows, t, hl, :], P[px][0:rows, k, :], t == 0, t == 9,
                                 toks + v_rdy + (pf[6] if t == 0 else []), inc=(k == 1))
                    st["p"][px] = [tok]
                    if pr == 4:
                        w = cp(ac, Oc[0:65, :], PS[0:65, 6, :], [tok] + st["oc"])
                        pf[6] = [w]

                        def finish():
                            for j in range(4):
                                tok = tr(PS[:, 7, 128 * j:128 * j + 65], Oc[0:65, 128 * j:128 * j + 128], ident[0:65, 0:65],
                                         [w] + pf[7], inc=(j == 3))
                            st["oc"] = [tok]
                            v4 = PS[:, 7, :].rearrange("p (t d) -> p t d", t=4)
                            r = recip(ri, v4[:, :, 64:65], [tok, dv.now])
                            e = tt(dv, O[:, 4 * qb:4 * qb + 4, 64 * hl:64 * hl + 64], v4[:, :, 0:64], bc(ri, [128, 4, 64]),
                                   ALU.mult, [r] + st["o_free"])
                            pf[7] = [e]
                        late.append(finish)
                for n, (qb, pr) in enumerate(steps):
                    px = n % 2
                    for k in range(2):
                        t = 2 * pr + k
                        rows = kvrows[t]
                        tok = mm(PS[0:rows, 2 * px + k, :], kT[y][0:KR, 128 * t:128 * t + rows],
                                 qT[y][0:KR, 512 * qb:512 * qb + 512], True, True, pf[2 * px + k] + hd["rdy"], inc=True)
                    if pr < 4:
                        e = [act(P[px], PS[:, 2 * px:2 * px + 2, :], ACT.Exp, [tok] + st["p"][px], scale=0.125)]
                    else:
                        e = [act(P[px][:, 0, :], PS[:, 2 * px, :], ACT.Exp, [tok] + st["p"][px], scale=0.125),
                             act(P[px][0:26, 1, :], PS[0:26, 2 * px + 1, :], ACT.Exp, [], scale=0.125)]
                    pf[2 * px] = e
                    pf[2 * px + 1] = e
                    side(2 * n, 2 * len(steps))
                    if pend:
                        pv()
                    pend.append((qb, pr, px, e))
                    side(2 * n + 1, 2 * len(steps))
                    if late and pr == 1:
                        late.pop()()
                st["free"][y] = [pe.now]
                pv()
                return late.pop()

            order = [(b, h) for b in range(2) for h in range(16)]
            hds = [{} for _ in order]
            for p in proj(0, 0, hds[0:2]) + maxes(0, hds[0]):
                p()
            fin = None
            for n, (b, h) in enumerate(order):
                hh = h // 8
                if h % 8 == 0:
                    v_rdy.clear()
                    v_half(b, hh, [pe.now])
                nxt = []
                if h % 2 == 0 and n + 2 < len(order):
                    nxt += proj(order[n + 2][0], order[n + 2][1] // 2, hds[n + 2:n + 4])
                if n + 1 < len(order):
                    mx = maxes((n + 1) % 4, hds[n + 1])
                    body = []
                    for z, p in enumerate(mx[:-3]):
                        if z % 5 == 2 and nxt:
                            body.append(nxt.pop(0))
                        body.append(p)
                    nxt = body + nxt + mx[-3:]
                if fin is not None:
                    nxt = nxt[:2] + [fin] + nxt[2:]
                at = [0]

                def side(i, of, nxt=nxt, at=at):
                    while at[0] < min(len(nxt), -(-(i + 1) * len(nxt) // (of - 1))):
                        nxt[at[0]]()
                        at[0] += 1
                fin = exp_head(h, n % 4, hds[n], side)
                if h % 8 == 7:
                    fin()
                    fin = None
                    ot_free = [[], []]
                    odone = dv.now
                    ev = {}
                    for i in range(9):
                        if i < 8:
                            x = i % 2
                            for c in range(4):
                                tok = tr(PS[:, 4 + x, 128 * c:128 * c + 128], O[:, i, 128 * c:128 * c + 128], ident,
                                         pf[4 + x] + [odone], inc=(c == 3))
                            e = cp(ac, OT[:, x], PS[:, 4 + x, :].rearrange("p (c n) -> p c n", c=4), [tok] + ot_free[x])
                            pf[4 + x] = [e]
                            ev[i] = e
                        if i > 0:
                            k = i - 1
                            bk = 6 + k % 2
                            for c in range(4):
                                tok = mm(PS[:, bk, 0:256], OT[:, k % 2, c, :], wo[:, 4 * hh + c, :], c == 0, c == 3, pf[bk] + [ev[k]], inc=(c == 3))
                            ot_free[k % 2] = [tok]
                            xv = X[:, 8 * b + k, :]
                            e = tt(dv, xv, PS[:, bk, 0:256], xv, ALU.add, [tok, dv.now])
                            pf[bk] = [e]
                    st["o_free"] = [pe.now]

        def softmax8(l, heap, w=()):
            mx = heap.take([NT])
            p = heap.take([NT, 8])
            s = heap.take([NT])
            r = heap.take([NT])
            t = red(mx, l, ALU.max, w)
            t = tt(dv, p, l, bc(mx.unsqueeze(2), [128, NT, 8]), ALU.subtract, [t])
            t = act(p, p, ACT.Exp, [t])
            t = red(s, p, ALU.add, [t])
            t = recip(r, s, [t])
            return p, r, t

        def first_max(l, heap, w=()):
            mx = heap.take([NT])
            sc = heap.take([NT, 8])
            oh = heap.take([NT, 8])
            t = red(mx, l, ALU.max, w)
            t = tt(dv, sc, l, bc(mx.unsqueeze(2), [128, NT, 8]), ALU.is_equal, [t])
            t = tt(dv, sc, sc, bc(rev.unsqueeze(1), [128, NT, 8]), ALU.mult, [t])
            t = red(mx, sc, ALU.max, [t])
            t = tt(dv, oh, sc, bc(mx.unsqueeze(2), [128, NT, 8]), ALU.is_equal, [t])
            return oh, t

        def logits8(wr, bias, heap):
            for i in range(NT):
                o = PS[:, 0, 8 * i:8 * i + 8]
                for c in range(2):
                    t = mm(o, XNT[:, c, 128 * i:128 * i + 128], wr(c), c == 0, c == 1 and bias is None, pf[0], inc=(i == NT - 1 and c == 1))
                if bias is not None:
                    t = mm(o, ones[0:1, 0:128], bias, False, True, (), inc=(i == NT - 1))
            l = heap.take([NT, 8])
            t = cp(dv, l, PS[:, 0, 0:128].rearrange("p (i e) -> p i e", e=8), [t])
            pf[0] = [t]
            return l, t

        def load_2():
            WA.clear()
            W[2] = load_w(WA, "pk2")

        def phase_2():
            w, wt = W[2]
            ew = w[:, 0:4096].rearrange("p (c e n) -> p c e n", c=2, e=8)
            rw = w[:, 4096:4112].rearrange("p (c n) -> p c n", c=2)
            rb = w[0:1, 4112:4120]
            lb = Load("d_eb")
            eb = scr.take([2048], F32, 0, 1)
            lb.add(eb, ins["pk2e"])
            layer_norm_T()
            for q in lanes:
                q.after([wt, lb.ready])
            l, t = logits8(lambda c: rw[:, c, :], rb, scr)
            p, r, t = softmax8(l, scr, [t])
            t2 = tt(dv, p, p, bc(r.unsqueeze(2), [128, NT, 8]), ALU.mult, [t])
            oh, t = first_max(p, scr, [t2])
            G = scr.take([NT, 8])
            t = tt(dv, G, oh, p, ALU.mult, [t])
            last = t
            n = 0
            for i in range(NT):
                for e2 in range(4):
                    b = n % 8
                    n += 1
                    for c in range(2):
                        mm(PS[:, b, :], XNT[:, c, 128 * i:128 * i + 128], ew[:, c, 2 * e2:2 * e2 + 2, :].rearrange("p e n -> p (e n)"),
                           c == 0, False, pf[b])
                    t = mm(PS[:, b, :], ones[0:1, 0:128], eb[0:1, 512 * e2:512 * e2 + 512], False, True, (), inc=True)
                    for k in range(2):
                        t2 = stt(X[:, i, :], PS[:, b, 256 * k:256 * k + 256], G[:, i, 2 * e2 + k:2 * e2 + k + 1], X[:, i, :],
                                 ALU.mult, ALU.add, [t, last])
                        last = t2
                    pf[b] = [t2]

        def load_3():
            WB[0].clear()
            W[3] = load_w(WB[0], "pk3")

        def phase_3():
            w, wt = W[3]
            wqkv = w[:, 0:1536].rearrange("p (c n) -> p c n", c=2)
            wo = w_rows(w[:, 1536:2048])
            rows = scr.take([1024], F32, 0, 1)
            lr = Load("d_pk3r")
            lr.add(rows, ins["pk3r"])
            layer_norm_T()
            qk = [scr.take([2, 768]) for _ in range(2)]
            pr = [scr.take([2, 2, D]) for _ in range(2)]
            sc = [scr.take([2, 2, 16]) for _ in range(2)]
            mx = [scr.take([2, 16]) for _ in range(2)]
            O = scr.take([NT, D])
            ex = [scr.take([2, 2, 16]) for _ in range(2)]
            for q in lanes:
                q.after([wt, lr.ready])
            fr = [[], []]
            for i in range(8):
                x = i % 2
                ts_ = []
                for b in range(2):
                    for z in range(2):
                        bank = 4 * x + 2 * b + z
                        lo, hi = (0, 512) if z == 0 else (512, 768)
                        for c in range(2):
                            mm(PS[:, bank, 0:hi - lo], XNT[:, c, b * S + 128 * i:b * S + 128 * i + 128], wqkv[:, c, lo:hi], c == 0, False, pf[bank])
                        t = mm(PS[:, bank, 0:hi - lo], ones[0:1, 0:128], rows[0:1, lo:hi], False, True, (), inc=True)
                        t = cp(ac, qk[x][:, b, lo:hi], PS[:, bank, 0:hi - lo], [t] + fr[x])
                        pf[bank] = [t]
                Q, K, V = qk[x][:, :, 0:256], qk[x][:, :, 256:512], qk[x][:, :, 512:768]
                d0 = [t, dv.now]
                for r in range(2):
                    t = tt(dv, pr[x][:, r], bc(Q[:, r:r + 1, :], [128, 2, 256]), K, ALU.mult, d0)
                t = red(sc[x], pr[x].rearrange("p r c (h d) -> p (r c) h d", d=16), ALU.add, [t])
                t = tt(dv, mx[x], sc[x][:, :, 0, :], sc[x][:, :, 1, :], ALU.max, [t])
                t = tt(dv, sc[x], sc[x], bc(mx[x].unsqueeze(2), [128, 2, 2, 16]), ALU.subtract, [t])
                t = act(ex[x], sc[x], ACT.Exp, [t], scale=0.25)
                t = tt(dv, mx[x], ex[x][:, :, 0, :], ex[x][:, :, 1, :], ALU.add, [t])
                t = recip(mx[x], mx[x], [t])
                t = tt(dv, ex[x], ex[x], bc(mx[x].unsqueeze(2), [128, 2, 2, 16]), ALU.mult, [t])
                for r in range(2):
                    for c in range(2):
                        tt(dv, pr[x][:, r, c].rearrange("p (h d) -> p h d", d=16),
                           V[:, c].rearrange("p (h d) -> p h d", d=16), bc(ex[x][:, r, c].unsqueeze(2), [128, 16, 16]), ALU.mult, [t])
                t2 = dv.now
                for r in range(2):
                    t = tt(dv, O[:, 8 * r + i, :], pr[x][:, r, 0], pr[x][:, r, 1], ALU.add, [t2])
                fr[x] = [t]
            barrier()
            to_T(lambda i, c: O[:, i, 128 * c:128 * c + 128], lambda c, k: XNT[:, c, 512 * k:512 * k + 512], 2, lambda i: [])
            barrier()
            add_proj(X, lambda c, i: XNT[:, c, 128 * i:128 * i + 128], 2, wo, rows[0:1, 768:1024])

        def load_4():
            WB[1].clear()
            W[4] = load_w(WB[1], "pk4")

        def phase_4():
            w, wt = W[4]
            wq = w_seg(w[:, 0:1536])
            wo = w_rows(w[:, 1536:2048])
            rows = scr.take([1024], F32, 0, 1)
            lr = Load("d_pk4r")
            lr.add(rows, ins["pk4r"])
            layer_norm_T()
            pe.after([lr.ready])
            att = Attention(KC, False, plain_qkv(wq, None, rows[:, 0:768].rearrange("p (s n) -> p s n", s=2), wt))
            att.run()
            out_proj(att, wo, rows[0:1, 768:1024], X, wt)

        def load_5():
            WA.clear()
            W[5] = load_w(WA, "pk5", dt=I32)

        def phase_5():
            wi, wt = W[5]
            wf = wi.bitcast(F32)
            for q in lanes:
                q.after([wt])
            for k in range(3):
                ts([dv, gp, dv][k], wf[:, 1536 * k:1536 * k + 1536], wi[:, 1536 * k:1536 * k + 1536], 1.0 / 127.0, None, ALU.mult, None)
            wg = wf[:, 0:1536].rearrange("p (c n) -> p c n", c=2)
            wu = wf[:, 1536:3072].rearrange("p (c n) -> p c n", c=2)
            wd = wf[:, 3072:4608].rearrange("p (f n) -> p f n", f=6)
            layer_norm_T()
            for q in lanes:
                q.after([gp.now])
            hT = [scr.take([6, 512]) for _ in range(2)]
            sg = [scr.take([512]) for _ in range(2)]
            swiglu(4, 6, lambda f, c: wg[:, c, 128 * f:128 * f + 128], lambda f, c: wu[:, c, 128 * f:128 * f + 128], hT, sg,
                   lambda f: wd[:, f, :], None, X)

        swi = {"n": 0, "sgf": [[], []], "hf": [[], []], "pend": None, "last": {}}

        def swiglu_reset():
            swi.update({"n": 0, "sgf": [[], []], "hf": [[], []], "pend": None, "last": {}})

        def swiglu_down(item):
            hT, x, nf, wd, gate, dst, k, hr = item
            for i2 in range(2):
                b = 4 + (2 * k + i2) % 4
                for z in range(2):
                    i = 2 * i2 + z
                    for f in range(nf):
                        t = mm(PS[:, b, 256 * z:256 * z + 256], hT[x][:, f, 128 * i:128 * i + 128], wd(f), f == 0, f == nf - 1,
                               pf[b] + hr, inc=(f == nf - 1))
                i = 4 * k + 2 * i2
                if gate is None:
                    v = dst[:, i:i + 2, :]
                    e = tt(dv, v, PS[:, b, :].rearrange("p (k c) -> p k c", k=2), v, ALU.add, [t])
                else:
                    for z in range(2):
                        e = stt(dst[:, i + z, :], PS[:, b, 256 * z:256 * z + 256], gate(i + z), dst[:, i + z, :], ALU.mult, ALU.add,
                                [t] + swi["last"].get(i + z, []))
                        swi["last"][i + z] = [e]
                pf[b] = [e]
            swi["hf"][x] = [t]

        def swiglu(nblk, nf, wg, wu, hT, sg, wd, gate, dst, finish=True):
            for k in range(nblk):
                x = swi["n"] % 2
                swi["n"] += 1
                hr = []
                for f in range(nf):
                    y = f % 2
                    for z, w in ((0, wg), (1, wu)):
                        for c in range(2):
                            t = mm(PS[:, 2 * y + z, :], w(f, c), XNT[:, c, 512 * k:512 * k + 512], c == 0, c == 1, pf[2 * y + z], inc=(c == 1))
                        if z == 0:
                            a = act(sg[y], PS[:, 2 * y, :], ACT.Silu, [t] + swi["sgf"][y])
                            pf[2 * y] = [a]
                    e = tt(dv, hT[x][:, f, :], PS[:, 2 * y + 1, :], sg[y], ALU.mult, [t, a] + swi["hf"][x])
                    pf[2 * y + 1] = [e]
                    swi["sgf"][y] = [e]
                    hr.append(e)
                if swi["pend"] is not None:
                    swiglu_down(swi["pend"])
                swi["pend"] = (hT, x, nf, wd, gate, dst, k, hr)
            if finish:
                swiglu_down(swi["pend"])
                swi["pend"] = None

        def load_6():
            WB[0].clear()
            W[6] = [load_w(WB[0], "pk6b")]

        def phase_6():
            WA.clear()
            wa, ta = load_w(WA, "pk6")
            wb, tb = W[6][0]
            at = [0]

            def part(n):
                v = wa[:, at[0]:at[0] + n]
                at[0] += n
                return v
            inp = part(2048).rearrange("p (c n) -> p c n", c=2)
            xpw = part(192).rearrange("p (c n) -> p c n", c=4)
            opw = part(1024).rearrange("p (c n) -> p c n", c=4)
            fw1 = part(2048).rearrange("p (c n) -> p c n", c=2)
            dtw = part(512)
            cw = part(16).rearrange("p (c n) -> p c n", c=4)
            cb = part(4)
            dtb = part(4)
            alog = part(64).rearrange("p (c n) -> p c n", c=4)
            Dc = part(4)
            lg = part(2)
            lb = part(2)
            fb1 = part(8)
            fb2 = part(256)
            fw2 = wb.rearrange("p (c n) -> p c n", c=8)
            layer_norm_T()
            for q in lanes:
                q.after([ta, tb])
            u = scr.take([4, S])
            de = scr.take([4, S])
            du = scr.take([4, S])
            dbl = scr.take([S])
            MO = scr.take([NT, D])
            dA = [scr.take([4, 512]) for _ in range(2)]
            dB = [scr.take([4, 512]) for _ in range(2)]
            Cs = [scr.take([512]) for _ in range(3)]
            bcs = scr.take([S], BF16)
            eye3 = scr.take([32], BF16)
            PC = 4
            h = [scr.take([4, 512]) for _ in range(2)]
            xp = [h[k].rearrange("p a b -> p (a b)")[:, 0:1027] for k in range(2)]
            hl = scr.take([16, 4])
            An = scr.take([4, 16])
            rbc = dB[0][:, 0, :]
            mid = dB[0][:, 1, 0:256].bitcast(BF16)
            for k in range(3):
                cp(dv, eye3[32 * k:32 * k + 32, :], ident[0:32, 0:32])
            t = act(An, alog, ACT.Exp)
            ts(dv, An, An, -1.0, None, ALU.mult, None, [t])
            barrier()
            for sq in range(4):
                if sq == 2:
                    barrier()
                    flipped_T()
                    barrier()
                b = sq % 2
                rev_ = sq >= 2

                def xz(chunk, half, bank):
                    for c in range(2):
                        t = mm(PS[:, bank, :], inp[:, c, 128 * chunk:128 * chunk + 128],
                               XNT[:, c, b * S + 512 * half:b * S + 512 * half + 512], c == 0, c == 1, pf[bank], inc=(c == 1))
                    return t
                z0 = [fill(dv, v[:, 0:3], 0.0) for v in xp]
                xpf = [[], []]
                silu = []
                for c in range(4):
                    x = c % 2
                    for half in range(2):
                        bank = 2 * x + half
                        t = xz(c, half, bank)
                        t = act(xp[x][:, 3 + 512 * half:515 + 512 * half], PS[:, bank, :], ACT.Copy, [t] + xpf[x])
                        pf[bank] = [t]
                    t = ts(dv, u[:, c, :], xp[x][:, 0:S], cw[:, c, 0:1], cb[:, c:c + 1], ALU.mult, ALU.add, [t] + z0)
                    for i in range(1, 4):
                        t = stt(u[:, c, :], xp[x][:, i:i + S], cw[:, c, i:i + 1], u[:, c, :], ALU.mult, ALU.add, [t])
                    xpf[x] = [t]
                    silu.append(t)
                for c in range(4):
                    t = act(u[:, c, :], u[:, c, :], ACT.Silu, [silu[c]])
                for half in range(2):
                    for c in range(4):
                        p = mm(PS[0:48, 4 + half, :], xpw[:, c, :], u[:, c, 512 * half:512 * half + 512], c == 0, c == 3, pf[4 + half] + [t], inc=(c == 3))
                    s_ = slice(512 * half, 512 * half + 512)
                    e = cp(ac, dbl[32:48, s_], PS[32:48, 4 + half, :], [p])
                    src = PS[0:32, 4 + half, :]
                    t1 = cp(dv, bcs[0:32, s_], src, [p, e])
                    t1 = tt(dv, rbc[0:32, 0:512], src, bcs[0:32, s_], ALU.subtract, [t1])
                    pf[4 + half] = [e, t1]
                    t2 = cp(dv, bcs[32:64, s_], rbc[0:32, 0:512], [t1])
                    t2 = cp(dv, mid[0:32, 0:512], rbc[0:32, 0:512], [t1])
                    t2 = tt(dv, bcs[64:96, s_], rbc[0:32, 0:512], mid[0:32, 0:512], ALU.subtract, [t2])
                    pe.after([t2])
                    dv.after([t2])
                n = 0
                for c in range(4):
                    for half in range(2):
                        bank = n % 4
                        n += 1
                        p = mm(PS[:, bank, :], dtw[32:48, 128 * c:128 * c + 128], dbl[32:48, 512 * half:512 * half + 512], True, True, pf[bank] + [e], inc=True)
                        s_ = slice(512 * half, 512 * half + 512)
                        a = act(de[:, c, s_], PS[:, bank, :], ACT.Abs, [p], bias=dtb[:, c:c + 1])
                        m = ts(dv, du[:, c, s_], PS[:, bank, :], dtb[:, c:c + 1], 0.0, ALU.add, ALU.max, [p, a])
                        pf[bank] = [a, m]
                t = act(de, de, ACT.Exp, [ac.now], scale=-1.0)
                t = act(de, de, ACT.Ln, [t], bias=ones[:, 0:1])
                t = tt(dv, de, de, du, ALU.add, [t, dv.now])
                t = tt(dv, du, de, u, ALU.mult, [t])
                dv.after([t])
                ac.after([t])
                seq = [(half, n) for half in range(2) for n in range(16)]
                dAf, dBf, hf, cf, Bf = [[], []], [[], []], [[], []], [[], [], []], [[], []]
                made = {}

                def spread(k):
                    half, n = seq[k]
                    x = k % 2
                    s_ = slice(512 * half, 512 * half + 512)
                    pb = mm(PS[:, 4 + x, :], bc(eye3[0:96, n:n + 1], [96, 128]), bcs[0:96, s_], True, True, pf[4 + x], inc=True)
                    pc = mm(PS[:, 6 + x, :], bc(eye3[0:96, 16 + n:17 + n], [96, 128]), bcs[0:96, s_], True, True, pf[6 + x], inc=True)
                    for c in range(4):
                        a = act(dA[x][:, c, :], de[:, c, s_], ACT.Exp, dAf[x], scale=An[:, c, n:n + 1])
                    c_ = act(Cs[k % 3], PS[:, 6 + x, :], ACT.Copy, [pc] + cf[k % 3])
                    pf[6 + x] = [c_]
                    made[k] = (pb, a, c_)

                def bu(k):
                    half, n = seq[k]
                    x = k % 2
                    s_ = slice(512 * half, 512 * half + 512)
                    t = tt(dv, dB[x], du[:, :, s_], bc(PS[:, 4 + x, :].unsqueeze(1), [128, 4, 512]), ALU.mult, [made[k][0]] + dBf[x])
                    pf[4 + x] = [t]
                    Bf[x] = [t]
                yw = {}

                def ysum(k):
                    half, n = seq[k]
                    for c in range(4):
                        y = mm(PS[:, c, :], ident, h[k % 2][:, c, :], n == 0, n == 15, yw[k] + (pf[c] if n == 0 else []), inc=(c == 3))
                    return y

                def out_half(half, y):
                    s_ = slice(512 * half, 512 * half + 512)
                    for c in range(4):
                        t = stt(du[:, c, s_], u[:, c, s_], Dc[:, c:c + 1], PS[:, c, :], ALU.mult, ALU.add, [y, dv.now])
                        pf[c] = [t]
                spread(0)
                spread(1)
                bu(0)
                for k, (half, n) in enumerate(seq):
                    x = k % 2
                    if k == 16:
                        y = ysum(15)
                        hf[1] = [y]
                        out_half(0, y)
                        bu(16)
                    sc = []
                    for c in range(4):
                        ini = 0.0 if half == 0 else hl[:, n, c:c + 1]
                        t2 = dv.put(lambda e, c=c, x=x, ini=ini: e.tensor_tensor_scan(
                            out=h[x][:, c, :], data0=dA[x][:, c, :], data1=dB[x][:, c, :], initial=ini, op0=ALU.mult, op1=ALU.add),
                            [made[k][1]] + Bf[x] + hf[x])
                        sc.append(t2)
                    dAf[x] = [t2]
                    dBf[x] = [t2]
                    if k + 1 < 32 and k != 15:
                        bu(k + 1)
                    hw = []
                    if half == 0:
                        hw = [cp(gp, hl[:, n, :], h[x][:, :, 511], [t2])]
                    c3 = bc(Cs[k % 3].unsqueeze(1), [128, PC, 512])
                    g = [tt(gp, h[x][:, 0:PC, :], h[x][:, 0:PC, :], c3, ALU.mult, [made[k][2], t2] + hw)]
                    if PC < 4:
                        c3 = bc(Cs[k % 3].unsqueeze(1), [128, 4 - PC, 512])
                        g.append(tt(dv, h[x][:, PC:4, :], h[x][:, PC:4, :], c3, ALU.mult, [made[k][2], t2] + hw))
                    yw[k] = g
                    cf[k % 3] = g
                    if k + 2 < 32:
                        spread(k + 2)
                    if k > 0 and k != 16:
                        y = ysum(k - 1)
                        hf[1 - x] = [y]
                y = ysum(31)
                hf[1] = [y]
                out_half(1, y)
                t = dv.now
                n = 0
                szf = [[], [], [], []]
                for c in range(4):
                    for half in range(2):
                        bank = n % 4
                        p = xz(4 + c, half, bank)
                        a = act(dB[0][:, bank, :], PS[:, bank, :], ACT.Silu, [p, t] + szf[bank])
                        pf[bank] = [a]
                        s_ = slice(512 * half, 512 * half + 512)
                        e = tt(dv, du[:, c, s_], du[:, c, s_], dB[0][:, bank, :], ALU.mult, [a, t])
                        szf[bank] = [e]
                        n += 1
                tf = [[], []]
                for i in range(8):
                    bank = 4 + i % 2
                    for c in range(4):
                        p = mm(PS[:, bank, 0:256], du[:, c, 128 * i:128 * i + 128], opw[:, c, :], c == 0, c == 3, pf[bank] + [e], inc=(c == 3))
                    if not rev_:
                        t = cp(evac_lane(), MO[:, 8 * b + i, :], PS[:, bank, 0:256], [p])
                        pf[bank] = [t]
                    else:
                        tmp = dA[0][:, i % 2, 0:256]
                        t = cp(ac, tmp, PS[:, bank, 0:256], [p] + tf[i % 2])
                        pf[bank] = [t]
                        p = mm(PS[:, 6 + i % 2, 0:256], anti, tmp, True, True, pf[6 + i % 2] + [t], inc=True)
                        tf[i % 2] = [p]
                        o = MO[:, 8 * b + 7 - i, :]
                        t = tt(dv, o, o, PS[:, 6 + i % 2, 0:256], ALU.add, [p])
                        pf[6 + i % 2] = [t]
                if sq == 3:
                    barrier()
                else:
                    oproj = [pe.now, dv.now, ac.now, gp.now]
                    dv.after(oproj)
            scr.at = scr.lo
            xn = scr.take([NT, D])
            st_at = scr.at
            layer_norm_T(src=MO, keep=xn, mul=lambda c: lg[:, c:c + 1], add=lambda c: lb[:, c:c + 1])
            scr.at = st_at
            hT = [scr.take([8, 512]) for _ in range(2)]
            hTf = [[], []]
            n = 0
            for k in range(4):
                x = k % 2
                hr = []
                for f in range(8):
                    bank = n % 4
                    n += 1
                    for c in range(2):
                        t = mm(PS[:, bank, :], fw1[:, c, 128 * f:128 * f + 128], XNT[:, c, 512 * k:512 * k + 512], c == 0, c == 1, pf[bank], inc=(c == 1))
                    t = act(hT[x][:, f, :], PS[:, bank, :], ACT.Gelu, [t] + hTf[x], bias=fb1[:, f:f + 1])
                    pf[bank] = [t]
                    hr.append(t)
                add_proj(X, lambda c, i, x=x, k=k: hT[x][:, c, 128 * (i - 4 * k):128 * (i - 4 * k) + 128], 8, lambda c: fw2[:, c, :],
                         fb2[0:1, :], tiles=range(4 * k, 4 * k + 4), w=hr, banks=(4, 5, 6, 7))
                hTf[x] = [pe.now]

        def flipped_T():
            order = [7, 6, 5, 4, 3, 2, 1, 0, 15, 14, 13, 12, 11, 10, 9, 8]
            base = scr.lo + 4096 * 3 + 1024 + 4096
            hp = Heap(base, base + 4096 * 2)
            mv, rs = stats(lambda i: X[:, i, :], NT, hp, 1e-5)
            xn = hp.take([NT, D])
            done = [normalise(xn[:, i, :], X[:, i, :], mv, rs, i) for i in range(NT)]
            for k in range(4):
                for c in range(2):
                    bank = (2 * k + c) % 8
                    for j in range(4):
                        i = order[4 * k + j]
                        t = mm(PS[:, bank, 128 * j:128 * j + 128], xn[:, i, 128 * c:128 * c + 128], anti, True, True, pf[bank] + [done[i]], inc=(j == 3))
                    t = cp(evac_lane(), XNT[:, c, 512 * k:512 * k + 512], PS[:, bank, :], [t])
                    pf[bank] = [t]

        def load_7():
            WB[1].clear()
            W[7] = load_w(WB[1], "pk7")

        def phase_7():
            w, wt = W[7]
            wq = w[:, 0:2048].rearrange("p (k n) -> p k n", k=8)
            ws = w[:, 2048:2054].rearrange("p (z c) -> p z c", z=3)
            row = scr.take([260], F32, 0, 1)
            ct = scr.take([4, D])
            ld = Load("d_p7")
            ld.add(row[:, 0:257], ins["pk7r"])
            for b in range(2):
                ld.add(ct[:, 2 * b, :], ins["ctx"][b, 0:128, :])
                ld.add(ct[0:26, 2 * b + 1, :], ins["ctx"][b, 128:154, :])
            XN = scr.take([NT, D])
            layer_norm_T(keep=XN)
            HQ = scr.take([NT, D])
            hqT = scr.take([2, 2048])
            prod = scr.take([2, 2048])
            d3 = scr.take([2, 308])
            rr = scr.take([308])
            nm = scr.take([NT])
            sm = scr.take([NT])
            ri = scr.take([NT])
            Pm = [scr.take([KC]) for _ in range(2)]
            PT = [scr.take([2, 128]) for _ in range(2)]
            ml = scr.take([2])
            M = scr.take([2])
            e_ = scr.take([NT])
            hc = scr.take([2, 2])
            sr = scr.take([2])
            w4 = scr.take([2, 2, D])
            for q in lanes:
                q.after([wt, ld.ready])
            for c in range(2):
                t = ts(dv, d3[:, c, :], ctxT[:, c, :], ws[:, 2, c:c + 1], ws[:, 0, c:c + 1], ALU.mult, ALU.add)
            for c in range(2):
                p = mm(PS[0:1, 0, 0:308], ws[:, 1, c:c + 1], ctxT[:, c, :], c == 0, c == 1, pf[0], inc=(c == 1))
            t = ts(dv, rr[0:1, :], PS[0:1, 0, 0:308], row[0:1, 256:257], None, ALU.add, None, [p, t])
            pf[0] = [t]
            pe.after([t])
            pfree = [[], []]
            ptfree = [[], []]
            for i in range(NT):
                b, x = i // 8, i % 2
                bk = 4 * x
                for c in range(2):
                    mm(PS[:, bk, 0:KC], XNT[:, c, 128 * i:128 * i + 128], d3[:, c, KC * b:KC * b + KC], c == 0, False, pf[bk])
                p = mm(PS[:, bk, 0:KC], ones[0:1, 0:128], rr[0:1, KC * b:KC * b + KC], False, True, (), inc=True)
                t = red(nm[:, i:i + 1], PS[:, bk, 0:KC], ALU.max, [p], neg=True)
                t = act(Pm[x], PS[:, bk, 0:KC], ACT.Exp, [t] + pfree[x], bias=nm[:, i:i + 1], acc=sm[:, i:i + 1])
                pf[bk] = [t]
                r = recip(ri[:, i:i + 1], sm[:, i:i + 1], [t])
                tr(PS[:, bk + 1, 0:128], Pm[x][:, 0:128], ident, [t] + pf[bk + 1])
                p = tr(PS[0:26, bk + 1, 128:256], Pm[x][:, 128:154], ident, (), inc=True)
                pfree[x] = [p]
                e1 = cp(ac, PT[x][:, 0, :], PS[:, bk + 1, 0:128], [p] + ptfree[x])
                e2 = cp(ac, PT[x][0:26, 1, :], PS[0:26, bk + 1, 128:256], [])
                pf[bk + 1] = [e2]
                mm(PS[:, bk + 2, 0:256], PT[x][:, 0, :], ct[:, 2 * b, :], True, False, [e2] + pf[bk + 2])
                p = mm(PS[:, bk + 2, 0:256], PT[x][0:26, 1, :], ct[0:26, 2 * b + 1, :], False, True, (), inc=True)
                ptfree[x] = [p]
                t = ts(dv, HQ[:, i, :], PS[:, bk + 2, 0:256], ri[:, i:i + 1], None, ALU.mult, None, [p, r])
                pf[bk + 2] = [t]
            t = red(ml, nm.rearrange("p (b t) -> p b t", b=2), ALU.min, [dv.now], neg=True)
            t = gp.put(lambda e: e.partition_all_reduce(M, ml, 128, bass.bass_isa.ReduceOp.max), [t])
            t = ts(dv, M, M, -1.0, None, ALU.mult, None, [t])
            for b in range(2):
                t2 = act(e_[:, 8 * b:8 * b + 8], nm[:, 8 * b:8 * b + 8], ACT.Exp, [t], bias=M[:, b:b + 1], scale=-1.0)
            for b in range(2):
                for c in range(3):
                    o = PS[:, 3, 4 * b + c:4 * b + c + 1]
                    for k in range(8):
                        i = 8 * b + k
                        l = XN[:, i, 128 * c:128 * c + 128] if c < 2 else ones
                        p = mm(o, l, e_[:, i:i + 1], k == 0, k == 7, [t2] + pf[3], inc=(k == 7))
            v = PS[:, 3, 0:8].rearrange("p (b c) -> p b c", b=2)
            t = recip(sr, v[:, :, 2], [p])
            t = tt(dv, hc, v[:, :, 0:2], bc(sr.unsqueeze(2), [128, 2, 2]), ALU.mult, [t])
            pf[3] = [t]
            for b in range(2):
                for c in range(2):
                    t2 = stt(w4[:, b, c, :], wq[:, 6 + c, :], hc[:, b, c:c + 1], wq[:, c, :], ALU.mult, ALU.add, [t])
            barrier()
            to_T(lambda i, c: HQ[:, i, 128 * c:128 * c + 128], lambda c, k: hqT[:, c, 512 * k:512 * k + 512], 2, lambda i: [])
            barrier()
            tt(gp, prod[:, 0, :], XNT[:, 0, :], hqT[:, 0, :], ALU.mult)
            tt(dv, prod[:, 1, :], XNT[:, 1, :], hqT[:, 1, :], ALU.mult)
            barrier()

            def lhs(c, i):
                return [XNT, hqT, prod][c // 2][:, c % 2, 128 * i:128 * i + 128]
            for b in range(2):
                add_proj(X, lhs, 6, lambda c, b=b: w4[:, b, c, :] if c < 2 else wq[:, c, :], row[0:1, 0:256],
                         tiles=range(8 * b, 8 * b + 8))

        def top2(l, heap, t):
            oh1, t = first_max(l, heap, [t])
            l2 = heap.take([NT, 8])
            t = stt(l2, oh1, NEG, l, ALU.mult, ALU.add, [t])
            oh2, t = first_max(l2, heap, [t])
            return oh1, oh2, l2, t

        def load_8():
            WB[0].clear()
            W[8] = load_w(WB[0], "pk8")

        def add_H(H):
            for k in range(4):
                v = X[:, 4 * k:4 * k + 4, :]
                tt([dv, gp][k % 2], v, v, H[:, 4 * k:4 * k + 4, :], ALU.add, [q.now for q in (dv, gp)])

        def phase_8():
            w, wt = W[8]
            WA.clear()
            H = WA.take([NT, D])
            zt = WA.take([1024])
            sp.after([fill(gp, zt, 0.0)])
            zero_rows(xg8, 6144, zt)
            zero_done = zeros.ready
            wo = w_rows(w[:, 1536:2048])
            l1 = w[:, 2048:2050]
            l2 = w[:, 2050:2052]
            gw = w[:, 2052:2068].rearrange("p (c n) -> p c n", c=2)
            for q in lanes:
                q.after([wt])
            layer_norm_T(keep=H)
            barrier()
            rms_T(H, lambda c: l1[:, c:c + 1], 1e-5)
            barrier()
            att = Attention(S, False, plain_qkv(w_seg(w[:, 0:1536]), None, None, wt))
            att.run()
            out_proj(att, wo, None, H, wt)
            barrier()
            scr.clear()
            xn = scr.take([NT, D])
            rms_T(H, lambda c: l2[:, c:c + 1], 1e-5, keep=xn)
            l, t = logits8(lambda c: gw[:, c, :], None, scr)
            oh1, oh2, lm, t = top2(l, scr, t)
            ohs = (oh1, oh2)
            loc, cnt, tl = places(ohs, scr, t)
            m3 = scr.take([8, 8])
            tiles_ = scr.take([8])
            end = scr.take([8])
            beg = scr.take([8])
            tmp = scr.take([NT, 8])
            idf = scr.take([2, NT])
            idx = scr.take([2, NT], I32)
            te = scr.take([24, 8])
            wif = scr.take([24])
            widx = scr.take([24], I32)
            t2 = ts(dv, m3, bc(el8.unsqueeze(1), [128, 8, 8]), 256.0, None, ALU.mult, None, [tl])
            t2 = tt(dv, m3, bc(cnt.unsqueeze(2), [128, 8, 8]), m3, ALU.is_gt, [t2])
            t2 = red(tiles_, m3, ALU.add, [t2])
            t2 = dv.put(lambda e: e.tensor_tensor_scan(out=end, data0=ones[:, 0:8], data1=tiles_, initial=0.0, op0=ALU.mult, op1=ALU.add), [t2])
            t2 = tt(dv, beg, end, tiles_, ALU.subtract, [t2])
            for z in range(2):
                t2 = stt(loc[z], bc(beg.unsqueeze(2), [128, 8, NT]), 256.0, loc[z], ALU.mult, ALU.add, [t2])
                t2 = tt(dv, tmp, ohs[z], loc[z].rearrange("p e i -> p i e"), ALU.mult, [t2])
                t2 = red(idf[:, z, :], tmp, ALU.add, [t2])
                t2 = cp(dv, idx[:, z, :], idf[:, z, :], [t2])
                lsc = scatter_rows(xg8, 6143, xn, idx[:, z, :], [t2, zero_done])
            t2 = tt(dv, te, bc(end.unsqueeze(1), [128, 24, 8]), bc(iota24.unsqueeze(2), [128, 24, 8]), ALU.is_le, [t2])
            t2 = red(wif, te, ALU.add, [t2])
            t2 = ts(dv, wif, wif, 7.0, 128.0, ALU.min, ALU.mult, [t2])
            t2 = ts(dv, wif, wif, pcol, None, ALU.add, None, [t2])
            tw = cp(dv, widx, wif, [t2])
            g2 = scr.take([2, NT])
            m1 = g2[:, 0, :]
            m2 = g2[:, 1, :]
            ta = red(m1, l, ALU.max, [t])
            tb = red(m2, lm, ALU.max, [t])
            t = tt(dv, m2, m2, m1, ALU.subtract, [ta, tb])
            t = act(m2, m2, ACT.Exp, [t])
            t = ts(dv, m1, m2, 1.0, None, ALU.add, None, [t])
            t = recip(m1, m1, [t])
            t = tt(dv, m2, m2, m1, ALU.mult, [t])
            dv.after([t])
            NTL = 23
            ring = [scr.take([3072]) for _ in range(3)]
            XE = [scr.take([2, D]) for _ in range(2)]
            XT = [scr.take([2, 256]) for _ in range(2)]
            Y = [scr.take([2, D]) for _ in range(2)]
            hT = [scr.take([4, 256]) for _ in range(2)]
            sg = [scr.take([256]) for _ in range(2)]
            yz = [xn, scr.take([NT, D])]
            lwt = [Load("d_w8a"), Load("d_w8b"), Load("d_w8c")]
            lxe = [Load("d_x8a"), Load("d_x8b")]
            lye = [Load("d_y8a"), Load("d_y8b")]
            xef, xtf, hf, sgf = [[], []], [[], []], [[], []], [[], []]
            wrows = ins["pk8e"].rearrange("e p n -> (e p) n")

            def load_w8(j, w):
                gp.after(w)
                l = lwt[j % 3]
                gp.items.append(move_rows(ring[j % 3], None, wrows, bass.IndirectOffsetOnAxis(widx[:, j:j + 1], 0), 1023, l.sem))
                l.n += 16

            def load_x(j):
                lxe[j % 2].add(XE[j % 2], xg8[256 * j:256 * j + 256, :].rearrange("(j p) c -> p j c", p=128), [lsc.ready] + xef[j % 2])

            def turn_x(j):
                bk = 4 + j % 2
                for c in range(2):
                    for i in range(2):
                        t = tr(PS[:, bk, 256 * c + 128 * i:256 * c + 128 * i + 128], XE[j % 2][:, i, 128 * c:128 * c + 128], ident,
                               [lxe[j % 2].ready] + pf[bk], inc=(c == 1 and i == 1))
                xef[j % 2] = [t]
                for c in range(2):
                    t2 = ts(dv, XT[j % 2][:, c, :], PS[:, bk, 256 * c:256 * c + 256], l2[:, c:c + 1], None, ALU.mult, None, [t] + xtf[j % 2])
                pf[bk] = [t2]
                return [t2]

            def down(item):
                j, w2, hr = item
                x = j % 2
                bk = 6 + x
                for i in range(2):
                    for f in range(4):
                        t = mm(PS[:, bk, 256 * i:256 * i + 256], hT[x][:, f, 128 * i:128 * i + 128], w2[:, f, :], f == 0, f == 3, pf[bk] + hr,
                               inc=(i == 1 and f == 3))
                hf[x] = [t]
                e = cp(ac, Y[x], PS[:, bk, :].rearrange("p (k c) -> p k c", k=2), [t, lye[x].ready])
                pf[bk] = [e]
                lye[x].add(yg8[256 * j:256 * j + 256, :].rearrange("(j p) c -> p j c", p=128), Y[x], [e])
                return t
            for j in range(3):
                load_w8(j, [tw])
            load_x(0)
            load_x(1)
            xt = turn_x(0)
            pend = None
            nb = 0
            for j in range(NTL):
                x = j % 2
                rg = ring[j % 3]
                w13 = [rg[:, 1024 * z:1024 * z + 1024].rearrange("p (c n) -> p c n", c=2) for z in range(2)]
                w2 = rg[:, 2048:3072].rearrange("p (f n) -> p f n", f=4)
                pe.after([lwt[j % 3].ready] + xt)
                hr = []
                for f in range(4):
                    bk = nb % 4
                    y = nb % 2
                    nb += 1
                    for z in range(2):
                        for c in range(2):
                            t = mm(PS[:, bk, 256 * z:256 * z + 256], w13[z][:, c, 128 * f:128 * f + 128], XT[x][:, c, :], c == 0, c == 1, pf[bk],
                                   inc=(z == 1 and c == 1))
                    a = act(sg[y], PS[:, bk, 0:256], ACT.Silu, [t] + sgf[y])
                    e = tt(dv, hT[x][:, f, :], PS[:, bk, 256:512], sg[y], ALU.mult, [a] + hf[x])
                    pf[bk] = [e]
                    sgf[y] = [e]
                    hr.append(e)
                xtf[x] = [t]
                if j + 1 < NTL:
                    xt = turn_x(j + 1)
                if j + 2 < NTL:
                    load_x(j + 2)
                if pend is not None:
                    t = down(pend)
                    if j + 2 < NTL:
                        load_w8(j + 2, [t])
                pend = (j, w2, hr)
            down(pend)
            combine(yg8, 5887, yz, idx, g2, [lye[0].ready, lye[1].ready, lsc.ready], H)

        def load_9():
            WB[1].clear()
            W[9] = load_w(WB[1], "pk9")

        def phase_9():
            w, wt = W[9]
            dq, uqT = w[:, 0:16], w[:, 16:32]
            dkv = w[:, 32:64].rearrange("p (c n) -> p c n", c=2)
            ukvT = w[:, 64:128].rearrange("p (c n) -> p c n", c=2)
            kr, qr = w[0:64, 128:144], w[0:64, 144:160]
            woT = w[0:16, 160:176]
            nw = w[:, 176:208].rearrange("p (z d) -> p z d", z=2)
            for q in lanes:
                q.after([wt])
            layer_norm_T()
            sm = scr.take([80])
            BD = scr.take([5, 8, 16])
            RQ = scr.take([NT, 2, 16])
            mark = scr.at
            sq = [scr.take([2, 256]) for _ in range(2)]
            sd = scr.take([NT * 32])
            mm(PS[0:16, 0, 0:16], dq, uqT, True, True)
            for c in range(2):
                mm(PS[0:16, 0, 16:48], dkv[:, c, :], ukvT[:, c, :], c == 0, c == 1)
            p = mm(PS[0:16, 0, 48:64], kr, qr, True, True, (), inc=True)
            t1 = cp(dv, sm[0:16, 0:64], PS[0:16, 0, 0:64], [p])
            t2 = cp(dv, sm[0:16, 64:80], woT)
            p = mm(PS[:, 1, 0:80], rep16, sm[0:16, :], True, True, [t1, t2], inc=True)
            t = tt(dv, BD, bc(PS[:, 1, 0:80].rearrange("p (z d) -> p z d", z=5).unsqueeze(2), [128, 5, 8, 16]),
                   bc(bdm.unsqueeze(1).unsqueeze(3), [128, 5, 8, 16]), ALU.mult, [p])
            pe.after([t])
            for q in (pe,):
                q.after([t])
            flat = BD.rearrange("p z h d -> p (z h d)")
            fr = [[], []]
            pf[0] = []
            for i in range(NT):
                x = i % 2
                for hh in range(2):
                    p = mm(PS[:, 2 + x, 256 * hh:256 * hh + 256], XNT[:, hh, 128 * i:128 * i + 128], flat[:, 0:256], True, True, pf[2 + x], inc=(hh == 1))
                a = act(sq[x], PS[:, 2 + x, :].rearrange("p (s n) -> p s n", s=2), ACT.Square, [p] + fr[x])
                pf[2 + x] = [a]
                t = red(RQ[:, i], sq[x].rearrange("p s (h d) -> p s h d", d=16), ALU.add, [a])
                fr[x] = [t]
            rq = RQ.rearrange("p i s h -> p (i s h)")
            t = ts(dv, rq, rq, 1.0 / 16, 1.1920929e-07, ALU.mult, ALU.add, [dv.now])
            t = act(sd, rq, ACT.Sqrt, [t])
            t = recip(rq, sd, [t])
            barrier()
            scr.at = mark

            def qkv(b, hh, t, rows, hq, hk, ps, w):
                r0 = b * S + 128 * t
                return mm(ps[:, 0:512], XNT[:, hh, r0:r0 + 128], flat[:, 0:512], True, True, w, inc=True)

            def post(b, hh, t, ps, w, a):
                t1 = tt(dv, a.rearrange("p z h d -> p (z h) d"), ps[:, 0:256].rearrange("p (h d) -> p h d", d=16),
                        bc(RQ[:, 8 * b + t, hh, :].unsqueeze(2), [128, 16, 16]), ALU.mult, w)
                t2 = tt(dv, a, a, bc(nw.unsqueeze(2), [128, 2, 8, 16]), ALU.mult, [t1])
                t3 = tt(dv, a[:, 1], a[:, 1], ps[:, 384:512].rearrange("p (h d) -> p h d", d=16), ALU.add, [t2])
                return t3, [t3]
            att = Attention(S, True, qkv, post=post)
            att.run()
            barrier()
            to_T(lambda i, c: att.O[:, i, 128 * c:128 * c + 128], lambda c, k: XNT[:, c, 512 * k:512 * k + 512], 2, lambda i: [])
            barrier()
            for i in range(0, NT, 2):
                bk = (i // 2) % 8
                for z in range(2):
                    for c in range(2):
                        p = mm(PS[:, bk, 256 * z + 128 * c:256 * z + 128 * c + 128], XNT[:, c, 128 * (i + z):128 * (i + z) + 128], flat[:, 512:640],
                               True, True, pf[bk], inc=(z == 1 and c == 1))
                v = X[:, i:i + 2, :]
                t = tt(dv, v, PS[:, bk, :].rearrange("p (k c) -> p k c", k=2), v, ALU.add, [p])
                pf[bk] = [t]

        def load_10():
            WB[0].clear()
            W[10] = load_w(WB[0], "pk10")

        def phase_10():
            w, wt = W[10]
            b1 = scr.take([NT, KC])
            bT = scr.take([2, 2048])
            row = scr.take([256], F32, 0, 1)
            ld = Load("d_p10")
            ld.add(row, ins["pk10r"])
            mi = b1.bitcast(I32)
            for b in range(2):
                ld.add(mi[:, 8 * b:8 * b + 8, :], ins["mask32"][b, 0].rearrange("(t p) k -> p t k", p=128))
            layer_norm_T()
            mark = scr.at
            b2 = scr.take([NT, KC])
            an = scr.take([NT])
            for q in lanes:
                q.after([wt, ld.ready])
            t = ts(dv, b1, mi, 0.0, None, ALU.not_equal, None)
            t = red(an, b1, ALU.max, [t])
            t1 = ts(dv, an, an, BIG, None, ALU.mult, None, [t])
            t2 = ts(dv, b2, b1, 2 * BIG, None, ALU.mult, None, [t])
            t2 = tt(dv, b2, b2, bc(an.unsqueeze(2), [128, NT, KC]), ALU.subtract, [t1, t2])
            ts(dv, b1, b1, BIG, -1e9, ALU.mult, ALU.add, [t2])
            for k in range(4):
                for z in range(2):
                    rows = 128 if z == 0 else 26
                    bk = 2 * (k % 4) + z
                    for j in range(4):
                        p = tr(PS[0:rows, bk, 128 * j:128 * j + 128], b2[:, 4 * k + j, 128 * z:128 * z + rows], ident, [t2] + pf[bk], inc=(j == 3))
                    t = cp(evac_lane(), bT[0:rows, z, 512 * k:512 * k + 512], PS[0:rows, bk, :], [p])
                    pf[bk] = [t]
            barrier()
            scr.at = mark
            att = Attention(KC, False, plain_qkv(w_seg(w[:, 0:1536]), None, None, wt), bound=(b1, bT))
            att.run()
            out_proj(att, w_rows(w[:, 1536:2048]), row[0:1, 0:256], X, wt)

        def load_11():
            WB[1].clear()
            W[11] = load_w(WB[1], "pk11")

        def phase_11():
            w, wt = W[11]
            WA.clear()
            H = WA.take([NT, D])
            lw = w[:, 2048:2056].rearrange("p (z c) -> p z c", z=4)
            wr = w[:, 2056:2072].rearrange("p (c n) -> p c n", c=2)
            wo = w_rows(w[:, 1536:2048])
            row = scr.take([1024], F32, 0, 1)
            ld = Load("d_p11")
            ld.add(row, ins["pk11r"])
            for q in lanes:
                q.after([wt, ld.ready])
            zt = WA.take([1024])
            sp.after([fill(gp, zt, 0.0)])
            zero_rows(xg, 4096, zt)
            zero_done = zeros.ready
            layer_norm_T(keep=H)
            barrier()
            layer_norm_T(src=H, mul=lambda c: lw[:, 0, c:c + 1], add=lambda c: lw[:, 1, c:c + 1])
            barrier()
            att = Attention(S, False, plain_qkv(w_seg(w[:, 0:1536]), None, row[:, 0:768].rearrange("p (s n) -> p s n", s=2), wt))
            att.run()
            out_proj(att, wo, row[0:1, 768:1024], H, wt)
            barrier()
            scr.clear()
            ring = [scr.take([4360]) for _ in range(2)]
            lw1 = [Load("d_w1a"), Load("d_w1b")]
            lw2 = [Load("d_w2a"), Load("d_w2b")]

            def load_w1(e, w=()):
                lw1[e % 2].add(ring[e % 2][:, 0:2056], ins["pk11e"][e, :, 0:2056], w)

            def load_w2(e, w=()):
                lw2[e % 2].add(ring[e % 2][:, 2056:4360], ins["pk11e"][e, :, 2056:4360], w)
            for k in range(2):
                load_w1(k)
                load_w2(k)
            xn = scr.take([NT, D])
            layer_norm_T(src=H, keep=xn, mul=lambda c: lw[:, 2, c:c + 1], add=lambda c: lw[:, 3, c:c + 1])
            l, t = logits8(lambda c: wr[:, c, :], None, scr)
            p, r, t2 = softmax8(l, scr, [t])
            t2 = tt(dv, p, p, bc(r.unsqueeze(2), [128, NT, 8]), ALU.mult, [t2])
            oh1, t = first_max(p, scr, [t2])
            l2 = scr.take([NT, 8])
            t = stt(l2, oh1, NEG, l, ALU.mult, ALU.add, [t])
            oh2, t = first_max(l2, scr, [t])
            ohs = (oh1, oh2)
            loc, tot, t = places(ohs, scr, t)
            drop = scr.take([8, NT])
            idf = scr.take([2, NT])
            idx = scr.take([2, NT], I32)
            tmp = scr.take([NT, 8])
            e512 = bc(el8.unsqueeze(2), [128, 8, NT])
            for z in range(2):
                t = ts(dv, drop, loc[z], 512.0, None, ALU.is_ge, None, [t])
                t = stt(loc[z], e512, 512.0, loc[z], ALU.mult, ALU.add, [t])
                t = stt(loc[z], drop, 131072.0, loc[z], ALU.mult, ALU.add, [t])
                t = tt(dv, tmp, ohs[z], loc[z].rearrange("p e i -> p i e"), ALU.mult, [t])
                t = red(idf[:, z, :], tmp, ALU.add, [t])
                t = cp(dv, idx[:, z, :], idf[:, z, :], [t])
                lsc = scatter_rows(xg, 4095, xn, idx[:, z, :], [t, zero_done])
                t = ts(dv, drop, drop, -1.0, 1.0, ALU.mult, ALU.add, [t])
                t = tt(dv, ohs[z], ohs[z], drop.rearrange("p e i -> p i e"), ALU.mult, [t])
            G = scr.take([NT, 8])
            g2 = scr.take([2, NT])
            dn = scr.take([NT])
            t = tt(dv, G, oh1, oh2, ALU.add, [t])
            t = tt(dv, G, G, p, ALU.mult, [t])
            t = red(dn, G, ALU.add, [t])
            t = ts(dv, dn, dn, 1.1920929e-07, None, ALU.max, None, [t])
            t = recip(dn, dn, [t])
            t = ts(dv, dn, dn, 0.8, None, ALU.mult, None, [t])
            t = tt(dv, G, G, bc(dn.unsqueeze(2), [128, NT, 8]), ALU.mult, [t])
            for z in range(2):
                t = tt(dv, tmp, ohs[z], G, ALU.mult, [t])
                t = red(g2[:, z, :], tmp, ALU.add, [t])
            dv.after([t])
            XE = [scr.take([4, D]) for _ in range(2)]
            Y = [scr.take([4, D]) for _ in range(2)]
            hT = [scr.take([8, 512]) for _ in range(2)]
            ye = scr.take([NT, D])
            yz = [xn, ye]
            lxe = [Load("d_xe0"), Load("d_xe1")]
            lye = [Load("d_ye0"), Load("d_ye1")]
            xef, hf = [[], []], [[], []]
            xt_free = [[] for _ in range(4)]

            def load_x(e):
                lxe[e % 2].add(XE[e % 2], xg[512 * e:512 * e + 512, :].rearrange("(j p) c -> p j c", p=128), [lsc.ready] + xef[e % 2])

            def turn_x(e):
                toks = []
                for c in range(2):
                    bk = 6 + c
                    for j in range(4):
                        t = tr(PS[:, bk, 128 * j:128 * j + 128], XE[e % 2][:, j, 128 * c:128 * c + 128], ident,
                               [lxe[e % 2].ready] + pf[bk], inc=(j == 3))
                    v = XNT[:, c, 512 * (e % 4):512 * (e % 4) + 512]
                    t = ts(dv, v, PS[:, bk, :], lw[:, 2, c:c + 1], lw[:, 3, c:c + 1], ALU.mult, ALU.add, [t] + xt_free[e % 4])
                    pf[bk] = [t]
                    toks.append(t)
                xef[e % 2] = [pe.now]
                return toks

            lw2_at = {}

            def down(item):
                e, w2, b2, hr = item
                x = e % 2
                hr = hr + [lw2_at[e]]
                dv.after([lw2_at[e]])
                for i2 in range(2):
                    bk = 4 + i2
                    for z in range(2):
                        i = 2 * i2 + z
                        for f in range(8):
                            t = mm(PS[:, bk, 256 * z:256 * z + 256], hT[x][:, f, 128 * i:128 * i + 128], w2[:, f, :], f == 0, f == 7, pf[bk] + hr,
                                   inc=(f == 7))
                    t2 = tt(dv, Y[x][:, 2 * i2:2 * i2 + 2, :], PS[:, bk, :].rearrange("p (k c) -> p k c", k=2),
                            bc(b2.unsqueeze(1), [128, 2, D]), ALU.add, [t, lye[x].ready])
                    pf[bk] = [t2]
                hf[x] = [t]
                lye[x].add(yg[512 * e:512 * e + 512, :].rearrange("(j p) c -> p j c", p=128), Y[x], [t2])
            load_x(0)
            load_x(1)
            for z in range(2):
                fill(gp, yz[z], 0.0, [lsc.ready, gp.now])
            xt = turn_x(0)
            pend = None
            for e in range(8):
                y = e % 2
                w1 = ring[y][:, 0:2048].rearrange("p (c n) -> p c n", c=2)
                bb = ring[y][:, 2048:2056]
                w2 = ring[y][:, 2056:4104].rearrange("p (f n) -> p f n", f=8)
                b2 = ring[y][:, 4104:4360]
                for q in (pe, ac, dv):
                    q.after([lw1[y].ready])
                hr = []
                pe.after(xt)
                for f in range(8):
                    bk = f % 4
                    for c in range(2):
                        t = mm(PS[:, bk, :], w1[:, c, 128 * f:128 * f + 128], XNT[:, c, 512 * (e % 4):512 * (e % 4) + 512], c == 0, c == 1, pf[bk], inc=(c == 1))
                    if f % 2:
                        t = act(hT[y][:, f, :], PS[:, bk, :], ACT.Relu, [t] + hf[y], bias=bb[:, f:f + 1])
                    else:
                        t = ts(dv, hT[y][:, f, :], PS[:, bk, :], bb[:, f:f + 1], 0.0, ALU.add, ALU.max, [t] + hf[y])
                    pf[bk] = [t]
                    hr.append(t)
                xt_free[e % 4] = [pe.now]
                if e + 2 < 8:
                    load_w1(e + 2, [pe.now] + hr)
                if e + 1 < 8:
                    xt = turn_x(e + 1)
                if e + 2 < 8:
                    load_x(e + 2)
                if pend is not None:
                    down(pend)
                    if e + 1 < 8:
                        load_w2(e + 1, [pe.now, dv.now])
                pend = (e, w2, b2, hr)
                lw2_at[e] = lw2[y].ready
            down(pend)
            combine(yg, 4095, yz, idx, g2, [lye[0].ready, lye[1].ready, gp.now], H)

        def places(ohs, heap, t):
            loc = [heap.take([8, NT]) for _ in range(2)]
            tot = [heap.take([8, NT + 1]) for _ in range(2)]
            of = [heap.take([8, NT + 1]) for _ in range(2)]
            on = heap.take([NT + 1])
            fill(dv, tot[0], 0.0)
            fill(dv, tot[1], 0.0)
            zz = fill(dv, on, 1.0)
            for z, oh in enumerate(ohs):
                f = oh.rearrange("p i e -> p (i e)")
                p1 = mm(PS[:, 2 * z + 1, 0:128], upper, f, True, True, [t] + pf[2 * z + 1], inc=True)
                p2 = mm(PS[:, 2 * z + 2, 0:128], ones, f, True, True, pf[2 * z + 2], inc=True)
                t1 = cp(dv, tot[z][:, :, 1:NT + 1], PS[:, 2 * z + 2, 0:128].rearrange("p (i e) -> p e i", e=8), [p2, zz])
                pf[2 * z + 2] = [t1]
                if z == 1:
                    t1 = cp(dv, tot[1][:, :, 0], of[0][:, :, NT], [t1, dv.now])
                for e in range(8):
                    t2 = dv.put(lambda q, e=e, z=z: q.tensor_tensor_scan(out=of[z][:, e, :], data0=on, data1=tot[z][:, e, :],
                                                                        initial=0.0, op0=ALU.mult, op1=ALU.add), [t1])
                t2 = tt(dv, loc[z], PS[:, 2 * z + 1, 0:128].rearrange("p (i e) -> p e i", e=8), of[z][:, :, 0:NT], ALU.add, [p1, t2])
                pf[2 * z + 1] = [t2]
                t2 = ts(dv, loc[z], loc[z], -1.0, None, ALU.add, None, [t2])
            return loc, of[1][:, :, NT], t2

        def move_rows(o, oo, i, io, bound, s):
            return lambda e: e.indirect_dma_start(o, oo, i, io, bounds_check=bound, oob_is_err=False).then_inc(s, 16)

        rows_moved = {}

        def rows_load(name):
            if name not in rows_moved:
                rows_moved[name] = Load(name)
            return rows_moved[name]

        def scatter_rows(dst, bound, src, idx, w):
            l = rows_load("d_scatter")
            gp.after(w)
            for i in range(NT):
                gp.items.append(move_rows(dst, bass.IndirectOffsetOnAxis(idx[:, i:i + 1], 0), src[:, i, :], None, bound, l.sem))
                l.n += 16
            return l

        def combine(src, bound, yz, idx, g2, w, H):
            gp.after(w)
            for z in range(2):
                for k in range(4):
                    l = Load(f"d_gather{bound}_{z}_{k}")
                    for i in range(4 * k, 4 * k + 4):
                        gp.items.append(move_rows(yz[z][:, i, :], None, src, bass.IndirectOffsetOnAxis(idx[:, z, i:i + 1], 0), bound, l.sem))
                        l.n += 16
                    for i in range(4 * k, 4 * k + 4):
                        stt(H[:, i, :], yz[z][:, i, :], g2[:, z, i:i + 1], H[:, i, :], ALU.mult, ALU.add, [l.ready, dv.now])
            barrier()
            add_H(H)

        zeros = Load("d_zero")

        def zero_rows(dst, rows, z):
            for k in range(rows // 512):
                zeros.add(dst[512 * k:512 * k + 512, :].rearrange("(p j) c -> p (j c)", p=128), z)

        xg8 = nc.dram_tensor("xg8", (6144, D), F32, kind="Internal").ap()
        yg8 = nc.dram_tensor("yg8", (5888, D), F32, kind="Internal").ap()
        xg = nc.dram_tensor("xg", (4096, D), F32, kind="Internal").ap()
        yg = nc.dram_tensor("yg", (4096, D), F32, kind="Internal").ap()

        LOADS = {0: load_0, 1: load_1, 2: load_2, 3: load_3, 4: load_4, 5: load_5, 6: load_6, 7: load_7, 8: load_8, 9: load_9,
                 10: load_10, 11: load_11}
        AHEAD = {1: 0, 3: 2, 4: 3, 5: 4, 6: 5, 7: 6, 8: 7, 9: 8, 10: 9, 11: 10}
        loaded = set()

        def load_for(p):
            if p not in loaded:
                loaded.add(p)
                LOADS[p]()

        FN = {0: phase_0, 1: phase_1, 2: phase_2, 3: phase_3, 4: phase_4, 5: phase_5, 6: phase_6, 7: phase_7,
              8: phase_8, 9: phase_9, 10: phase_10, 11: phase_11}
        for p in phases:
            scr.clear()
            load_for(p)
            for nxt, at in AHEAD.items():
                if at == p and nxt in phases:
                    load_for(nxt)
            FN[p]()
            barrier()
        lo = Load("d_out")
        for i in range(4):
            lo.add(out.rearrange("b (t p) c -> p (b t) c", p=128)[:, 4 * i:4 * i + 4, :], X[:, 4 * i:4 * i + 4, :],
                   [q.now for q in lanes])
        sp.after([lo.ready])

        block = ctx.enter_context(nc.Block())

        @block.sync
        def _(e):
            for f in sp.items:
                f(e)

        @block.tensor
        def _(e):
            for f in pe.items:
                f(e)

        @block.scalar
        def _(e):
            for f in ac.items:
                f(e)

        @block.vector
        def _(e):
            for f in dv.items:
                f(e)

        @block.gpsimd
        def _(e):
            for f in gp.items:
                f(e)


def ch(w):
    w = np.asarray(w)
    k, n = w.shape
    return w.reshape(k // 128, 128, n).transpose(1, 0, 2).reshape(128, (k // 128) * n)


def cols(v):
    return np.asarray(v).reshape(-1, 128).T


def pad_rows(w):
    w = np.asarray(w)
    return np.concatenate([w, np.zeros((128 - w.shape[0], w.shape[1]), w.dtype)], 0)


def every(v):
    v = np.asarray(v).reshape(1, -1)
    return np.broadcast_to(v, (128, v.shape[1]))


def seg(wq, wk, wv):
    k = wq.shape[0] // 128
    w = np.stack([np.asarray(a).reshape(k, 128, 2, 128) for a in (wq, wk, wv)], 3)
    return w.transpose(1, 0, 2, 3, 4).reshape(128, -1)


def seg_row(bq, bk, bv):
    return np.stack([np.asarray(a).reshape(2, 128) for a in (bq, bk, bv)], 1).reshape(1, 768)


def cat(*a):
    return np.ascontiguousarray(np.concatenate(a, axis=1))


def constants():
    p = np.arange(128)
    c = np.zeros((128, 840), np.float32)
    c[:, 0:128] = np.eye(128)
    c[:, 128:256] = np.eye(128)[::-1]
    c[0:16, 256:384] = np.tile(np.eye(16), (1, 8))
    c[:, 384:512] = np.where(p[None, :] > p[:, None], NEG, 0.0)
    c[:, 512:640] = np.where(p[:, None] > p[None, :], NEG, 0.0)
    c[:, 640:768] = p[:, None] <= p[None, :]
    c[:, 768:776] = (p[:, None] // 16) == np.arange(8)[None, :]
    c[:, 776:784] = 8.0 - np.arange(8)[None, :]
    c[:, 786:794] = np.arange(8)[None, :]
    c[:, 794:818] = np.arange(24)[None, :]
    c[:, 818] = p
    return c


def layout(I):
    o = {}
    o["consts"] = constants()
    o["x"] = np.asarray(I["x"])
    ctx = np.asarray(I["ctx_1024"])
    o["ctx"] = ctx
    o["ctxT"] = ch(ctx.reshape(308, 256).T)
    o["mask8"] = np.ascontiguousarray(I["mask_BxS2_bf1"]).view(np.uint8).reshape(1, 308)
    o["mask32"] = np.asarray(I["mask_Bx1xSxS2_if1"])
    a = {k[8:]: np.asarray(v) for k, v in I.items() if k.startswith("L0_attn_")}
    ukv = np.stack([a["W_UK"].reshape(64, 2, 128), a["W_UV"].reshape(64, 2, 128)], 2).reshape(64, 512)
    o["pk0"] = cat(ch(a["W_DKV"]), pad_rows(ukv), ch(a["W_UQ"]), ch(a["W_O"]))
    a = {k[9:]: np.asarray(v) for k, v in I.items() if k.startswith("L0_xattn_")}

    o["pk1"] = cat(ch(a["Wq"]), ch(a["Wk"]), ch(a["Wv"]), cols(a["gl"]), cols(a["bl"]), cols(a["gm"]), cols(a["bm"]))
    o["pk1o"] = ch(a["Wo"])
    a = {k[7:]: np.asarray(v) for k, v in I.items() if k.startswith("L0_ffn_")}
    o["pk2"] = cat(ch(a["expert_w"].transpose(1, 0, 2).reshape(256, 2048)), ch(a["router_w"]), every(a["router_b"]))
    o["pk2e"] = a["expert_b"].reshape(1, 2048)
    a = {k[8:]: np.asarray(v) for k, v in I.items() if k.startswith("L1_attn_")}
    o["pk3"] = cat(ch(a["Wqkv"].T), ch(a["Wproj"].T))
    o["pk3r"] = np.concatenate([a["bqkv"], a["bproj"]]).reshape(1, 1024)
    a = {k[9:]: np.asarray(v) for k, v in I.items() if k.startswith("L1_xattn_")}
    o["pk4"] = cat(seg(a["Wq"].T, a["Wk"].T, a["Wv"].T), ch(a["Wo"].T))
    o["pk4r"] = cat(seg_row(a["bq"], a["bk"], a["bv"]), a["bo"].reshape(1, 256))
    a = {k[7:]: np.asarray(v) for k, v in I.items() if k.startswith("L1_ffn_")}
    o["pk5"] = cat(ch(a["w_gate"].T), ch(a["w_up"].T), ch(a["w_down"].T))
    a = {k[8:]: np.asarray(v) for k, v in I.items() if k.startswith("L2_attn_")}
    o["pk6"] = cat(ch(a["in_proj_w"]), ch(np.concatenate([a["x_proj_w"][:, 16:48], a["x_proj_w"][:, 0:16]], 1)), ch(a["out_proj_w"]), ch(a["ff_w1"]), pad_rows(np.concatenate([np.zeros((32, 512), np.float32), a["dt_proj_w"]], 0)), ch(a["conv_w"]),
                   cols(a["conv_b"]), cols(a["dt_proj_b"]), ch(a["A_log"]), cols(a["D"]), cols(a["ln_g"]), cols(a["ln_b"]), cols(a["ff_b1"]),
                   every(a["ff_b2"]))
    o["pk6b"] = ch(a["ff_w2"])
    a = {k[9:]: np.asarray(v) for k, v in I.items() if k.startswith("L2_xattn_")}
    o["pk7"] = cat(ch(a["W_qv"]), cols(a["w_sim"]))
    o["pk7r"] = np.concatenate([a["b_qv"], a["b_sim"]]).reshape(1, 257)
    a = {k[7:]: np.asarray(v) for k, v in I.items() if k.startswith("L2_ffn_")}
    o["pk8"] = cat(seg(a["wq"].T, a["wk"].T, a["wv"].T), ch(a["wo"].T), cols(a["ln1_w"]), cols(a["ln2_w"]), ch(a["gate_w"].T))
    o["pk8e"] = np.stack([cat(ch(a["w1"][e].T), ch(a["w3"][e].T), ch(a["w2"][e].T)) for e in range(8)])
    a = {k[8:]: np.asarray(v) for k, v in I.items() if k.startswith("L3_attn_")}
    o["pk9"] = cat(a["W_DQ"], np.ascontiguousarray(a["W_UQ"].T), ch(a["W_DKV"]), ch(a["W_UKV"].T), pad_rows(a["W_KR"]), pad_rows(a["W_QR"]),
                   pad_rows(a["W_O"].T), every(a["q_norm_w"]), every(a["k_norm_w"]))
    a = {k[9:]: np.asarray(v) for k, v in I.items() if k.startswith("L3_xattn_")}
    o["pk10"] = cat(seg(a["Wq"].T, a["Wk"].T, a["Wv"].T), ch(a["Wo"].T))
    o["pk10r"] = a["bo"].reshape(1, 256)
    a = {k[7:]: np.asarray(v) for k, v in I.items() if k.startswith("L3_ffn_")}
    o["pk11"] = cat(seg(a["wq"], a["wk"], a["wv"]), ch(a["wo"]), cols(a["ln1_g"]), cols(a["ln1_b"]), cols(a["ln2_g"]), cols(a["ln2_b"]),
                    ch(a["wr"]))
    o["pk11r"] = cat(seg_row(a["bq"], a["bk"], a["bv"]), a["bo"].reshape(1, 256))
    o["pk11e"] = np.stack([cat(ch(a["w1"][e]), cols(a["b1"][e]), ch(a["w2"][e]), every(a["b2"][e])) for e in range(8)])
    return {k: np.ascontiguousarray(v) for k, v in o.items()}


def kernel(**inputs):
    import concourse.bacc as _bacc
    from concourse import mybir as _mybir
    from concourse.bass_utils import run_bass_kernel_spmd as _run

    nc = _bacc.Bacc("TRN2", target_bir_lowering=False, num_devices=1)
    arrays = layout(inputs)
    ins = {}
    for name, a in arrays.items():
        ins[name] = nc.dram_tensor(f"in_{name}", a.shape, _mybir.dt.from_np(a.dtype), kind="ExternalInput").ap()
    out = nc.dram_tensor("out_0", (2, 1024, 256), _mybir.dt.float32, kind="ExternalOutput").ap()
    build(nc, ins, out, range(12))
    r = _run(nc, [{f"in_{k}": v for k, v in arrays.items()}], core_ids=[0])
    return r.results[0]["out_0"]
```

```python
from contextlib import ExitStack

import numpy as np
import concourse.bass as bass
from concourse import mybir

F32 = mybir.dt.float32
BF16 = mybir.dt.bfloat16
I32 = mybir.dt.int32
U8 = mybir.dt.uint8
F32R = mybir.dt.float32r
ALU = mybir.AluOpType
ACT = mybir.ActivationFunctionType
AX = mybir.AxisListType
NEG = -1e30
BIG = 1e30
S = 1024
NT = 16
KC = 154
D = 256
QH = 96
QM = 98


class Lane:

    def __init__(self, sem):
        self.sem = sem
        self.items = []
        self.count = 0
        self.seen = {}

    def after(self, toks):
        for sem, value in toks:
            if self.seen.get(sem.name, 0) < value:
                self.seen[sem.name] = value
                self.items.append(waiter(sem, value))

    def put(self, fn, toks=(), inc=True):
        self.after(toks)
        if inc:
            self.count += 1
            self.items.append(counted(fn, self.sem))
        else:
            self.items.append(fn)
        return (self.sem, self.count)

    @property
    def now(self):
        return (self.sem, self.count)


def waiter(sem, value):
    return lambda e: e.wait_ge(sem, value)


def counted(fn, sem):
    return lambda e: fn(e).then_inc(sem, 1)


def bc(ap, shape):
    return ap.broadcast_to(list(shape))


def build(nc, ins, out, phases):
    ctx = ExitStack()
    with ctx:
        def sem(name):
            return ctx.enter_context(nc.semaphore(name))

        pe = Lane(sem("s_pe"))
        ac = Lane(sem("s_act"))
        dv = Lane(sem("s_dve"))
        gp = Lane(sem("s_pool"))
        sp = Lane(sem("s_sp"))
        lanes = [pe, ac, dv, gp]

        TOT = 53200
        LOW = 20500
        RRW = 17616
        AR = ctx.enter_context(nc.sbuf_tensor("AR", [128, LOW], F32))
        with nc.sbuf_tensor("SC", [128, TOT - LOW], F32) as SC:
            pass
        RR = ctx.enter_context(nc.sbuf_tensor("RR", [128, RRW], F32R))
        SC1 = ctx.enter_context(nc.sbuf_tensor("SC1", [128, TOT - LOW - RRW], F32))
        upper_part = {"now": SC}
        PS = ctx.enter_context(nc.psum_tensor("PS", [128, 8, 512], F32))

        def view(off, dims, dt=F32, p0=0, p1=128):
            n = int(np.prod(dims))
            words = n if dt in (F32, I32) else n // 2
            if off < LOW:
                ap = AR[p0:p1, off:off + words]
            elif upper_part["now"] is SC:
                ap = SC[p0:p1, off - LOW:off - LOW + words]
            else:
                ap = SC1[p0:p1, off - LOW - RRW:off - LOW - RRW + words]
            if dt != F32:
                ap = ap.bitcast(dt)
            if len(dims) == 1:
                return ap
            names = "abcd"[:len(dims)]
            return ap.rearrange(f"p ({' '.join(names)}) -> p {' '.join(names)}",
                                **{k: v for k, v in zip(names, dims)})

        class Heap:
            def __init__(self, lo, hi):
                self.lo, self.hi, self.at = lo, hi, lo

            def take(self, dims, dt=F32, p0=0, p1=128):
                n = int(np.prod(dims))
                words = n if dt in (F32, I32) else (n + 1) // 2
                off = self.at
                self.at += words
                assert self.at <= self.hi, (self.at, self.hi)
                return view(off, dims, dt, p0, p1)

            def clear(self):
                self.at = self.lo

        fixed = Heap(0, 10000)
        WA = Heap(10000, 16300)
        WB = [Heap(16300, 18400), Heap(18400, 20500)]
        scr = Heap(LOW, TOT)

        X = fixed.take([NT, D])
        XNT = fixed.take([2, 2048])
        consts = fixed.take([840])
        ident = consts[:, 0:128]
        anti = consts[:, 128:256]
        rep16 = consts[0:16, 256:384]
        maskS_f = consts[:, 384:512]
        maskT_f = consts[:, 512:640]
        upper = consts[:, 640:768]
        bdm = consts[:, 768:776]
        rev = consts[:, 776:784]
        el8 = consts[:, 786:794]
        iota24 = consts[:, 794:818]
        pcol = consts[:, 818:819]
        ctxT = fixed.take([2, 308])
        ones = fixed.take([128])
        identb = fixed.take([128], BF16)
        maskS = fixed.take([128], BF16)
        maskT = fixed.take([128], BF16)

        def mm(o, l, r, start, stop, w=(), inc=False, tile=None):
            if tile is None:
                return pe.put(lambda e: e.matmul(o, l, r, start=start, stop=stop), w, inc)
            return pe.put(lambda e: e.matmul(o, l, r, start=start, stop=stop, tile_position=tile), w, inc)

        def tr(o, i, idn, w=(), inc=False):
            return pe.put(lambda e: e.transpose(o, i, idn), w, inc)

        def act(o, i, f, w=(), bias=None, scale=None, acc=None):
            kw = {}
            if bias is not None:
                kw["bias"] = bias
            if scale is not None:
                kw["scale"] = scale
            if acc is not None:
                kw["accum_out"] = acc
            return ac.put(lambda e: e.activation(o, i, f, **kw), w)

        def tt(q, o, a, b, op, w=()):
            return q.put(lambda e: e.tensor_tensor(o, a, b, op), w)

        def ts(q, o, a, s1, s2, op0, op1, w=()):
            if op1 is None:
                return q.put(lambda e: e.tensor_scalar(o, a, s1, None, op0), w)
            return q.put(lambda e: e.tensor_scalar(o, a, s1, s2, op0, op1), w)

        def stt(o, a, s, b, op0, op1, w=()):
            return dv.put(lambda e: e.scalar_tensor_tensor(out=o, in0=a, scalar=s, in1=b, op0=op0, op1=op1), w)

        def red(o, a, op, w=(), neg=False):
            if neg:
                return dv.put(lambda e: e.tensor_reduce(o, a, AX.X, op, negate=True), w)
            return dv.put(lambda e: e.tensor_reduce(o, a, AX.X, op), w)

        def high(o, i, w=()):
            return ts(dv, o.bitcast(I32), i.bitcast(I32), -4096, None, ALU.bitwise_and, None, w)

        def cp(q, o, i, w=()):
            if q is ac:
                return act(o, i, ACT.Copy, w)
            return q.put(lambda e: e.tensor_copy(o, i), w)

        def fill(q, o, v, w=()):
            return q.put(lambda e: e.memset(o, v), w)

        def recip(o, i, w=()):
            return dv.put(lambda e: e.reciprocal(o, i), w)

        def dma(o, i, s, w=()):
            sp.after(w)
            sp.items.append(lambda e: e.dma_start(o, i).then_inc(s, 16))

        def barrier():
            toks = [q.now for q in lanes]
            for q in lanes + [sp]:
                q.after(toks)
            for b in range(8):
                pf[b] = []

        pf = {b: [] for b in range(8)}
        turn = [0]

        def evac_lane():
            turn[0] += 1
            return ac if turn[0] % 2 else dv

        class Load:

            def __init__(self, name):
                self.sem = sem(name)
                self.n = 0

            def add(self, o, i, w=()):
                dma(o, i, self.sem, w)
                self.n += 16

            @property
            def ready(self):
                return (self.sem, self.n)

        l0 = Load("d_const")
        l0.add(consts[:, 0:840], ins["consts"])
        lx = Load("d_x")
        for i in range(4):
            lx.add(X[:, 4 * i:4 * i + 4, :],
                   ins["x"].rearrange("b (t p) c -> p (b t) c", p=128)[:, 4 * i:4 * i + 4, :])
        lc = Load("d_ctx")
        lc.add(ctxT, ins["ctxT"].rearrange("p (c n) -> p c n", c=2))
        fill(dv, ones, 1.0)
        cp(dv, identb, ident, [l0.ready])
        cp(dv, maskS, maskS_f)
        cp(dv, maskT, maskT_f)
        dv.after([lx.ready, lc.ready])
        ac.after([lx.ready, lc.ready])
        pe.after([l0.ready, lc.ready])
        gp.after([l0.ready, lc.ready, lx.ready])
        barrier()

        def load_w(heap, name, parts=128, width=None, dt=F32):
            heap_ap = heap.take([ins[name].shape[1]], dt, 0, parts)
            l = Load(f"d_{name}")
            n = ins[name].shape[1]
            half = (n + 1) // 2
            if n > 1024:
                l.add(heap_ap[:, 0:half], ins[name][:, 0:half], [])
                l.add(heap_ap[:, half:n], ins[name][:, half:n], [])
            else:
                l.add(heap_ap, ins[name], [])
            return heap_ap, l.ready

        def stats(src, n, heap, eps, rows=128, w=()):
            st = heap.take([n, 6])
            mv = heap.take([n, 2])
            ve = heap.take([n])
            sd = heap.take([n])
            rs = heap.take([n])
            dv.after(w)
            for i in range(n):
                dv.put(lambda e, i=i: e.bn_stats(st[0:rows, i, :], src(i)))
            t = dv.now
            for i in range(n):
                dv.put(lambda e, i=i: e.bn_aggr(mv[0:rows, i, :], st[0:rows, i, :]), [t])
            t = ts(dv, ve[0:rows], mv[0:rows, :, 1], eps, None, ALU.add, None, [dv.now])
            t = act(sd[0:rows], ve[0:rows], ACT.Sqrt, [t])
            t = recip(rs[0:rows], sd[0:rows], [t])
            dv.after([t])
            return mv, rs

        def normalise(dst, src, mv, rs, i, rows=128, w=()):
            return ts(dv, dst, src, mv[0:rows, i, 0:1], rs[0:rows, i:i + 1], ALU.subtract, ALU.mult, w)

        def normalised(dst, src, heap, eps, w=()):
            st = heap.take([NT, 6])
            mv = heap.take([NT, 2])
            sd = heap.take([NT])
            rs = heap.take([NT])
            dv.after(w)
            roots, done = {}, []

            def root(g):
                for i in range(4 * g, 4 * g + 4):
                    t = dv.put(lambda e, i=i: e.bn_stats(st[:, i, :], src[:, i, :]))
                for i in range(4 * g, 4 * g + 4):
                    t2 = dv.put(lambda e, i=i: e.bn_aggr(mv[:, i, :], st[:, i, :]), [t])
                s_ = slice(4 * g, 4 * g + 4)
                t = ts(dv, sd[:, s_], mv[:, s_, 1], eps, None, ALU.add, None, [t2])
                roots[g] = act(sd[:, s_], sd[:, s_], ACT.Sqrt, [t])

            def scale(g):
                s_ = slice(4 * g, 4 * g + 4)
                t = recip(rs[:, s_], sd[:, s_], [roots[g]])
                for i in range(4 * g, 4 * g + 4):
                    done.append(normalise(dst[:, i, :], src[:, i, :], mv, rs, i, w=[t]))
            root(0)
            root(1)
            for g in range(4):
                scale(g)
                if g + 2 < 4:
                    root(g + 2)
            return done

        def to_T(src, dst, chunks, ready, idn=None, mul=None, add=None, banks=range(8), groups=4, order=None):
            idn = ident if idn is None else idn
            toks = []
            nb = len(banks)
            n = 0
            for k in range(groups):
                for c in range(chunks):
                    b = banks[n % nb]
                    n += 1
                    for j in range(4):
                        i = 4 * k + j
                        t = tr(PS[:, b, 128 * j:128 * j + 128], src(i if order is None else order[i], c), idn,
                               pf[b] + ready(i if order is None else order[i]), inc=(j == 3))
                    if mul is None:
                        t = cp(ac, dst(c, k), PS[:, b, :], [t])
                    elif add is None:
                        t = act(dst(c, k), PS[:, b, :], ACT.Copy, [t], scale=mul(c))
                    else:
                        t = act(dst(c, k), PS[:, b, :], ACT.Identity, [t], scale=mul(c), bias=add(c))
                    pf[b] = [t]
                    toks.append(t)
            return toks

        def layer_norm_T(keep=None, mul=None, add=None, idn=None, order=None, src=None, eps=1e-5, twice=False):
            mark = scr.at
            src = X if src is None else src
            xn = keep if keep is not None else scr.take([NT, D])
            done = normalised(xn, src, scr, eps)
            if twice:
                done = normalised(xn, xn, scr, eps, [dv.now])
            toks = to_T(lambda i, c: xn[:, i, 128 * c:128 * c + 128],
                        lambda c, k: XNT[:, c, 512 * k:512 * k + 512], 2, lambda i: [done[i]],
                        idn=idn, mul=mul, add=add, order=order)
            scr.at = mark
            for q in lanes + [sp]:
                q.after(toks + [dv.now])
            return toks

        def rms_T(src, wcol, eps, keep=None):
            mark = scr.at
            sq = scr.take([2, D])
            ms = scr.take([NT])
            sd = scr.take([NT])
            rs = scr.take([NT])
            xn = keep if keep is not None else scr.take([NT, D])
            done, roots = [], {}

            def root(g):
                s_ = slice(4 * g, 4 * g + 4)
                for i in range(4 * g, 4 * g + 4):
                    t = act(sq[:, i % 2, :], src[:, i, :], ACT.Square, [ac.now], acc=ms[:, i:i + 1])
                t = ts(dv, sd[:, s_], ms[:, s_], 1.0 / D, eps, ALU.mult, ALU.add, [t])
                roots[g] = t

            def scale(g):
                s_ = slice(4 * g, 4 * g + 4)
                t = act(sd[:, s_], sd[:, s_], ACT.Sqrt, [roots[g]])
                t = recip(rs[:, s_], sd[:, s_], [t])
                for i in range(4 * g, 4 * g + 4):
                    done.append(ts(dv, xn[:, i, :], src[:, i, :], rs[:, i:i + 1], None, ALU.mult, None, [t]))
            root(0)
            root(1)
            for g in range(4):
                scale(g)
                if g + 2 < 4:
                    root(g + 2)
            toks = to_T(lambda i, c: xn[:, i, 128 * c:128 * c + 128],
                        lambda c, k: XNT[:, c, 512 * k:512 * k + 512], 2, lambda i: [done[i]], mul=wcol)
            scr.at = mark
            for q in lanes + [sp]:
                q.after(toks + [dv.now])

        def add_proj(dst, lhs, nchunks, rhs, bias=None, tiles=range(NT), w=(), banks=range(8)):
            pe.after(w)
            n = 0
            toks = []
            for g in range(0, len(tiles), 2):
                b = banks[n % len(banks)]
                n += 1
                for k in range(2):
                    i = tiles[g + k]
                    o = PS[:, b, 256 * k:256 * k + 256]
                    for c in range(nchunks):
                        last = (c == nchunks - 1) and bias is None
                        t = mm(o, lhs(c, i), rhs(c), c == 0, last, pf[b], inc=(last and k == 1))
                    if bias is not None:
                        t = mm(o, ones[0:1, 0:128], bias, False, True, (), inc=(k == 1))
                i = tiles[g]
                v = dst[:, i:i + 2, :]
                t = tt(dv, v, PS[:, b, :].rearrange("p (k c) -> p k c", k=2), v, ALU.add, [t])
                pf[b] = [t]
                toks.append(t)
            return toks

        class Attention:

            def __init__(self, KV, causal, qkv, post=None, mask=None, bias=None, depth=3):
                self.depth = depth
                self.KV, self.causal, self.qkv, self.post, self.mask, self.bias = KV, causal, qkv, post, mask, bias
                self.qS = [scr.take([8, S], BF16) for _ in range(2)]
                kn = S if KV == S else 160
                self.kS = [scr.take([8, kn], BF16) for _ in range(2)]
                self.nk = (KV + 127) // 128
                self.vE = [scr.take([self.nk, 152]) for _ in range(2)]
                self.vh = [v[:, :, 0:136].rearrange("p t (h e) -> p t h e", e=17) for v in self.vE]
                self.P = [scr.take([2, 512]) for _ in range(depth)]
                self.O = scr.take([NT, D])
                self.ST = [scr.take([2, 8, 104], BF16) for _ in range(3)]
                self.R = [scr.take([2, 8, 16]) for _ in range(3)]
                self.A = [scr.take([2, 8, 16]) for _ in range(3)]
                self.Oc = scr.take([512])
                self.Mst = scr.take([4, 4, 32], BF16)
                self.m2 = scr.take([4, 4, 2])
                self.nm = scr.take([4, 4])
                self.ri = scr.take([4, 4, 1])
                for v in self.vE:
                    fill(gp, v, 0.0)
                for v in self.ST:
                    fill(gp, v, 0.0)
                fill(gp, self.Mst, 0.0)
                g = gp.now
                full, part = KV // 128, KV % 128
                if part:
                    for v in self.P:
                        fill(gp, v, 0.0)
                for v in self.vh:
                    fill(gp, v[:, 0:full, :, 16:17], 1.0, [g])
                    if part:
                        fill(gp, v[0:part, full, :, 16:17], 1.0, [g])
                for v in self.ST:
                    fill(gp, v[:, 1, :, QH:QM], 1.0, [g])
                self.ready0 = gp.now
                self.st_free = [[], [], []]
                self.r_free = [[], [], []]
                self.banks = [0, 1, 2, 3, 4, 5, 7]
                self.n_bank = 0
                self.seg_free = [[], []]
                self.seg_ready = [[], []]
                self.p_free = [[] for _ in range(depth)]
                self.n_prep = 0

            def prep(self, s):
                b, hh, par = s // 2, s % 2, s % 2
                self.seg_ready[par] = []
                if self.KV == S:
                    work = [(t, 128, True, True) for t in range(8)]
                else:
                    work = [(t, 128 if t == 0 else 26, False, True) for t in range(2)]
                    work += [(t, 128, True, False) for t in range(8)]
                splits, turns = [], []
                for t, rows, hq, hk in work:
                    st = {}
                    splits.append(lambda t=t, rows=rows, hq=hq, hk=hk, st=st: self.split(b, hh, par, t, rows, hq, hk, st))
                    turns.append([lambda t=t, rows=rows, st=st, z=z: self.turn(par, t, rows, z, st)
                                  for z, on in ((0, hq), (1, hk)) if on])
                pieces = splits[0:2]
                for k in range(len(work)):
                    pieces += splits[k + 2:k + 3] + turns[k]
                return pieces

            def bank(self):
                self.n_bank += 1
                return self.banks[self.n_bank % len(self.banks)]

            def split(self, b, hh, par, t, rows, hq, hk, st):
                bank = self.bank()
                x = self.n_prep % 3
                self.n_prep += 1
                st["x"] = x
                ps = PS[0:rows, bank, :]
                tok = self.qkv(b, hh, t, rows, hq, hk, ps, pf[bank])
                lo, hi = (0 if hq else 1), (2 if hk else 1)
                ST, R, a = self.ST[x], self.R[x], self.A[x]
                rd = []
                w = [tok] + self.st_free[x] + self.r_free[x]
                if self.bias is not None:
                    bs = self.bias[0:rows, hh]
                    if hk:
                        rd.append(tt(dv, self.vh[par][0:rows, t, :, 0:16], ps[:, 256:384].rearrange("p (h d) -> p h d", h=8),
                                     bs[:, 256:384].rearrange("p (h d) -> p h d", h=8), ALU.add, [tok] + self.seg_free[par]))
                        self.seg_ready[par].append(rd[-1])
                    ta = tt(dv, a[0:rows, lo:hi], ps[:, 128 * lo:128 * hi].rearrange("p (z h d) -> p z h d", h=8, d=16),
                            bs[:, 128 * lo:128 * hi].rearrange("p (z h d) -> p z h d", h=8, d=16), ALU.add, w)
                    rd.append(ta)
                elif hk:
                    rd.append(act(self.vh[par][0:rows, t, :, 0:16], ps[:, 256:384].rearrange("p (h d) -> p h d", h=8),
                                  ACT.Copy, [tok] + self.seg_free[par]))
                    self.seg_ready[par].append(rd[-1])
                if self.post is not None:
                    dv.after(rd)
                    ta, more = self.post(b, hh, t, ps, w, a)
                    rd += more
                elif self.bias is None:
                    ta = act(a[0:rows, lo:hi], ps[:, 128 * lo:128 * hi].rearrange("p (z h d) -> p z h d", h=8, d=16), ACT.Copy, w,
                             scale=self.mask[2][:, 8 * b + t:8 * b + t + 1] if self.mask is not None and hq else None)
                    rd.append(ta)
                pf[bank] = rd

                def slots(z, js):
                    v = ST[0:rows, z, :, 0:96].rearrange("p h (j d) -> p h j d", d=16)
                    if len(js) == 1:
                        return v[:, :, js[0], :]
                    step = js[1] - js[0]
                    return v[:, :, js[0]:js[-1] + 1:step, :]

                def dup(v, n):
                    return bc(v[0:rows].unsqueeze(2), [rows, 8, n, 16])
                done = []
                w = [ta] + self.st_free[x]
                if hq:
                    done.append(act(slots(0, [0, 1, 2]), dup(a[:, 0], 3), ACT.Copy, w))
                if hk:
                    done.append(act(slots(1, [0, 3]), dup(a[:, 1], 2), ACT.Copy, w))
                    done.append(act(slots(1, [5]), a[0:rows, 1], ACT.Copy, w))
                first = ST[0:rows, lo:hi, :, 0:16]
                t1 = tt(dv, R[0:rows, lo:hi], a[0:rows, lo:hi], first, ALU.subtract, done + self.r_free[x])
                if hq:
                    t2 = cp(gp, slots(0, [3, 4]), dup(R[:, 0], 2), [t1])
                if hk:
                    t2 = cp(gp, slots(1, [1, 4]), dup(R[:, 1], 2), [t1])
                done.append(t2)
                if hq:
                    done.append(tt(gp, slots(0, [5]), R[0:rows, 0], slots(0, [3]), ALU.subtract, [t2]))
                if hk:
                    done.append(tt(gp, slots(1, [2]), R[0:rows, 1], slots(1, [1]), ALU.subtract, [t2]))
                self.r_free[x] = [gp.now]
                st["done"] = done
                self.st_free[x] = []

            def turn(self, par, t, rows, z, st):
                bank = self.bank()
                x = st["x"]
                pb = PS[:, bank, :].bitcast(BF16).rearrange("p (h n) -> p h n", h=8)
                for h in range(8):
                    tok = tr(pb[0:104, h, 0:rows], self.ST[x][0:rows, z, h, :], identb[0:rows, 0:rows],
                             st["done"] + pf[bank], inc=(h == 7))
                self.st_free[x] = self.st_free[x] + [tok]
                dst = (self.qS if z == 0 else self.kS)[par]
                e = cp(evac_lane(), dst[0:QM, :, 128 * t:128 * t + rows], pb[0:QM, :, 0:rows],
                       [tok] + self.seg_free[par])
                pf[bank] = [e]
                self.seg_ready[par].append(e)

            def max_pieces(self, s, g, qb, u):
                par = s % 2
                qS, kS = self.qS[par], self.kS[par]
                b = s // 2
                pieces = []
                KV = self.KV
                st = {}
                if KV == S:
                    nh = (qb + 1) if self.causal else 2
                    for qt in range(4):
                        for j in range(4):
                            def piece(qt=qt, j=j):
                                h = 4 * g + j
                                q0 = 512 * qb + 128 * qt
                                for half in range(nh):
                                    bank = self.bank()
                                    n = 512
                                    diag = False
                                    if self.causal and half == nh - 1:
                                        n = 128 * (qt + 1)
                                        diag = True
                                    o = PS[:, bank, 0:n]
                                    tok = mm(o, qS[0:QH, h, q0:q0 + 128], kS[0:QH, h, 512 * half:512 * half + n],
                                             True, not diag, pf[bank] + self.seg_ready[par], inc=not diag)
                                    if diag:
                                        tok = mm(PS[:, bank, n - 128:n], identb, maskS, False, True, (), inc=True)
                                    e = red(self.m2[:, qt, j, half:half + 1], o, ALU.max, [tok] + st.get("w", []))
                                    pf[bank] = [e]
                            pieces.append(piece)
                else:
                    nh = 1
                    for qt in range(4):
                        for jj in range(2):
                            def piece(qt=qt, jj=jj):
                                bank = self.bank()
                                q0 = 512 * qb + 128 * qt
                                for k in range(2):
                                    h = 4 * g + 2 * jj + k
                                    o = PS[:, bank, KC * k:KC * k + KC]
                                    last = self.mask is None
                                    tok = mm(o, qS[0:QH, h, q0:q0 + 128], kS[0:QH, h, 0:KC],
                                             True, last, pf[bank] + self.seg_ready[par], inc=(last and k == 1))
                                    if not last:
                                        tok = mm(o, identb, self.mask[0][:, 8 * b + 4 * qb + qt, :], False, True, inc=(k == 1))
                                v = PS[:, bank, 0:2 * KC].rearrange("p (k n) -> p k n", k=2)
                                e = red(self.m2[:, qt, 2 * jj:2 * jj + 2, 0], v, ALU.max, [tok])
                                pf[bank] = [e]
                            pieces.append(piece)

                def fin1():
                    t = dv.now
                    if nh == 2:
                        t = red(self.nm, self.m2, ALU.max, [t], neg=True)
                    else:
                        t = ts(dv, self.nm, self.m2[:, :, :, 0], -1.0, None, ALU.mult, None, [t])
                    t = cp(dv, self.Mst[:, :, :, 0], self.nm, [t] + st_m["free"])
                    t = tt(dv, self.Mst[:, :, :, 1], self.nm, self.Mst[:, :, :, 0], ALU.subtract, [t])
                    st["m"] = t

                def fin2():
                    bank = self.bank()
                    pb = PS[:, bank, :].bitcast(BF16)
                    for qt in range(4):
                        tok = tr(pb[:, 128 * qt:128 * qt + 128], self.Mst[:, qt].rearrange("p j r -> p (j r)"), identb,
                                 [st["m"]] + pf[bank], inc=(qt == 3))
                    st_m["free"] = [tok]
                    es = []
                    for j in range(4):
                        es.append(cp(dv, qS[QH:QM, 4 * g + j, 512 * qb:512 * qb + 512], pb[32 * j:32 * j + 2, 0:512],
                                     [tok] + self.seg_ready[par]))
                    pf[bank] = es
                    self.m_ready[u] = es
                st_m = self.st_m
                pieces.append(fin1)
                pieces.append(fin2)
                return pieces

            def exp_unit(self, s, g, qb, u, side):
                par, b, hh = s % 2, s // 2, s % 2
                qS, kS, vE = self.qS[par], self.kS[par], self.vE[par]
                nk = 4 * (qb + 1) if self.causal else self.nk
                q0 = 512 * qb
                steps = [(t, jj) for t in range(nk) for jj in range(2)]
                pend = []
                mw = self.m_ready[u]

                def pv(item):
                    t, jj, rows, lo, par2, tok = item
                    for k in range(2):
                        j = 2 * jj + k
                        x = mm(PS[32 * j:32 * j + 32, 6, lo:512], vE[:, t, 17 * (4 * g + j):17 * (4 * g + j) + 32],
                               self.P[par2][:, k, lo:512], t == 0, t == nk - 1, [tok] + (pf[6] if t == 0 else []),
                               inc=(k == 1), tile=(0, 32 * j))
                    self.p_free[par2] = [x]
                    return x
                for n, (t, jj) in enumerate(steps):
                    rows = min(128, self.KV - 128 * t)
                    lo = 0
                    diag = self.causal and t >= 4 * qb
                    if diag:
                        lo = 128 * (t - 4 * qb)
                    pr = n % self.depth
                    for k in range(2):
                        h = 4 * g + 2 * jj + k
                        bank = (2 * n + k) % 3
                        tok = mm(PS[0:rows, bank, lo:512], kS[0:QM, h, 128 * t:128 * t + rows], qS[0:QM, h, q0 + lo:q0 + 512],
                                 True, not diag and self.mask is None, pf[bank] + mw, inc=(not diag and self.mask is None))
                        if self.mask is not None:
                            tok = mm(PS[0:rows, bank, :], identb[0:rows, 0:rows], self.mask[1][0:rows, t, b * S + q0:b * S + q0 + 512],
                                     False, True, inc=True)
                        if diag:
                            tok = mm(PS[0:rows, bank, lo:lo + 128], identb, maskT, False, True, (), inc=True)
                        e = act(self.P[pr][0:rows, k, lo:512], PS[0:rows, bank, lo:512], ACT.Exp, [tok] + self.p_free[pr], scale=0.25)
                        pf[bank] = [e]
                    side()
                    if len(pend) == self.depth - 1:
                        pv(pend.pop(0))
                    pend.append((t, jj, rows, lo, pr, e))
                    side()
                for item in pend:
                    last = pv(item)
                w = cp(ac, self.Oc, PS[:, 6, :], [last] + self.oc_free)
                pf[6] = [w]

                def finish():
                    bank = self.bank()
                    for qt in range(4):
                        tok = tr(PS[:, bank, 128 * qt:128 * qt + 128], self.Oc[:, 128 * qt:128 * qt + 128], ident,
                                 [w] + pf[bank], inc=(qt == 3))
                    self.oc_free = [tok]
                    pv4 = PS[:, bank, :].rearrange("p (t j d) -> p t j d", t=4, j=4)
                    r = recip(self.ri, pv4[:, :, :, 16:17], [tok, dv.now])
                    i0 = 8 * b + 4 * qb
                    c0 = 128 * hh + 64 * g
                    o = self.O[:, i0:i0 + 4, c0:c0 + 64].rearrange("p t (j d) -> p t j d", j=4)
                    e = tt(dv, o, pv4[:, :, :, 0:16], bc(self.ri, [128, 4, 4, 16]), ALU.mult, [r])
                    pf[bank] = [e]
                return finish

            def run(self):
                self.m_ready = {}
                self.st_m = {"free": []}
                self.oc_free = []
                if self.causal:
                    units = [(s, g, qb) for s in range(4) for qb in range(2) for g in range(2)]
                    share = (0.2, 0.05, 1.0)
                else:
                    units = [(s, g, qb) for s in range(4) for g in range(2) for qb in range(2)]
                    share = (1 / 3, 1 / 2, 1.0)
                for q in (ac, dv, pe):
                    q.after([self.ready0])
                for p in self.prep(0) + self.max_pieces(*units[0], 0):
                    p()
                self.banks = [3, 4, 5, 7]
                pre = []
                fin = None
                users = {0: [], 1: []}
                for u, (s, g, qb) in enumerate(units):
                    if u % 4 == 0 and s + 1 < 4:
                        self.seg_free[(s + 1) % 2] = users[(s + 1) % 2]
                        pre = self.prep(s + 1)
                    nxt = []
                    if u + 1 < len(units):
                        k = -int(-len(pre) * share[min(u % 4, 2)] // 1)
                        own, pre = pre[:k], pre[k:]
                        mx = self.max_pieces(*units[u + 1], u + 1)
                        body, (fin1, fin2) = mx[:-2], mx[-2:]
                        tail = own[max(0, k - 3):]
                        own = own[:max(0, k - 3)]
                        tot = len(body) + len(own)
                        bi = oi = 0
                        for z in range(tot):
                            if oi < len(own) and (oi * tot <= z * len(own) or bi == len(body)):
                                nxt.append(own[oi])
                                oi += 1
                            else:
                                nxt.append(body[bi])
                                bi += 1
                        nxt += [fin1] + (tail or [None, None]) + [fin2]
                    if fin is not None:
                        nxt = nxt[:1] + [fin] + nxt[1:]
                    nk = 4 * (qb + 1) if self.causal else self.nk
                    calls = 4 * nk - 1
                    at = [0, 0]

                    def side(nxt=nxt, at=at, calls=calls):
                        at[1] += 1
                        while at[0] < min(len(nxt), -(-at[1] * len(nxt) // calls)):
                            if nxt[at[0]] is not None:
                                nxt[at[0]]()
                            at[0] += 1
                    fin = self.exp_unit(s, g, qb, u, side)
                    users[s % 2] = [pe.now]
                fin()

        def out_proj(att, wo, bias, dst, wtok):
            barrier()
            pe.after([wtok])
            project_T(att.O, wo, bias, dst)

        def project_T(O, wo, bias, dst):
            ready = {}

            def turn(k):
                ready[k] = []
                for c in range(2):
                    bk = (2 * k + c) % 4
                    for j in range(4):
                        t = tr(PS[:, bk, 128 * j:128 * j + 128], O[:, 4 * k + j, 128 * c:128 * c + 128], ident, pf[bk], inc=(j == 3))
                    t = cp(ac, XNT[:, c, 512 * k:512 * k + 512], PS[:, bk, :], [t])
                    pf[bk] = [t]
                    ready[k].append(t)
            turn(0)
            for k in range(4):
                if k + 1 < 4:
                    turn(k + 1)
                add_proj(dst, lambda c, i: XNT[:, c, 128 * i:128 * i + 128], 2, wo, bias, tiles=range(4 * k, 4 * k + 4),
                         w=ready[k], banks=(4 + 2 * (k % 2), 5 + 2 * (k % 2)))

        def add_bias(dst, bias):
            for k in range(4):
                v = dst[:, 4 * k:4 * k + 4, :]
                tt(gp, v, v, bc(bias.unsqueeze(1), [128, 4, D]), ALU.add)

        def plain_qkv(wq, wtok):
            def f(b, hh, t, rows, hq, hk, ps, w):
                pe.after([wtok])
                r0 = b * S + 128 * t
                tok = None
                if hq and hk:
                    src, lo, hi = (lambda c: XNT[:, c, r0:r0 + 128]), 0, 384
                elif hq:
                    src, lo, hi = (lambda c: XNT[:, c, r0:r0 + 128]), 0, 128
                else:
                    k0 = KC * b + 128 * t
                    src, lo, hi = (lambda c: ctxT[:, c, k0:k0 + rows]), 128, 384
                for c in range(2):
                    tok = mm(ps[:, lo:hi], src(c), wq(c, hh, lo, hi), c == 0, c == 1, w, inc=(c == 1))
                return tok
            return f

        def w_seg(wap):
            v = wap.rearrange("p (c s n) -> p c s n", c=2, s=2)
            return lambda c, hh, lo, hi: v[:, c, hh, lo:hi]

        def w_rows(wap, n=256):
            v = wap.rearrange("p (c n) -> p c n", n=n)
            return lambda c: v[:, c, :]

        W = {}

        def load_0():
            WB[0].clear()
            W[0] = load_w(WB[0], "pk0")

        def phase_0():
            w, wt = W[0]
            dkv = w[:, 0:128].rearrange("p (c n) -> p c n", c=2)
            ukv = w[:, 128:640].rearrange("p (s n) -> p s n", s=2)
            uq = w[:, 640:1152].rearrange("p (c n) -> p c n", c=2)
            wo = w_rows(w[:, 1152:1664])
            ckv = scr.take([2048])
            fill(dv, ckv[64:128], 0.0)

            def qkv(b, hh, t, rows, hq, hk, ps, w):
                r0 = b * S + 128 * t
                for c in range(2):
                    mm(ps[:, 0:128], XNT[:, c, r0:r0 + 128], uq[:, c, 128 * hh:128 * hh + 128], c == 0, c == 1, w)
                return mm(ps[:, 128:384], ckv[:, r0:r0 + 128], ukv[:, hh, :], True, True, (), inc=True)
            att = Attention(S, True, qkv, depth=2)
            layer_norm_T(keep=att.O)
            pe.after([wt])
            for k in range(4):
                for c in range(2):
                    t = mm(PS[0:64, k, :], dkv[:, c, :], XNT[:, c, 512 * k:512 * k + 512], c == 0, c == 1, pf[k], inc=(c == 1))
                t = cp(evac_lane(), ckv[0:64, 512 * k:512 * k + 512], PS[0:64, k, :], [t])
                pf[k] = [t]
            barrier()
            att.run()
            out_proj(att, wo, None, X, wt)

        def load_1():
            WA.clear()
            WB[1].clear()
            W[1] = [load_w(WA, "pk1"), load_w(WB[1], "pk1o")]

        def phase_1():
            (wa, ta), (wb, tb) = W[1]
            wq = wa[:, 0:2048].rearrange("p (c n) -> p c n", c=2)
            wk = wa[:, 2048:4096].rearrange("p (c n) -> p c n", c=2)
            wv = wa[:, 4096:6144].rearrange("p (c n) -> p c n", c=2)
            g = wa[:, 6144:6152].rearrange("p (z c) -> p z c", z=4)
            wo = wb[:, 0:2048].rearrange("p (k n) -> p k n", k=8)
            for q in lanes:
                q.after([ta, tb])
            KV = S + KC
            KR = 97
            upper_part["now"] = SC1
            scr.at = LOW + RRW
            at = [0]

            def rr(n):
                at[0] += n
                return RR[:, at[0] - n:at[0]]
            qB = [rr(S) for _ in range(4)]
            kB = [rr(KV) for _ in range(4)]
            qL = [rr(S) for _ in range(4)]
            kL = [rr(KV) for _ in range(4)]

            def put(o, value, p0, p1, w, q=gp):
                if q is ac:
                    return act(o, bc(ones[p0:p1, 0:1], [p1 - p0, o.shape[1]]), ACT.Copy, w, scale=value)
                return ts(gp, o, bc(ones[p0:p1, 0:1], [p1 - p0, o.shape[1]]), value, None, ALU.mult, None, w)
            hl_at = scr.at
            hl = [scr.take([2, 512]) for _ in range(2)]
            ct = view(hl_at, [4, D])
            for y in range(4):
                for v, w_ in ((qB, 0.0), (kB, 1.0)):
                    put(v[y][64:128], w_, 64, 128, [[gp, ac][y % 2].now], [gp, ac][y % 2])
            for y in range(4):
                for v, w_ in ((qB, 1.0), (kB, 0.0)):
                    put(v[y][96:97], w_, 96, 97, [[gp, ac][y % 2].now], [gp, ac][y % 2])
            layer_norm_T(mul=lambda c: g[:, 0, c:c + 1], add=lambda c: g[:, 1, c:c + 1], twice=True)
            fT = scr.take([2, 308])
            mk = scr.take([308])
            lm = Load("d_mask")
            mk8 = scr.take([308 // 4 + 1])
            m8 = mk8.bitcast(U8)[0:1, 0:308]
            sp.after([fill(gp, ct, 0.0, [gp.now])])
            lm.add(m8, ins["mask8"])
            for b in range(2):
                lm.add(ct[:, 2 * b, :], ins["ctx"][b, 0:128, :])
                lm.add(ct[0:26, 2 * b + 1, :], ins["ctx"][b, 128:154, :])
            dv.after([lm.ready])
            ts(dv, mk[0:1, 0:308], m8, -1.0, -NEG, ALU.add, ALU.mult)
            mv, rs = stats(lambda i: ct[:, i, :], 4, scr, 1e-5)
            for b in range(2):
                for z in range(2):
                    rows = 128 if z == 0 else 26
                    i = 2 * b + z
                    t = normalise(ct[:, i, :], ct[:, i, :], mv, rs, i)
                    for c in range(2):
                        p = tr(PS[:, i, 128 * c:128 * c + rows], ct[0:rows, i, 128 * c:128 * c + 128], ident[0:rows, 0:rows],
                               [t] + pf[i], inc=(c == 1))
                    for c in range(2):
                        t = act(fT[:, c, KC * b + 128 * z:KC * b + 128 * z + rows], PS[:, i, 128 * c:128 * c + rows], ACT.Identity, [p],
                                scale=g[:, 2, c:c + 1], bias=g[:, 3, c:c + 1])
                    pf[i] = [t]
            vE = scr.take([10, 8, 65])
            P = [scr.take([2, 512]) for _ in range(2)]
            O = scr.take([8, 512])
            OT = P[0].rearrange("p a (b n) -> p a b n", b=4)
            Mst = scr.take([8, 65])
            m2 = scr.take([8, 3])
            nm = scr.take([8])
            WB[0].clear()
            Oc = WB[0].take([512])
            ri = scr.take([4, 1])
            fill(gp, vE[:, 9], 0.0, [gp.now])
            fill(gp, vE[:, 0:9, :, 64:65], 1.0, [gp.now])
            fill(gp, vE[0:26, 9, :, 64:65], 1.0, [gp.now])
            fill(gp, Mst, 0.0, [gp.now])
            barrier()

            def kvsrc(b, t, c):
                if t < 8:
                    return XNT[:, c, b * S + 128 * t:b * S + 128 * t + 128]
                lo = KC * b + 128 * (t - 8)
                return fT[:, c, lo:lo + (128 if t == 8 else 26)]
            kvrows = [128] * 9 + [26]
            st = {"p": [[], []], "oc": [], "free": [[], [], [], []], "mst": [], "o_free": [], "slot": 0, "hl": [[], []], "n": 0}

            def proj(b, j, hds, engines=None):
                pcs = []
                ys = [2 * (j % 2), 2 * (j % 2) + 1]
                for hd in hds:
                    hd["q"] = [[], []]
                    hd["k"] = [[], [], []]
                for z, k in ((0, 0), (1, 0), (1, 1), (1, 2), (0, 1)):
                    def piece(z=z, k=k):
                        n = 512 if k < 2 else KC
                        for c in range(2):
                            src = XNT[:, c, b * S + 512 * k:b * S + 512 * k + 512] if k < 2 else fT[:, c, KC * b:KC * b + KC]
                            tok = mm(PS[:, 7, 0:n], (wk if z else wq)[:, c, 128 * j:128 * j + 128], src, c == 0, c == 1, pf[7], inc=(c == 1))
                        x = st["n"] % 2
                        st["n"] += 1
                        s_ = slice(512 * k, 512 * k + n)
                        ps = PS[:, 7, 0:n]
                        ta = high(hl[x][:, 0, 0:n], ps, [tok] + st["hl"][x])
                        tb = tt(dv, hl[x][:, 1, 0:n], ps, hl[x][:, 0, 0:n], ALU.subtract, [ta])
                        pf[7] = [tb]
                        used = []
                        for i in range(2):
                            y = ys[i]
                            h_, l_ = [hl[x][64 * i:64 * i + 64, e, 0:n] for e in range(2)]
                            up, lo = (l_, h_) if z else (h_, l_)
                            L = (kL if z else qL)[y]
                            w_ = [cp(ac, (kB if z else qB)[y][0:64, s_], h_, [ta] + st["free"][y])]
                            if not z and st["free"][y]:
                                w_.append(put(qB[y][64:65, s_], 0.0, 64, 65, st["free"][y] + [gp.now]))
                            for o, v, q in ((L[0:64, s_], up, 0), (L[64:128, s_], lo, 1)):
                                q = engines[2 * i + q] if engines else gp
                                w_.append(cp(q, o, v, [tb] + ([gp.now] if q is gp else []) + st["free"][y]))
                            used += w_
                            if z == 1 and k == 2 and j < 2:
                                w_.append(cp(dv, kB[y][96:97, s_], mk[0:1, KC * b:KC * b + KC], st["free"][y]))
                            hds[i]["k" if z else "q"][k] = w_
                        st["hl"][x] = used
                    pcs.append(piece)
                return pcs

            def maxes(y, hd):
                pcs = []
                last_mx = [None]
                for qt in range(8):
                    for k in range(3):
                        def mx(qt=qt, k=k):
                            n = 512 if k < 2 else KC
                            bank = 3 + st["slot"] % 3
                            st["slot"] += 1
                            tok = mm(PS[:, bank, 0:n], qB[y][0:KR, 128 * qt:128 * qt + 128], kB[y][0:KR, 512 * k:512 * k + n],
                                     True, True, pf[bank] + hd["q"][qt // 4] + hd["k"][k], inc=True)
                            last_mx[0] = tok
                            e = red(m2[:, qt, k:k + 1], PS[:, bank, 0:n], ALU.max, [tok] + st["mst"])
                            pf[bank] = [e]
                        pcs.append(mx)

                def fin1():
                    t = red(nm, m2, ALU.max, [dv.now], neg=True)
                    hd["m"] = cp(dv, Mst[:, :, 64], nm, [t] + st["mst"])
                pcs.append(fin1)
                es = []
                for k in range(2):
                    def fin2(k=k):
                        for j in range(4):
                            tok = tr(PS[0:65, 7, 128 * j:128 * j + 128], Mst[:, 4 * k + j, :], ident, [hd["m"]] + pf[7], inc=(j == 3))
                        e = cp(dv, qB[y][64:65, 512 * k:512 * k + 512], PS[64:65, 7, :], [tok, last_mx[0]])
                        pf[7] = [e]
                        st["mst"] = [tok]
                        es.append(e)
                        hd["rdy"] = es + [x for v in hd["q"] + hd["k"] for x in v]
                    pcs.append(fin2)
                return pcs

            def v_half(b, hh, w):
                for t in range(10):
                    bank = 4 + t % 3
                    rows = kvrows[t]
                    for c in range(2):
                        tok = mm(PS[0:rows, bank, :], kvsrc(b, t, c), wv[:, c, 512 * hh:512 * hh + 512], c == 0, c == 1,
                                 pf[bank], inc=(c == 1))
                    e = cp(evac_lane(), vE[0:rows, t, :, 0:64], PS[0:rows, bank, :].rearrange("p (h d) -> p h d", h=8), [tok] + w)
                    pf[bank] = [e]
                    v_rdy.append(e)
            v_rdy = []

            def exp_head(h, y, hd, side):
                hl = h % 8
                steps = [(qb, pr) for qb in range(2) for pr in range(5)]
                pend = []
                late = []

                def pv():
                    qb, pr, px, toks = pend.pop(0)
                    for k in range(2):
                        t = 2 * pr + k
                        tok = mm(PS[0:65, 6, :], vE[:, t, hl, :], P[px][:, k, :], t == 0, t == 9,
                                 toks + v_rdy + (pf[6] if t == 0 else []), inc=(k == 1))
                    st["p"][px] = [tok]
                    if pr == 4:
                        w = cp(ac, Oc[0:65, :], PS[0:65, 6, :], [tok] + st["oc"])
                        pf[6] = [w]

                        def finish():
                            for j in range(4):
                                tok = tr(PS[:, 7, 128 * j:128 * j + 65], Oc[0:65, 128 * j:128 * j + 128], ident[0:65, 0:65],
                                         [w] + pf[7], inc=(j == 3))
                            st["oc"] = [tok]
                            v4 = PS[:, 7, :].rearrange("p (t d) -> p t d", t=4)
                            r = recip(ri, v4[:, :, 64:65], [tok, dv.now])
                            e = tt(dv, O[:, 4 * qb:4 * qb + 4, 64 * hl:64 * hl + 64], v4[:, :, 0:64], bc(ri, [128, 4, 64]),
                                   ALU.mult, [r] + st["o_free"])
                            pf[7] = [e]
                        late.append(finish)
                for n, (qb, pr) in enumerate(steps):
                    px = n % 2
                    for k in range(2):
                        t = 2 * pr + k
                        rows = kvrows[t]
                        bank = (2 * n + k) % 3
                        mm(PS[0:rows, bank, :], kB[y][0:KR, 128 * t:128 * t + rows],
                           qB[y][0:KR, 512 * qb:512 * qb + 512], True, False, pf[bank] + hd["rdy"])
                        tok = mm(PS[0:rows, bank, :], kL[y][:, 128 * t:128 * t + rows],
                                 qL[y][:, 512 * qb:512 * qb + 512], False, True, inc=True)
                        e = [act(P[px][0:rows, k, :], PS[0:rows, bank, :], ACT.Exp, [tok] + st["p"][px], scale=0.125)]
                        pf[bank] = e
                    side(2 * n, 2 * len(steps))
                    if pend:
                        pv()
                    pend.append((qb, pr, px, e))
                    side(2 * n + 1, 2 * len(steps))
                    if late and pr == 1:
                        late.pop()()
                st["free"][y] = [pe.now]
                pv()
                return late.pop()

            order = [(b, h) for b in range(2) for h in range(16)]
            hds = [{} for _ in order]
            for p in proj(0, 0, hds[0:2], (dv, ac, dv, gp)) + maxes(0, hds[0]):
                p()
            fin = None
            for n, (b, h) in enumerate(order):
                hh = h // 8
                if h % 8 == 0:
                    v_rdy.clear()
                    v_half(b, hh, [pe.now])
                nxt = []
                if h % 2 == 0 and n + 2 < len(order):
                    nxt += proj(order[n + 2][0], order[n + 2][1] // 2, hds[n + 2:n + 4])
                if n + 1 < len(order):
                    mx = maxes((n + 1) % 4, hds[n + 1])
                    body = []
                    for z, p in enumerate(mx[:-3]):
                        if z % 5 == 2 and nxt:
                            body.append(nxt.pop(0))
                        body.append(p)
                    nxt = body + nxt + mx[-3:]
                if fin is not None:
                    nxt = nxt[:2] + [fin] + nxt[2:]
                at = [0]

                def side(i, of, nxt=nxt, at=at):
                    while at[0] < min(len(nxt), -(-(i + 1) * len(nxt) // (of - 1))):
                        nxt[at[0]]()
                        at[0] += 1
                fin = exp_head(h, n % 4, hds[n], side)
                if h % 8 == 7:
                    fin()
                    fin = None
                    ot_free = [[pe.now], [pe.now]]
                    odone = dv.now
                    ev = {}
                    for i in range(9):
                        if i < 8:
                            x = i % 2
                            for c in range(4):
                                tok = tr(PS[:, 4 + x, 128 * c:128 * c + 128], O[:, i, 128 * c:128 * c + 128], ident,
                                         pf[4 + x] + [odone], inc=(c == 3))
                            e = cp(ac, OT[:, x], PS[:, 4 + x, :].rearrange("p (c n) -> p c n", c=4), [tok] + ot_free[x])
                            pf[4 + x] = [e]
                            ev[i] = e
                        if i > 0:
                            k = i - 1
                            bk = 6 + k % 2
                            for c in range(4):
                                tok = mm(PS[:, bk, 0:256], OT[:, k % 2, c, :], wo[:, 4 * hh + c, :], c == 0, c == 3, pf[bk] + [ev[k]], inc=(c == 3))
                            ot_free[k % 2] = [tok]
                            xv = X[:, 8 * b + k, :]
                            e = tt(dv, xv, PS[:, bk, 0:256], xv, ALU.add, [tok, dv.now])
                            pf[bk] = [e]
                    st["o_free"] = [pe.now]
                    st["p"][0] = [pe.now]
            upper_part["now"] = SC

        def softmax8(l, heap, w=()):
            mx = heap.take([NT])
            p = heap.take([NT, 8])
            s = heap.take([NT])
            r = heap.take([NT])
            t = red(mx, l, ALU.max, w)
            t = tt(dv, p, l, bc(mx.unsqueeze(2), [128, NT, 8]), ALU.subtract, [t])
            t = act(p, p, ACT.Exp, [t])
            t = red(s, p, ALU.add, [t])
            t = recip(r, s, [t])
            return p, r, t

        def first_max(l, heap, w=()):
            mx = heap.take([NT])
            sc = heap.take([NT, 8])
            oh = heap.take([NT, 8])
            t = red(mx, l, ALU.max, w)
            t = tt(dv, sc, l, bc(mx.unsqueeze(2), [128, NT, 8]), ALU.is_equal, [t])
            t = tt(dv, sc, sc, bc(rev.unsqueeze(1), [128, NT, 8]), ALU.mult, [t])
            t = red(mx, sc, ALU.max, [t])
            t = tt(dv, oh, sc, bc(mx.unsqueeze(2), [128, NT, 8]), ALU.is_equal, [t])
            return oh, t

        def logits8(wr, bias, heap):
            for i in range(NT):
                o = PS[:, 0, 8 * i:8 * i + 8]
                for c in range(2):
                    t = mm(o, XNT[:, c, 128 * i:128 * i + 128], wr(c), c == 0, c == 1 and bias is None, pf[0], inc=(i == NT - 1 and c == 1))
                if bias is not None:
                    t = mm(o, ones[0:1, 0:128], bias, False, True, (), inc=(i == NT - 1))
            l = heap.take([NT, 8])
            t = cp(dv, l, PS[:, 0, 0:128].rearrange("p (i e) -> p i e", e=8), [t])
            pf[0] = [t]
            return l, t

        def load_2():
            WA.clear()
            W[2] = load_w(WA, "pk2")

        def phase_2():
            w, wt = W[2]
            ew = w[:, 0:4096].rearrange("p (c e n) -> p c e n", c=2, e=8)
            rw = w[:, 4096:4112].rearrange("p (c n) -> p c n", c=2)
            rb = w[0:1, 4112:4120]
            lb = Load("d_eb")
            eb = scr.take([D], F32, 0, 8)
            lb.add(eb, ins["pk2e"])
            layer_norm_T()
            for q in lanes:
                q.after([wt, lb.ready])
            l, t = logits8(lambda c: rw[:, c, :], rb, scr)
            p, r, t = softmax8(l, scr, [t])
            t2 = tt(dv, p, p, bc(r.unsqueeze(2), [128, NT, 8]), ALU.mult, [t])
            oh, t = first_max(p, scr, [t2])
            G = scr.take([NT, 8])
            t = tt(dv, G, oh, p, ALU.mult, [t])
            GT = scr.take([2, 4, 128])
            gtf = [[], []]
            for k in range(4):
                for j in range(4):
                    p = tr(PS[0:8, k % 2, 128 * j:128 * j + 128], G[:, 4 * k + j, :], ident, [t] + pf[k % 2], inc=(j == 3))
                e = cp(ac, GT[0:8, k % 2], PS[0:8, k % 2, :].rearrange("p (j n) -> p j n", j=4), [p] + gtf[k % 2])
                pf[k % 2] = [e]
                for j in range(4):
                    bk = 2 + 2 * (k % 2) + j // 2
                    p = mm(PS[:, bk, 256 * (j % 2):256 * (j % 2) + 256], GT[0:8, k % 2, j, :], eb[0:8, :], True, True, [e] + pf[bk], inc=(j % 2 == 1))
                    if j % 2 == 1:
                        v = X[:, 4 * k + j - 1:4 * k + j + 1, :]
                        pf[bk] = [tt(dv, v, v, PS[:, bk, :].rearrange("p (j n) -> p j n", j=2), ALU.add, [p])]
                gtf[k % 2] = [p]
            last = dv.now
            n = 0
            for i in range(NT):
                for e2 in range(4):
                    b = n % 8
                    n += 1
                    for c in range(2):
                        t = mm(PS[:, b, :], XNT[:, c, 128 * i:128 * i + 128], ew[:, c, 2 * e2:2 * e2 + 2, :].rearrange("p e n -> p (e n)"),
                               c == 0, c == 1, pf[b], inc=(c == 1))
                    for k in range(2):
                        t2 = stt(X[:, i, :], PS[:, b, 256 * k:256 * k + 256], G[:, i, 2 * e2 + k:2 * e2 + k + 1], X[:, i, :],
                                 ALU.mult, ALU.add, [t, last])
                        last = t2
                    pf[b] = [t2]

        def load_3():
            WB[0].clear()
            W[3] = load_w(WB[0], "pk3")

        def phase_3():
            w, wt = W[3]
            wqkv = w[:, 0:1536].rearrange("p (c n) -> p c n", c=2)
            wo = w_rows(w[:, 1536:2048])
            rows = scr.take([1024])
            lr = Load("d_pk3r")
            lr.add(rows, ins["pk3r"])
            layer_norm_T()
            gp.after([lr.ready])
            add_bias(X, rows[:, 768:1024])
            qk = [scr.take([2, 768]) for _ in range(2)]
            pr = [scr.take([2, 2, D]) for _ in range(2)]
            sc = [scr.take([2, 2, 16]) for _ in range(2)]
            mx = [scr.take([2, 16]) for _ in range(2)]
            O = scr.take([NT, D])
            ex = [scr.take([2, 2, 16]) for _ in range(2)]
            for q in lanes:
                q.after([wt, lr.ready])
            fr = [[], []]
            for i in range(8):
                x = i % 2
                ts_ = []
                for b in range(2):
                    for z in range(2):
                        bank = 4 * x + 2 * b + z
                        lo, hi = (0, 512) if z == 0 else (512, 768)
                        for c in range(2):
                            t = mm(PS[:, bank, 0:hi - lo], XNT[:, c, b * S + 128 * i:b * S + 128 * i + 128], wqkv[:, c, lo:hi], c == 0, c == 1, pf[bank], inc=(c == 1))
                        t = tt(dv, qk[x][:, b, lo:hi], PS[:, bank, 0:hi - lo], rows[:, lo:hi], ALU.add, [t] + fr[x])
                        pf[bank] = [t]
                Q, K, V = qk[x][:, :, 0:256], qk[x][:, :, 256:512], qk[x][:, :, 512:768]
                d0 = [t, dv.now]
                for r in range(2):
                    t = tt(dv, pr[x][:, r], bc(Q[:, r:r + 1, :], [128, 2, 256]), K, ALU.mult, d0)
                t = red(sc[x], pr[x].rearrange("p r c (h d) -> p (r c) h d", d=16), ALU.add, [t])
                t = tt(dv, mx[x], sc[x][:, :, 0, :], sc[x][:, :, 1, :], ALU.max, [t])
                t = tt(dv, sc[x], sc[x], bc(mx[x].unsqueeze(2), [128, 2, 2, 16]), ALU.subtract, [t])
                t = act(ex[x], sc[x], ACT.Exp, [t], scale=0.25)
                t = tt(dv, mx[x], ex[x][:, :, 0, :], ex[x][:, :, 1, :], ALU.add, [t])
                t = recip(mx[x], mx[x], [t])
                t = tt(dv, ex[x], ex[x], bc(mx[x].unsqueeze(2), [128, 2, 2, 16]), ALU.mult, [t])
                for r in range(2):
                    for c in range(2):
                        tt([dv, gp][r], pr[x][:, r, c].rearrange("p (h d) -> p h d", d=16),
                           V[:, c].rearrange("p (h d) -> p h d", d=16), bc(ex[x][:, r, c].unsqueeze(2), [128, 16, 16]), ALU.mult, [t])
                t2 = [dv.now, gp.now]
                for r in range(2):
                    t = tt(dv, O[:, 8 * r + i, :], pr[x][:, r, 0], pr[x][:, r, 1], ALU.add, t2)
                fr[x] = [t]
            barrier()
            project_T(O, wo, None, X)

        def load_4():
            WB[1].clear()
            W[4] = load_w(WB[1], "pk4")

        def phase_4():
            w, wt = W[4]
            wq = w_seg(w[:, 0:1536])
            wo = w_rows(w[:, 1536:2048])
            rows = scr.take([1024])
            lr = Load("d_pk4r")
            lr.add(rows, ins["pk4r"])
            att = Attention(KC, False, plain_qkv(wq, wt), bias=rows[:, 0:768].rearrange("p (s n) -> p s n", s=2), depth=2)
            layer_norm_T(keep=att.O)
            for q in (dv, gp):
                q.after([lr.ready])
            add_bias(X, rows[:, 768:1024])
            att.run()
            out_proj(att, wo, None, X, wt)

        def load_5():
            WA.clear()
            W[5] = load_w(WA, "pk5", dt=I32)

        def phase_5():
            wi, wt = W[5]
            wf = wi.bitcast(F32)
            for q in lanes:
                q.after([wt])
            for k in range(3):
                ts([dv, gp, dv][k], wf[:, 1536 * k:1536 * k + 1536], wi[:, 1536 * k:1536 * k + 1536], 1.0 / 127.0, None, ALU.mult, None)
            wg = wf[:, 0:1536].rearrange("p (c n) -> p c n", c=2)
            wu = wf[:, 1536:3072].rearrange("p (c n) -> p c n", c=2)
            wd = wf[:, 3072:4608].rearrange("p (f n) -> p f n", f=6)
            layer_norm_T()
            for q in lanes:
                q.after([gp.now])
            hT = [scr.take([6, 512]) for _ in range(2)]
            sg = [scr.take([512]) for _ in range(2)]
            swiglu(4, 6, lambda f, c: wg[:, c, 128 * f:128 * f + 128], lambda f, c: wu[:, c, 128 * f:128 * f + 128], hT, sg,
                   lambda f: wd[:, f, :], None, X)

        swi = {"n": 0, "sgf": [[], []], "hf": [[], []], "pend": None, "last": {}}

        def swiglu_down(item):
            hT, x, nf, wd, gate, dst, k, hr = item
            for i2 in range(2):
                b = 4 + (2 * k + i2) % 4
                for z in range(2):
                    i = 2 * i2 + z
                    for f in range(nf):
                        t = mm(PS[:, b, 256 * z:256 * z + 256], hT[x][:, f, 128 * i:128 * i + 128], wd(f), f == 0, f == nf - 1,
                               pf[b] + hr, inc=(f == nf - 1))
                i = 4 * k + 2 * i2
                if gate is None:
                    v = dst[:, i:i + 2, :]
                    e = tt(dv, v, PS[:, b, :].rearrange("p (k c) -> p k c", k=2), v, ALU.add, [t])
                else:
                    for z in range(2):
                        e = stt(dst[:, i + z, :], PS[:, b, 256 * z:256 * z + 256], gate(i + z), dst[:, i + z, :], ALU.mult, ALU.add,
                                [t] + swi["last"].get(i + z, []))
                        swi["last"][i + z] = [e]
                pf[b] = [e]
            swi["hf"][x] = [t]

        def swiglu(nblk, nf, wg, wu, hT, sg, wd, gate, dst, finish=True):
            for k in range(nblk):
                x = swi["n"] % 2
                swi["n"] += 1
                hr = []
                for f in range(nf):
                    y = f % 2
                    for z, w in ((0, wg), (1, wu)):
                        for c in range(2):
                            t = mm(PS[:, 2 * y + z, :], w(f, c), XNT[:, c, 512 * k:512 * k + 512], c == 0, c == 1, pf[2 * y + z], inc=(c == 1))
                        if z == 0:
                            a = act(sg[y], PS[:, 2 * y, :], ACT.Silu, [t] + swi["sgf"][y])
                            pf[2 * y] = [a]
                    e = tt(dv, hT[x][:, f, :], PS[:, 2 * y + 1, :], sg[y], ALU.mult, [t, a] + swi["hf"][x])
                    pf[2 * y + 1] = [e]
                    swi["sgf"][y] = [e]
                    hr.append(e)
                if swi["pend"] is not None:
                    swiglu_down(swi["pend"])
                swi["pend"] = (hT, x, nf, wd, gate, dst, k, hr)
            if finish:
                swiglu_down(swi["pend"])
                swi["pend"] = None

        def load_6():
            WB[0].clear()
            W[6] = [load_w(WB[0], "pk6b")]

        def phase_6():
            WA.clear()
            wa, ta = load_w(WA, "pk6")
            wb, tb = W[6][0]
            at = [0]

            def part(n):
                v = wa[:, at[0]:at[0] + n]
                at[0] += n
                return v
            inp = part(2048).rearrange("p (c n) -> p c n", c=2)
            xpw = part(256).rearrange("p (c n) -> p c n", c=4)
            opw = part(1024).rearrange("p (c n) -> p c n", c=4)
            fw1 = part(2048).rearrange("p (c n) -> p c n", c=2)
            dtw = part(512)
            cw = part(16).rearrange("p (c n) -> p c n", c=4)
            cb = part(4)
            dtb = part(4)
            alog = part(64).rearrange("p (c n) -> p c n", c=4)
            Dc = part(4)
            lg = part(2)
            lb = part(2)
            fb1 = part(8)
            fb2 = part(256)
            fw2 = wb.rearrange("p (c n) -> p c n", c=8)
            layer_norm_T()
            for q in lanes:
                q.after([ta, tb])
            u = scr.take([4, S])
            de = scr.take([4, S])
            du = scr.take([4, S])
            dbl_at = scr.at
            dbl = scr.take([S])
            MO = scr.take([NT, D])
            da_at = scr.at
            dA = [scr.take([4, 512]) for _ in range(2)]
            dB = [scr.take([4, 512]) for _ in range(2)]
            Cs = [scr.take([512]) for _ in range(3)]
            bcs = scr.take([S], BF16)
            eye3 = scr.take([32], BF16)
            h_at = scr.at
            h = [scr.take([4, 512]) for _ in range(2)]
            mx = view(h_at, [4, S])
            xp = [h[k].rearrange("p a b -> p (a b)")[:, 0:1027] for k in range(2)]
            hl = scr.take([16, 4])
            An = scr.take([4, 16])
            rbc = dB[1][:, 0, :]
            mid = dB[1][:, 1, 0:256].bitcast(BF16)
            for k in range(3):
                cp(dv, eye3[32 * k:32 * k + 32, :], ident[0:32, 0:32])
            zd = fill(dv, dbl, 0.0)
            t = act(An, alog, ACT.Exp)
            ts(dv, An, An, -1.0, None, ALU.mult, None, [t])
            barrier()

            def flipped_T(w):
                order = [7, 6, 5, 4, 3, 2, 1, 0, 15, 14, 13, 12, 11, 10, 9, 8]
                xn = view(da_at, [NT, D])
                done = normalised(xn, X, Heap(dbl_at, dbl_at + S), 1e-5)
                for k in range(4):
                    for c in range(2):
                        bank = 4 + (2 * k + c) % 4
                        for j in range(4):
                            i = order[4 * k + j]
                            t = mm(PS[:, bank, 128 * j:128 * j + 128], xn[:, i, 128 * c:128 * c + 128], anti, True, True, pf[bank] + [done[i]], inc=(j == 3))
                        t = cp(ac, XNT[:, c, 512 * k:512 * k + 512], PS[:, bank, :], [t] + w)
                        pf[bank] = [t]
                pe.after([t])

            def xz(b, chunk, half, bank):
                for c in range(2):
                    t = mm(PS[:, bank, :], inp[:, c, 128 * chunk:128 * chunk + 128],
                           XNT[:, c, b * S + 512 * half:b * S + 512 * half + 512], c == 0, c == 1, pf[bank], inc=(c == 1))
                return t

            def pre_a(sq, free):
                b = sq % 2
                z0 = [fill(dv, v[:, 0:3], 0.0, free) for v in xp]
                xpf = [free, free]
                silu = []
                for c in range(4):
                    x = c % 2
                    for half in range(2):
                        bank = 2 * x + half
                        t = xz(b, c, half, bank)
                        t = act(xp[x][:, 3 + 512 * half:515 + 512 * half], PS[:, bank, :], ACT.Copy, [t] + xpf[x])
                        pf[bank] = [t]
                    t = ts(dv, u[:, c, :], xp[x][:, 0:S], cw[:, c, 0:1], cb[:, c:c + 1], ALU.mult, ALU.add, [t] + z0)
                    for i in range(1, 4):
                        t = stt(u[:, c, :], xp[x][:, i:i + S], cw[:, c, i:i + 1], u[:, c, :], ALU.mult, ALU.add, [t])
                    xpf[x] = [t]
                    silu.append(t)
                return [act(u[:, c, :], u[:, c, :], ACT.Silu, [silu[c]]) for c in range(4)]

            def pre_b(sq, ready, free, between=None):
                for c in range(4):
                    for half in range(2):
                        p = mm(PS[0:64, 4 + half, :], xpw[:, c, :], u[:, c, 512 * half:512 * half + 512], c == 0, c == 3,
                               (pf[4 + half] if c == 0 else []) + [ready[c]], inc=(c == 3))
                n = 0
                ee = []
                for half in range(2):
                    s_ = slice(512 * half, 512 * half + 512)
                    e = cp(ac, dbl[0:16, s_], PS[0:16, 4 + half, :], [p] + free)
                    ee.append(e)
                for half in range(2):
                    s_ = slice(512 * half, 512 * half + 512)
                    src = PS[32:64, 4 + half, :]
                    t1 = cp(dv, bcs[0:32, s_], src, [p, dv.now] + free)
                    t1 = tt(dv, rbc[0:32, 0:512], src, bcs[0:32, s_], ALU.subtract, [t1])
                    pf[4 + half] = [ee[half], t1]
                    t2 = cp(dv, bcs[32:64, s_], rbc[0:32, 0:512], [t1])
                    t2 = cp(dv, mid[0:32, 0:512], rbc[0:32, 0:512], [t1])
                    t2 = tt(dv, bcs[64:96, s_], rbc[0:32, 0:512], mid[0:32, 0:512], ALU.subtract, [t2])
                n = 0
                lasts = []
                for half in range(2):
                    s_ = slice(512 * half, 512 * half + 512)
                    for c in range(4):
                        bank = n % 4
                        n += 1
                        p = mm(PS[:, bank, :], dtw[:, 128 * c:128 * c + 128], dbl[:, s_], True, True, pf[bank] + [ee[half]], inc=True)
                        a = act(de[:, c, s_], PS[:, bank, :], ACT.Abs, [p] + free, bias=dtb[:, c:c + 1])
                        m = ts(dv, mx[:, c, s_], PS[:, bank, :], dtb[:, c:c + 1], 0.0, ALU.add, ALU.max, [p, a] + free)
                        pf[bank] = [a, m]
                    lasts.append((a, m))
                hs = [slice(0, 512), slice(512, 1024)]
                ts_ = [act(de[:, :, hs[z]], de[:, :, hs[z]], ACT.Exp, [lasts[z][0]], scale=-1.0) for z in range(2)]
                ts_ = [act(de[:, :, hs[z]], de[:, :, hs[z]], ACT.Ln, [ts_[z]], bias=ones[:, 0:1]) for z in range(2)]

                if between is not None:
                    between()

                def add(z):
                    return tt(dv, de[:, :, hs[z]], de[:, :, hs[z]], mx[:, :, hs[z]], ALU.add, [ts_[z], lasts[z][1]])

                def mul(z, t):
                    return tt(dv, du[:, :, hs[z]], de[:, :, hs[z]], u[:, :, hs[z]], ALU.mult, t)
                ac.after([add(0)])
                ac.after([add(1)])
                mul(0, [pe.now, dv.now])
                return mul

            def silu_z(sq, half, w):
                out_ = []
                for c in range(4):
                    p = xz(sq % 2, 4 + c, half, 4 + c)
                    a = act(dB[half][:, c, :], PS[:, 4 + c, :], ACT.Silu, [p] + w)
                    pf[4 + c] = [a]
                    out_.append(a)
                return out_

            def post_z(sq, first, w, t):
                es = []
                for half in range(2):
                    za = first if half == 0 else silu_z(sq, 1, w)
                    for c in range(4):
                        s_ = slice(512 * half, 512 * half + 512)
                        e = tt(dv, du[:, c, s_], du[:, c, s_], dB[half][:, c, :], ALU.mult, [za[c], t])
                    es.append(e)
                return es

            def post_o(sq, es, tiles, q):
                b = sq % 2
                pend = None

                def turn(item):
                    i, t = item
                    x = i % 2
                    p = mm(PS[:, 6 + x, 0:256], anti, tmp[x], True, True, pf[6 + x] + [t], inc=True)
                    tf[x] = [p]
                    o = MO[:, 8 * b + 7 - i, :]
                    t = tt(dv, o, o, PS[:, 6 + x, 0:256], ALU.add, [p])
                    pf[6 + x] = [t]
                tmp = [dA[0][:, x, 0:256] for x in range(2)]
                for i in tiles:
                    bank = 4 + i % 2
                    for c in range(4):
                        p = mm(PS[:, bank, 0:256], du[:, c, 128 * i:128 * i + 128], opw[:, c, :], c == 0, c == 3, pf[bank] + [es[i // 4]], inc=(c == 3))
                    if sq < 2:
                        t = cp(q, MO[:, 8 * b + i, :], PS[:, bank, 0:256], [p])
                        pf[bank] = [t]
                    else:
                        t = cp(q, tmp[i % 2], PS[:, bank, 0:256], [p] + tf[i % 2])
                        pf[bank] = [t]
                        if pend is not None:
                            turn(pend)
                        pend = (i, t)
                if pend is not None:
                    turn(pend)
            tf = [[], []]

            second = pre_b(0, pre_a(0, []), [zd])
            for sq in range(4):
                barrier()
                mul1 = second
                seq = [(half, n) for half in range(2) for n in range(16)]
                dAf, dBf, hf, cf, Bf = [[], []], [[], []], [[], []], [[], [], []], [[], []]
                made = {}

                def spread(k):
                    half, n = seq[k]
                    x = k % 2
                    s_ = slice(512 * half, 512 * half + 512)
                    pb = mm(PS[:, 4 + x, :], bc(eye3[0:96, n:n + 1], [96, 128]), bcs[0:96, s_], True, True, pf[4 + x], inc=True)
                    pc = mm(PS[:, 6 + x, :], bc(eye3[0:96, 16 + n:17 + n], [96, 128]), bcs[0:96, s_], True, True, pf[6 + x], inc=True)
                    for c in range(4):
                        a = act(dA[x][:, c, :], de[:, c, s_], ACT.Exp, dAf[x], scale=An[:, c, n:n + 1])
                    c_ = act(Cs[k % 3], PS[:, 6 + x, :], ACT.Copy, [pc] + cf[k % 3])
                    pf[6 + x] = [c_]
                    made[k] = (pb, a, c_)

                def bu(k):
                    half, n = seq[k]
                    x = k % 2
                    s_ = slice(512 * half, 512 * half + 512)
                    t = tt(dv, dB[x], du[:, :, s_], bc(PS[:, 4 + x, :].unsqueeze(1), [128, 4, 512]), ALU.mult, [made[k][0]] + dBf[x])
                    pf[4 + x] = [t]
                    Bf[x] = [t]
                yw = {}

                def ysum(k):
                    half, n = seq[k]
                    ys = []
                    for c in range(4):
                        y = mm(PS[:, c, :], ident, h[k % 2][:, c, :], n == 0, n == 15, [yw[k][c // 2]] + (pf[c] if n == 0 else []), inc=(c % 2 == 1))
                        if c % 2 == 1:
                            ys.append(y)
                    return ys

                def out_half(half, y):
                    s_ = slice(512 * half, 512 * half + 512)
                    for c in range(4):
                        t = stt(du[:, c, s_], u[:, c, s_], Dc[:, c:c + 1], PS[:, c, :], ALU.mult, ALU.add, y + [dv.now])
                        pf[c] = [t]
                spread(0)
                spread(1)
                bu(0)
                for k, (half, n) in enumerate(seq):
                    x = k % 2
                    if k == 16:
                        y = ysum(15)
                        hf[1] = y
                        out_half(0, y)
                        bu(16)
                    if k == 3:
                        mul1(1, [dv.now])
                    g = []
                    for c in range(4):
                        ini = 0.0 if half == 0 else hl[:, n, c:c + 1]
                        t2 = dv.put(lambda e, c=c, x=x, ini=ini: e.tensor_tensor_scan(
                            out=h[x][:, c, :], data0=dA[x][:, c, :], data1=dB[x][:, c, :], initial=ini, op0=ALU.mult, op1=ALU.add),
                            [made[k][1]] + Bf[x] + hf[x][c // 2:c // 2 + 1])
                        if c % 2 == 1:
                            hw = []
                            c2 = slice(c - 1, c + 1)
                            if half == 0:
                                hw = [cp(ac, hl[:, n, c2], h[x][:, c2, 511], [t2])]
                            c3 = bc(Cs[k % 3].unsqueeze(1), [128, 2, 512])
                            g.append(tt(gp, h[x][:, c2, :], h[x][:, c2, :], c3, ALU.mult, [made[k][2], t2] + hw))
                    dAf[x] = [t2]
                    dBf[x] = [t2]
                    if k + 1 < 32 and k != 15:
                        bu(k + 1)
                    yw[k] = g
                    cf[k % 3] = g
                    if k + 2 < 32:
                        spread(k + 2)
                    if k == 31:
                        first = silu_z(sq, 0, dBf[0])
                    if k > 0 and k != 16:
                        hf[1 - x] = ysum(k - 1)
                y = ysum(31)
                hf[1] = y
                out_half(1, y)
                t = dv.now
                es = post_z(sq, first, dBf[1], t)
                if sq < 3:
                    if sq == 1:
                        flipped_T([pe.now])
                    silu = pre_a(sq + 1, [t])
                    post_o(sq, es, range(0, 4), ac)
                    second = pre_b(sq + 1, silu, [pe.now], lambda sq=sq, es=es: post_o(sq, es, range(4, 8), dv))
                else:
                    post_o(sq, es, range(8), ac)
                    barrier()
            scr.at = scr.lo
            xn = scr.take([NT, D])
            st_at = scr.at
            layer_norm_T(src=MO, keep=xn, mul=lambda c: lg[:, c:c + 1], add=lambda c: lb[:, c:c + 1])
            scr.at = st_at
            add_bias(X, fb2)
            dv.after([gp.now])
            hT = [scr.take([8, 512]) for _ in range(2)]
            hTf = [[], []]
            n = 0
            pend = None

            def down(item):
                x, k, hr = item
                add_proj(X, lambda c, i: hT[x][:, c, 128 * (i - 4 * k):128 * (i - 4 * k) + 128], 8, lambda c: fw2[:, c, :],
                         None, tiles=range(4 * k, 4 * k + 4), w=hr, banks=(4, 5, 6, 7))
                hTf[x] = [pe.now]
            for k in range(4):
                x = k % 2
                hr = []
                for f in range(8):
                    bank = n % 4
                    n += 1
                    for c in range(2):
                        t = mm(PS[:, bank, :], fw1[:, c, 128 * f:128 * f + 128], XNT[:, c, 512 * k:512 * k + 512], c == 0, c == 1, pf[bank], inc=(c == 1))
                    t = act(hT[x][:, f, :], PS[:, bank, :], ACT.Gelu, [t] + hTf[x], bias=fb1[:, f:f + 1])
                    pf[bank] = [t]
                    hr.append(t)
                if pend is not None:
                    down(pend)
                pend = (x, k, hr)
            down(pend)

        def load_7():
            WB[1].clear()
            W[7] = load_w(WB[1], "pk7")

        def phase_7():
            w, wt = W[7]
            wq = w[:, 0:2048].rearrange("p (k n) -> p k n", k=8)
            ws = w[:, 2048:2054].rearrange("p (z c) -> p z c", z=3)
            row = scr.take([260])
            ct = scr.take([4, D])
            ld = Load("d_p7")
            ld.add(row[:, 0:257], ins["pk7r"])
            sp.after([fill(gp, ct, 0.0)])
            for b in range(2):
                ld.add(ct[:, 2 * b, :], ins["ctx"][b, 0:128, :])
                ld.add(ct[0:26, 2 * b + 1, :], ins["ctx"][b, 128:154, :])
            XN = scr.take([NT, D])
            layer_norm_T(keep=XN)
            HQ = scr.take([NT, D])
            hqT = scr.take([2, 2048])
            prod = scr.take([2, 2048])
            d3 = scr.take([2, 308])
            rr = scr.take([308])
            nm = scr.take([NT])
            sm = scr.take([NT])
            ri = scr.take([NT])
            Pm = [scr.take([KC]) for _ in range(2)]
            PT = [scr.take([2, 128]) for _ in range(2)]
            ml = scr.take([2])
            M = scr.take([2])
            e_ = scr.take([NT])
            hc = scr.take([2, 2])
            sr = scr.take([2])
            w4 = scr.take([2, 2, D])
            for x in range(2):
                fill(gp, PT[x], 0.0)
            for q in lanes:
                q.after([wt, ld.ready, gp.now])
            add_bias(X, row[:, 0:256])
            for c in range(2):
                t = ts(dv, d3[:, c, :], ctxT[:, c, :], ws[:, 2, c:c + 1], ws[:, 0, c:c + 1], ALU.mult, ALU.add)
            for c in range(2):
                p = mm(PS[0:1, 0, 0:308], ws[:, 1, c:c + 1], ctxT[:, c, :], c == 0, c == 1, pf[0], inc=(c == 1))
            t = ts(dv, rr[0:1, :], PS[0:1, 0, 0:308], row[0:1, 256:257], None, ALU.add, None, [p, t])
            pf[0] = [t]
            pe.after([t])
            pfree = [[], []]
            ptfree = [[], []]
            for i in range(NT):
                b, x = i // 8, i % 2
                bk = 4 * x
                for c in range(2):
                    mm(PS[:, bk, 0:KC], XNT[:, c, 128 * i:128 * i + 128], d3[:, c, KC * b:KC * b + KC], c == 0, False, pf[bk])
                p = mm(PS[:, bk, 0:KC], ones[0:1, 0:128], rr[0:1, KC * b:KC * b + KC], False, True, (), inc=True)
                t = red(nm[:, i:i + 1], PS[:, bk, 0:KC], ALU.max, [p], neg=True)
                t = act(Pm[x], PS[:, bk, 0:KC], ACT.Exp, [t] + pfree[x], bias=nm[:, i:i + 1], acc=sm[:, i:i + 1])
                pf[bk] = [t]
                r = recip(ri[:, i:i + 1], sm[:, i:i + 1], [t])
                tr(PS[:, bk + 1, 0:128], Pm[x][:, 0:128], ident, [t] + pf[bk + 1])
                p = tr(PS[0:26, bk + 1, 128:256], Pm[x][:, 128:154], ident, (), inc=True)
                pfree[x] = [p]
                e1 = cp(ac, PT[x][:, 0, :], PS[:, bk + 1, 0:128], [p] + ptfree[x])
                e2 = cp(ac, PT[x][0:26, 1, :], PS[0:26, bk + 1, 128:256], [])
                pf[bk + 1] = [e2]
                mm(PS[:, bk + 2, 0:256], PT[x][:, 0, :], ct[:, 2 * b, :], True, False, [e2] + pf[bk + 2])
                p = mm(PS[:, bk + 2, 0:256], PT[x][:, 1, :], ct[:, 2 * b + 1, :], False, True, (), inc=True)
                ptfree[x] = [p]
                t = ts(dv, HQ[:, i, :], PS[:, bk + 2, 0:256], ri[:, i:i + 1], None, ALU.mult, None, [p, r])
                pf[bk + 2] = [t]
            t = red(ml, nm.rearrange("p (b t) -> p b t", b=2), ALU.min, [dv.now], neg=True)
            t = gp.put(lambda e: e.partition_all_reduce(M, ml, 128, bass.bass_isa.ReduceOp.max), [t])
            t = ts(dv, M, M, -1.0, None, ALU.mult, None, [t])
            for b in range(2):
                t2 = act(e_[:, 8 * b:8 * b + 8], nm[:, 8 * b:8 * b + 8], ACT.Exp, [t], bias=M[:, b:b + 1], scale=-1.0)
            for b in range(2):
                for c in range(3):
                    o = PS[:, 3, 4 * b + c:4 * b + c + 1]
                    for k in range(8):
                        i = 8 * b + k
                        l = XN[:, i, 128 * c:128 * c + 128] if c < 2 else ones
                        p = mm(o, l, e_[:, i:i + 1], k == 0, k == 7, [t2] + pf[3], inc=(k == 7))
            v = PS[:, 3, 0:8].rearrange("p (b c) -> p b c", b=2)
            t = recip(sr, v[:, :, 2], [p])
            t = tt(dv, hc, v[:, :, 0:2], bc(sr.unsqueeze(2), [128, 2, 2]), ALU.mult, [t])
            pf[3] = [t]
            for b in range(2):
                for c in range(2):
                    t2 = stt(w4[:, b, c, :], wq[:, 6 + c, :], hc[:, b, c:c + 1], wq[:, c, :], ALU.mult, ALU.add, [t])
            barrier()
            to_T(lambda i, c: HQ[:, i, 128 * c:128 * c + 128], lambda c, k: hqT[:, c, 512 * k:512 * k + 512], 2, lambda i: [])
            barrier()
            tt(gp, prod[:, 0, :], XNT[:, 0, :], hqT[:, 0, :], ALU.mult)
            tt(dv, prod[:, 1, :], XNT[:, 1, :], hqT[:, 1, :], ALU.mult)
            barrier()

            def lhs(c, i):
                return [XNT, hqT, prod][c // 2][:, c % 2, 128 * i:128 * i + 128]
            for b in range(2):
                add_proj(X, lhs, 6, lambda c, b=b: w4[:, b, c, :] if c < 2 else wq[:, c, :], None,
                         tiles=range(8 * b, 8 * b + 8))

        def top2(l, heap, t):
            oh1, t = first_max(l, heap, [t])
            l2 = heap.take([NT, 8])
            t = stt(l2, oh1, NEG, l, ALU.mult, ALU.add, [t])
            oh2, t = first_max(l2, heap, [t])
            return oh1, oh2, l2, t

        def load_8():
            WB[0].clear()
            W[8] = load_w(WB[0], "pk8")

        def add_H(H):
            for k in range(4):
                v = X[:, 4 * k:4 * k + 4, :]
                tt([dv, gp][k % 2], v, v, H[:, 4 * k:4 * k + 4, :], ALU.add, [q.now for q in (dv, gp)])

        def phase_8():
            w, wt = W[8]
            WA.clear()
            H = WA.take([NT, D])
            zt = WA.take([1024])
            sp.after([fill(gp, zt, 0.0)])
            zero_rows(xg8, 6144, zt)
            zero_done = zeros.ready
            wo = w_rows(w[:, 1536:2048])
            l1 = w[:, 2048:2050]
            l2 = w[:, 2050:2052]
            gw = w[:, 2052:2068].rearrange("p (c n) -> p c n", c=2)
            for q in lanes:
                q.after([wt])
            att = Attention(S, False, plain_qkv(w_seg(w[:, 0:1536]), wt))
            layer_norm_T(keep=H)
            barrier()
            rms_T(H, lambda c: l1[:, c:c + 1], 1e-5, keep=att.O)
            barrier()
            att.run()
            out_proj(att, wo, None, H, wt)
            barrier()
            scr.clear()
            xn = scr.take([NT, D])
            rms_T(H, lambda c: l2[:, c:c + 1], 1e-5, keep=xn)
            l, t = logits8(lambda c: gw[:, c, :], None, scr)
            oh1, oh2, lm, t = top2(l, scr, t)
            ohs = (oh1, oh2)
            loc, cnt, tl = places(ohs, scr, t)
            m3 = scr.take([8, 8])
            tiles_ = scr.take([8])
            end = scr.take([8])
            beg = scr.take([8])
            tmp = scr.take([NT, 8])
            idf = scr.take([2, NT])
            idx = scr.take([2, NT], I32)
            te = scr.take([24, 8])
            wif = scr.take([24])
            widx = scr.take([24], I32)
            t2 = ts(dv, m3, bc(el8.unsqueeze(1), [128, 8, 8]), 256.0, None, ALU.mult, None, [tl])
            t2 = tt(dv, m3, bc(cnt.unsqueeze(2), [128, 8, 8]), m3, ALU.is_gt, [t2])
            t2 = red(tiles_, m3, ALU.add, [t2])
            t2 = dv.put(lambda e: e.tensor_tensor_scan(out=end, data0=ones[:, 0:8], data1=tiles_, initial=0.0, op0=ALU.mult, op1=ALU.add), [t2])
            t2 = tt(dv, beg, end, tiles_, ALU.subtract, [t2])
            t2 = tt(dv, te, bc(end.unsqueeze(1), [128, 24, 8]), bc(iota24.unsqueeze(2), [128, 24, 8]), ALU.is_le, [t2])
            t2 = red(wif, te, ALU.add, [t2])
            t2 = ts(dv, wif, wif, 7.0, 128.0, ALU.min, ALU.mult, [t2])
            t2 = ts(dv, wif, wif, pcol, None, ALU.add, None, [t2])
            tw = cp(dv, widx, wif, [t2])
            ring = [scr.take([3072]) for _ in range(3)]
            lwt = [Load("d_w8a"), Load("d_w8b"), Load("d_w8c")]
            wrows = ins["pk8e"].rearrange("e p n -> (e p) n")

            def load_w8(j, w):
                gp.after(w)
                l = lwt[j % 3]
                gp.items.append(move_rows(ring[j % 3], None, wrows, bass.IndirectOffsetOnAxis(widx[:, j:j + 1], 0), 1023, l.sem))
                l.n += 16

            for j in range(3):
                load_w8(j, [tw])
            for z in range(2):
                t2 = stt(loc[z], bc(beg.unsqueeze(2), [128, 8, NT]), 256.0, loc[z], ALU.mult, ALU.add, [t2])
                t2 = tt(dv, tmp, ohs[z], loc[z].rearrange("p e i -> p i e"), ALU.mult, [t2])
                t2 = red(idf[:, z, :], tmp, ALU.add, [t2])
                t2 = cp(dv, idx[:, z, :], idf[:, z, :], [t2])
                lsc = scatter_rows(xg8, 6143, xn, idx[:, z, :], [t2, zero_done])
            g2 = scr.take([2, NT])
            m1 = g2[:, 0, :]
            m2 = g2[:, 1, :]
            ta = red(m1, l, ALU.max, [t])
            tb = red(m2, lm, ALU.max, [t])
            t = tt(dv, m2, m2, m1, ALU.subtract, [ta, tb])
            t = act(m2, m2, ACT.Exp, [t])
            t = ts(dv, m1, m2, 1.0, None, ALU.add, None, [t])
            t = recip(m1, m1, [t])
            t = tt(dv, m2, m2, m1, ALU.mult, [t])
            dv.after([t])
            NTL = 23
            XE = [scr.take([2, D]) for _ in range(2)]
            XT = [scr.take([2, 256]) for _ in range(2)]
            Y = [scr.take([2, D]) for _ in range(2)]
            hT = [scr.take([4, 256]) for _ in range(2)]
            sg = [scr.take([256]) for _ in range(2)]
            yz = [xn, scr.take([NT, D])]
            lxe = [Load("d_x8a"), Load("d_x8b")]
            lye = [Load("d_y8a"), Load("d_y8b")]
            xef, xtf, hf, sgf = [[], []], [[], []], [[], []], [[], []]

            def load_x(j):
                lxe[j % 2].add(XE[j % 2], xg8[256 * j:256 * j + 256, :].rearrange("(j p) c -> p j c", p=128), [lsc.ready] + xef[j % 2])

            def turn_x(j):
                bk = 4 + j % 2
                for c in range(2):
                    for i in range(2):
                        t = tr(PS[:, bk, 256 * c + 128 * i:256 * c + 128 * i + 128], XE[j % 2][:, i, 128 * c:128 * c + 128], ident,
                               [lxe[j % 2].ready] + pf[bk], inc=(c == 1 and i == 1))
                xef[j % 2] = [t]
                for c in range(2):
                    t2 = ts(dv, XT[j % 2][:, c, :], PS[:, bk, 256 * c:256 * c + 256], l2[:, c:c + 1], None, ALU.mult, None, [t] + xtf[j % 2])
                pf[bk] = [t2]
                return [t2]

            def down(item):
                j, w2, hr = item
                x = j % 2
                bk = 6 + x
                for i in range(2):
                    for f in range(4):
                        t = mm(PS[:, bk, 256 * i:256 * i + 256], hT[x][:, f, 128 * i:128 * i + 128], w2[:, f, :], f == 0, f == 3, pf[bk] + hr,
                               inc=(i == 1 and f == 3))
                hf[x] = [t]
                e = cp(ac, Y[x], PS[:, bk, :].rearrange("p (k c) -> p k c", k=2), [t, lye[x].ready])
                pf[bk] = [e]
                lye[x].add(yg8[256 * j:256 * j + 256, :].rearrange("(j p) c -> p j c", p=128), Y[x], [e])
                return t
            load_x(0)
            load_x(1)
            xt = turn_x(0)
            pend = None
            nb = 0
            for j in range(NTL):
                x = j % 2
                rg = ring[j % 3]
                w13 = [rg[:, 1024 * z:1024 * z + 1024].rearrange("p (c n) -> p c n", c=2) for z in range(2)]
                w2 = rg[:, 2048:3072].rearrange("p (f n) -> p f n", f=4)
                pe.after([lwt[j % 3].ready] + xt)
                hr = []
                for f in range(4):
                    bk = nb % 4
                    y = nb % 2
                    nb += 1
                    for z in range(2):
                        for c in range(2):
                            t = mm(PS[:, bk, 256 * z:256 * z + 256], w13[z][:, c, 128 * f:128 * f + 128], XT[x][:, c, :], c == 0, c == 1, pf[bk],
                                   inc=(z == 1 and c == 1))
                    a = act(sg[y], PS[:, bk, 0:256], ACT.Silu, [t] + sgf[y])
                    e = tt(dv, hT[x][:, f, :], PS[:, bk, 256:512], sg[y], ALU.mult, [a] + hf[x])
                    pf[bk] = [e]
                    sgf[y] = [e]
                    hr.append(e)
                xtf[x] = [t]
                if j + 1 < NTL:
                    xt = turn_x(j + 1)
                if j + 2 < NTL:
                    load_x(j + 2)
                if pend is not None:
                    t = down(pend)
                    if j + 2 < NTL:
                        load_w8(j + 2, [t])
                pend = (j, w2, hr)
            down(pend)
            combine(yg8, 5887, yz, idx, g2, [lye[0].ready, lye[1].ready, lsc.ready], H)

        def load_9():
            WB[1].clear()
            W[9] = load_w(WB[1], "pk9")

        def phase_9():
            w, wt = W[9]
            dq, uqT = w[:, 0:16], w[:, 16:32]
            dkv = w[:, 32:64].rearrange("p (c n) -> p c n", c=2)
            ukvT = w[:, 64:128].rearrange("p (c n) -> p c n", c=2)
            kr, qr = w[0:64, 128:144], w[0:64, 144:160]
            woT = w[0:16, 160:176]
            nw = w[:, 176:208].rearrange("p (z d) -> p z d", z=2)
            for q in lanes:
                q.after([wt])
            sm = scr.take([80])
            BD = scr.take([5, 8, 16])
            RQ = scr.take([NT, 2, 16])
            flat = BD.rearrange("p z h d -> p (z h d)")

            def qkv(b, hh, t, rows, hq, hk, ps, w):
                r0 = b * S + 128 * t
                return mm(ps[:, 0:512], XNT[:, hh, r0:r0 + 128], flat[:, 0:512], True, True, w, inc=True)

            def post(b, hh, t, ps, w, a):
                t1 = tt(dv, a.rearrange("p z h d -> p (z h) d"), ps[:, 0:256].rearrange("p (h d) -> p h d", d=16),
                        bc(RQ[:, 8 * b + t, hh, :].unsqueeze(2), [128, 16, 16]), ALU.mult, w)
                t2 = tt(dv, a, a, bc(nw.unsqueeze(2), [128, 2, 8, 16]), ALU.mult, [t1])
                t3 = tt(dv, a[:, 1], a[:, 1], ps[:, 384:512].rearrange("p (h d) -> p h d", d=16), ALU.add, [t2])
                return t3, [t3]
            att = Attention(S, True, qkv, post=post)
            layer_norm_T(keep=att.O)
            sq = [att.P[0][:, x, :].rearrange("p (s n) -> p s n", s=2) for x in range(2)]
            sd = att.P[1].rearrange("p a b -> p (a b)")[:, 0:NT * 32]
            mm(PS[0:16, 0, 0:16], dq, uqT, True, True)
            for c in range(2):
                mm(PS[0:16, 0, 16:48], dkv[:, c, :], ukvT[:, c, :], c == 0, c == 1)
            p = mm(PS[0:16, 0, 48:64], kr, qr, True, True, (), inc=True)
            t1 = cp(dv, sm[0:16, 0:64], PS[0:16, 0, 0:64], [p])
            t2 = cp(dv, sm[0:16, 64:80], woT)
            p = mm(PS[:, 1, 0:80], rep16, sm[0:16, :], True, True, [t1, t2], inc=True)
            t = tt(dv, BD, bc(PS[:, 1, 0:80].rearrange("p (z d) -> p z d", z=5).unsqueeze(2), [128, 5, 8, 16]),
                   bc(bdm.unsqueeze(1).unsqueeze(3), [128, 5, 8, 16]), ALU.mult, [p])
            pe.after([t])
            for q in (pe,):
                q.after([t])
            fr = [[], []]
            pf[0] = []
            for i in range(NT):
                x = i % 2
                for hh in range(2):
                    p = mm(PS[:, 2 + x, 256 * hh:256 * hh + 256], XNT[:, hh, 128 * i:128 * i + 128], flat[:, 0:256], True, True, pf[2 + x], inc=(hh == 1))
                a = act(sq[x], PS[:, 2 + x, :].rearrange("p (s n) -> p s n", s=2), ACT.Square, [p] + fr[x])
                pf[2 + x] = [a]
                t = red(RQ[:, i], sq[x].rearrange("p s (h d) -> p s h d", d=16), ALU.add, [a])
                fr[x] = [t]
            rq = RQ.rearrange("p i s h -> p (i s h)")
            t = ts(dv, rq, rq, 1.0 / 16, 1.1920929e-07, ALU.mult, ALU.add, [dv.now])
            t = act(sd, rq, ACT.Sqrt, [t])
            t = recip(rq, sd, [t])
            barrier()
            att.run()
            barrier()
            to_T(lambda i, c: att.O[:, i, 128 * c:128 * c + 128], lambda c, k: XNT[:, c, 512 * k:512 * k + 512], 2, lambda i: [])
            barrier()
            for i in range(0, NT, 2):
                bk = (i // 2) % 8
                for z in range(2):
                    for c in range(2):
                        p = mm(PS[:, bk, 256 * z + 128 * c:256 * z + 128 * c + 128], XNT[:, c, 128 * (i + z):128 * (i + z) + 128], flat[:, 512:640],
                               True, True, pf[bk], inc=(z == 1 and c == 1))
                v = X[:, i:i + 2, :]
                t = tt(dv, v, PS[:, bk, :].rearrange("p (k c) -> p k c", k=2), v, ALU.add, [p])
                pf[bk] = [t]

        def load_10():
            WB[0].clear()
            W[10] = load_w(WB[0], "pk10")

        def phase_10():
            w, wt = W[10]
            b1 = scr.take([NT, KC])
            an = scr.take([NT])
            mq = scr.take([NT, KC], BF16)
            mT = scr.take([2, 2048], BF16)
            row = scr.take([256])
            ld = Load("d_p10")
            ld.add(row, ins["pk10r"])
            mi = b1.bitcast(I32)
            for b in range(2):
                ld.add(mi[:, 8 * b:8 * b + 8, :], ins["mask32"][b, 0].rearrange("(t p) k -> p t k", p=128))
            att = Attention(KC, False, plain_qkv(w_seg(w[:, 0:1536]), wt), mask=(mq, mT, an))
            layer_norm_T(keep=att.O)
            for q in lanes:
                q.after([wt, ld.ready])
            t = ts(dv, b1, mi, 0.0, None, ALU.not_equal, None)
            t = red(an, b1, ALU.max, [t])
            t = ts(dv, b1, b1, 1.0, -NEG, ALU.subtract, ALU.mult, [t])
            t2 = tt(dv, mq, b1, bc(an.unsqueeze(2), [128, NT, KC]), ALU.mult, [t])
            for k in range(4):
                for z in range(2):
                    rows = 128 if z == 0 else 26
                    bk = 2 * k + z
                    pb = PS[:, bk, 0:256].bitcast(BF16)
                    for j in range(4):
                        p = tr(pb[0:rows, 128 * j:128 * j + 128], mq[:, 4 * k + j, 128 * z:128 * z + rows], identb, [t2] + pf[bk], inc=(j == 3))
                    t = cp(evac_lane(), mT[0:rows, z, 512 * k:512 * k + 512], pb[0:rows, :], [p])
                    pf[bk] = [t]
            barrier()
            add_bias(X, row)
            att.run()
            out_proj(att, w_rows(w[:, 1536:2048]), None, X, wt)

        def load_11():
            WB[1].clear()
            W[11] = load_w(WB[1], "pk11")

        def phase_11():
            w, wt = W[11]
            WA.clear()
            H = WA.take([NT, D])
            lw = w[:, 2048:2056].rearrange("p (z c) -> p z c", z=4)
            wr = w[:, 2056:2072].rearrange("p (c n) -> p c n", c=2)
            wo = w_rows(w[:, 1536:2048])
            row = scr.take([1024])
            ld = Load("d_p11")
            ld.add(row, ins["pk11r"])
            att = Attention(S, False, plain_qkv(w_seg(w[:, 0:1536]), wt), bias=row[:, 0:768].rearrange("p (s n) -> p s n", s=2))
            for q in lanes:
                q.after([wt, ld.ready])
            zt = WA.take([1024])
            sp.after([fill(gp, zt, 0.0)])
            zero_rows(xg, 4096, zt)
            zero_done = zeros.ready
            layer_norm_T(keep=H)
            barrier()
            layer_norm_T(src=H, keep=att.O, mul=lambda c: lw[:, 0, c:c + 1], add=lambda c: lw[:, 1, c:c + 1])
            barrier()
            add_bias(H, row[:, 768:1024])
            att.run()
            out_proj(att, wo, None, H, wt)
            barrier()
            scr.clear()
            ring = [scr.take([4360]) for _ in range(2)]
            lw1 = [Load("d_w1a"), Load("d_w1b")]
            lw2 = [Load("d_w2a"), Load("d_w2b")]

            def load_w1(e, w=()):
                lw1[e % 2].add(ring[e % 2][:, 0:2056], ins["pk11e"][e, :, 0:2056], w)

            def load_w2(e, w=()):
                lw2[e % 2].add(ring[e % 2][:, 2056:4360], ins["pk11e"][e, :, 2056:4360], w)
            for k in range(2):
                load_w1(k)
                load_w2(k)
            xn = scr.take([NT, D])
            layer_norm_T(src=H, keep=xn, mul=lambda c: lw[:, 2, c:c + 1], add=lambda c: lw[:, 3, c:c + 1])
            l, t = logits8(lambda c: wr[:, c, :], None, scr)
            p, r, t2 = softmax8(l, scr, [t])
            t2 = tt(dv, p, p, bc(r.unsqueeze(2), [128, NT, 8]), ALU.mult, [t2])
            oh1, t = first_max(p, scr, [t2])
            l2 = scr.take([NT, 8])
            t = stt(l2, oh1, NEG, l, ALU.mult, ALU.add, [t])
            oh2, t = first_max(l2, scr, [t])
            ohs = (oh1, oh2)
            loc, tot, t = places(ohs, scr, t)
            drop = scr.take([8, NT])
            idf = scr.take([2, NT])
            idx = scr.take([2, NT], I32)
            tmp = scr.take([NT, 8])
            e512 = bc(el8.unsqueeze(2), [128, 8, NT])
            for z in range(2):
                t = ts(dv, drop, loc[z], 512.0, None, ALU.is_ge, None, [t])
                t = stt(loc[z], e512, 512.0, loc[z], ALU.mult, ALU.add, [t])
                t = stt(loc[z], drop, 131072.0, loc[z], ALU.mult, ALU.add, [t])
                t = tt(dv, tmp, ohs[z], loc[z].rearrange("p e i -> p i e"), ALU.mult, [t])
                t = red(idf[:, z, :], tmp, ALU.add, [t])
                t = cp(dv, idx[:, z, :], idf[:, z, :], [t])
                lsc = scatter_rows(xg, 4095, xn, idx[:, z, :], [t, zero_done])
                t = ts(dv, drop, drop, -1.0, 1.0, ALU.mult, ALU.add, [t])
                t = tt(dv, ohs[z], ohs[z], drop.rearrange("p e i -> p i e"), ALU.mult, [t])
            G = scr.take([NT, 8])
            g2 = scr.take([2, NT])
            dn = scr.take([NT])
            t = tt(dv, G, oh1, oh2, ALU.add, [t])
            t = tt(dv, G, G, p, ALU.mult, [t])
            t = red(dn, G, ALU.add, [t])
            t = ts(dv, dn, dn, 1.1920929e-07, None, ALU.max, None, [t])
            t = recip(dn, dn, [t])
            t = ts(dv, dn, dn, 0.8, None, ALU.mult, None, [t])
            t = tt(dv, G, G, bc(dn.unsqueeze(2), [128, NT, 8]), ALU.mult, [t])
            for z in range(2):
                t = tt(dv, tmp, ohs[z], G, ALU.mult, [t])
                t = red(g2[:, z, :], tmp, ALU.add, [t])
            dv.after([t])
            XE = [scr.take([4, D]) for _ in range(2)]
            Y = [scr.take([4, D]) for _ in range(2)]
            hT = [scr.take([8, 512]) for _ in range(2)]
            ye = scr.take([NT, D])
            yz = [xn, ye]
            lxe = [Load("d_xe0"), Load("d_xe1")]
            lye = [Load("d_ye0"), Load("d_ye1")]
            xef, hf = [[], []], [[], []]
            xt_free = [[] for _ in range(4)]

            def load_x(e):
                lxe[e % 2].add(XE[e % 2], xg[512 * e:512 * e + 512, :].rearrange("(j p) c -> p j c", p=128), [lsc.ready] + xef[e % 2])

            def turn_x(e):
                toks = []
                for c in range(2):
                    bk = 6 + c
                    for j in range(4):
                        t = tr(PS[:, bk, 128 * j:128 * j + 128], XE[e % 2][:, j, 128 * c:128 * c + 128], ident,
                               [lxe[e % 2].ready] + pf[bk], inc=(j == 3))
                    v = XNT[:, c, 512 * (e % 4):512 * (e % 4) + 512]
                    t = ts(dv, v, PS[:, bk, :], lw[:, 2, c:c + 1], lw[:, 3, c:c + 1], ALU.mult, ALU.add, [t] + xt_free[e % 4])
                    pf[bk] = [t]
                    toks.append(t)
                xef[e % 2] = [pe.now]
                return toks

            lw2_at = {}

            def down(item):
                e, w2, b2, hr = item
                x = e % 2
                hr = hr + [lw2_at[e]]
                dv.after([lw2_at[e]])
                for i2 in range(2):
                    bk = 4 + i2
                    for z in range(2):
                        i = 2 * i2 + z
                        for f in range(8):
                            t = mm(PS[:, bk, 256 * z:256 * z + 256], hT[x][:, f, 128 * i:128 * i + 128], w2[:, f, :], f == 0, f == 7, pf[bk] + hr,
                                   inc=(f == 7))
                    t2 = tt(dv, Y[x][:, 2 * i2:2 * i2 + 2, :], PS[:, bk, :].rearrange("p (k c) -> p k c", k=2),
                            bc(b2.unsqueeze(1), [128, 2, D]), ALU.add, [t, lye[x].ready])
                    pf[bk] = [t2]
                hf[x] = [t]
                lye[x].add(yg[512 * e:512 * e + 512, :].rearrange("(j p) c -> p j c", p=128), Y[x], [t2])
            load_x(0)
            load_x(1)
            for z in range(2):
                fill(gp, yz[z], 0.0, [lsc.ready, gp.now])
            xt = turn_x(0)
            pend = None
            for e in range(8):
                y = e % 2
                w1 = ring[y][:, 0:2048].rearrange("p (c n) -> p c n", c=2)
                bb = ring[y][:, 2048:2056]
                w2 = ring[y][:, 2056:4104].rearrange("p (f n) -> p f n", f=8)
                b2 = ring[y][:, 4104:4360]
                for q in (pe, ac, dv):
                    q.after([lw1[y].ready])
                hr = []
                pe.after(xt)
                for f in range(8):
                    bk = f % 4
                    for c in range(2):
                        t = mm(PS[:, bk, :], w1[:, c, 128 * f:128 * f + 128], XNT[:, c, 512 * (e % 4):512 * (e % 4) + 512], c == 0, c == 1, pf[bk], inc=(c == 1))
                    if f % 2:
                        t = act(hT[y][:, f, :], PS[:, bk, :], ACT.Relu, [t] + hf[y], bias=bb[:, f:f + 1])
                    else:
                        t = ts(dv, hT[y][:, f, :], PS[:, bk, :], bb[:, f:f + 1], 0.0, ALU.add, ALU.max, [t] + hf[y])
                    pf[bk] = [t]
                    hr.append(t)
                xt_free[e % 4] = [pe.now]
                if e + 2 < 8:
                    load_w1(e + 2, [pe.now] + hr)
                if e + 1 < 8:
                    xt = turn_x(e + 1)
                if e + 2 < 8:
                    load_x(e + 2)
                if pend is not None:
                    down(pend)
                    if e + 1 < 8:
                        load_w2(e + 1, [pe.now, dv.now])
                pend = (e, w2, b2, hr)
                lw2_at[e] = lw2[y].ready
            down(pend)
            combine(yg, 4095, yz, idx, g2, [lye[0].ready, lye[1].ready, gp.now], H)

        def places(ohs, heap, t):
            loc = [heap.take([8, NT]) for _ in range(2)]
            tot = [heap.take([8, NT + 1]) for _ in range(2)]
            of = [heap.take([8, NT + 1]) for _ in range(2)]
            on = heap.take([NT + 1])
            fill(dv, tot[0], 0.0)
            fill(dv, tot[1], 0.0)
            zz = fill(dv, on, 1.0)
            for z, oh in enumerate(ohs):
                f = oh.rearrange("p i e -> p (i e)")
                p1 = mm(PS[:, 2 * z + 1, 0:128], upper, f, True, True, [t] + pf[2 * z + 1], inc=True)
                p2 = mm(PS[:, 2 * z + 2, 0:128], ones, f, True, True, pf[2 * z + 2], inc=True)
                t1 = cp(dv, tot[z][:, :, 1:NT + 1], PS[:, 2 * z + 2, 0:128].rearrange("p (i e) -> p e i", e=8), [p2, zz])
                pf[2 * z + 2] = [t1]
                if z == 1:
                    t1 = cp(dv, tot[1][:, :, 0], of[0][:, :, NT], [t1, dv.now])
                for e in range(8):
                    t2 = dv.put(lambda q, e=e, z=z: q.tensor_tensor_scan(out=of[z][:, e, :], data0=on, data1=tot[z][:, e, :],
                                                                        initial=0.0, op0=ALU.mult, op1=ALU.add), [t1])
                t2 = tt(dv, loc[z], PS[:, 2 * z + 1, 0:128].rearrange("p (i e) -> p e i", e=8), of[z][:, :, 0:NT], ALU.add, [p1, t2])
                pf[2 * z + 1] = [t2]
                t2 = ts(dv, loc[z], loc[z], -1.0, None, ALU.add, None, [t2])
            return loc, of[1][:, :, NT], t2

        def move_rows(o, oo, i, io, bound, s):
            return lambda e: e.indirect_dma_start(o, oo, i, io, bounds_check=bound, oob_is_err=False).then_inc(s, 16)

        rows_moved = {}

        def rows_load(name):
            if name not in rows_moved:
                rows_moved[name] = Load(name)
            return rows_moved[name]

        def scatter_rows(dst, bound, src, idx, w):
            l = rows_load("d_scatter")
            gp.after(w)
            for i in range(NT):
                gp.items.append(move_rows(dst, bass.IndirectOffsetOnAxis(idx[:, i:i + 1], 0), src[:, i, :], None, bound, l.sem))
                l.n += 16
            return l

        def combine(src, bound, yz, idx, g2, w, H):
            gp.after(w)
            for z in range(2):
                for k in range(4):
                    l = Load(f"d_gather{bound}_{z}_{k}")
                    for i in range(4 * k, 4 * k + 4):
                        gp.items.append(move_rows(yz[z][:, i, :], None, src, bass.IndirectOffsetOnAxis(idx[:, z, i:i + 1], 0), bound, l.sem))
                        l.n += 16
                    for i in range(4 * k, 4 * k + 4):
                        stt(H[:, i, :], yz[z][:, i, :], g2[:, z, i:i + 1], H[:, i, :], ALU.mult, ALU.add, [l.ready, dv.now])
            barrier()
            add_H(H)

        zeros = Load("d_zero")

        def zero_rows(dst, rows, z):
            for k in range(rows // 512):
                zeros.add(dst[512 * k:512 * k + 512, :].rearrange("(p j) c -> p (j c)", p=128), z)

        xg8 = nc.dram_tensor("xg8", (6144, D), F32, kind="Internal").ap()
        yg8 = nc.dram_tensor("yg8", (5888, D), F32, kind="Internal").ap()
        xg = nc.dram_tensor("xg", (4096, D), F32, kind="Internal").ap()
        yg = nc.dram_tensor("yg", (4096, D), F32, kind="Internal").ap()

        LOADS = {0: load_0, 1: load_1, 2: load_2, 3: load_3, 4: load_4, 5: load_5, 6: load_6, 7: load_7, 8: load_8, 9: load_9,
                 10: load_10, 11: load_11}
        AHEAD = {1: 0, 3: 2, 4: 3, 5: 4, 6: 5, 7: 6, 8: 7, 9: 8, 10: 9, 11: 10}
        loaded = set()

        def load_for(p):
            if p not in loaded:
                loaded.add(p)
                LOADS[p]()

        FN = {0: phase_0, 1: phase_1, 2: phase_2, 3: phase_3, 4: phase_4, 5: phase_5, 6: phase_6, 7: phase_7,
              8: phase_8, 9: phase_9, 10: phase_10, 11: phase_11}
        for p in phases:
            scr.clear()
            load_for(p)
            for nxt, at in AHEAD.items():
                if at == p and nxt in phases:
                    load_for(nxt)
            FN[p]()
            barrier()
        lo = Load("d_out")
        for i in range(4):
            lo.add(out.rearrange("b (t p) c -> p (b t) c", p=128)[:, 4 * i:4 * i + 4, :], X[:, 4 * i:4 * i + 4, :],
                   [q.now for q in lanes])
        sp.after([lo.ready])

        block = ctx.enter_context(nc.Block())

        @block.sync
        def _(e):
            for f in sp.items:
                f(e)

        @block.tensor
        def _(e):
            for f in pe.items:
                f(e)

        @block.scalar
        def _(e):
            for f in ac.items:
                f(e)

        @block.vector
        def _(e):
            for f in dv.items:
                f(e)

        @block.gpsimd
        def _(e):
            for f in gp.items:
                f(e)


def ch(w):
    w = np.asarray(w)
    k, n = w.shape
    return w.reshape(k // 128, 128, n).transpose(1, 0, 2).reshape(128, (k // 128) * n)


def cols(v):
    return np.asarray(v).reshape(-1, 128).T


def pad_rows(w):
    w = np.asarray(w)
    return np.concatenate([w, np.zeros((128 - w.shape[0], w.shape[1]), w.dtype)], 0)


def every(v):
    v = np.asarray(v).reshape(1, -1)
    return np.broadcast_to(v, (128, v.shape[1]))


def seg(wq, wk, wv):
    k = wq.shape[0] // 128
    w = np.stack([np.asarray(a).reshape(k, 128, 2, 128) for a in (wq, wk, wv)], 3)
    return w.transpose(1, 0, 2, 3, 4).reshape(128, -1)


def seg_row(bq, bk, bv):
    return np.stack([np.asarray(a).reshape(2, 128) for a in (bq, bk, bv)], 1).reshape(1, 768)


def cat(*a):
    return np.ascontiguousarray(np.concatenate(a, axis=1))


def constants():
    p = np.arange(128)
    c = np.zeros((128, 840), np.float32)
    c[:, 0:128] = np.eye(128)
    c[:, 128:256] = np.eye(128)[::-1]
    c[0:16, 256:384] = np.tile(np.eye(16), (1, 8))
    c[:, 384:512] = np.where(p[None, :] > p[:, None], NEG, 0.0)
    c[:, 512:640] = np.where(p[:, None] > p[None, :], NEG, 0.0)
    c[:, 640:768] = p[:, None] <= p[None, :]
    c[:, 768:776] = (p[:, None] // 16) == np.arange(8)[None, :]
    c[:, 776:784] = 8.0 - np.arange(8)[None, :]
    c[:, 786:794] = np.arange(8)[None, :]
    c[:, 794:818] = np.arange(24)[None, :]
    c[:, 818] = p
    return c


def layout(I):
    o = {}
    o["consts"] = constants()
    o["x"] = np.asarray(I["x"])
    ctx = np.asarray(I["ctx_1024"])
    o["ctx"] = ctx
    o["ctxT"] = ch(ctx.reshape(308, 256).T)
    o["mask8"] = np.ascontiguousarray(I["mask_BxS2_bf1"]).view(np.uint8).reshape(1, 308)
    o["mask32"] = np.asarray(I["mask_Bx1xSxS2_if1"])
    a = {k[8:]: np.asarray(v) for k, v in I.items() if k.startswith("L0_attn_")}
    ukv = np.stack([a["W_UK"].reshape(64, 2, 128), a["W_UV"].reshape(64, 2, 128)], 2).reshape(64, 512)
    o["pk0"] = cat(ch(a["W_DKV"]), pad_rows(ukv), ch(a["W_UQ"]), ch(a["W_O"]))
    a = {k[9:]: np.asarray(v) for k, v in I.items() if k.startswith("L0_xattn_")}

    o["pk1"] = cat(ch(a["Wq"]), ch(a["Wk"]), ch(a["Wv"]), cols(a["gl"]), cols(a["bl"]), cols(a["gm"]), cols(a["bm"]))
    o["pk1o"] = ch(a["Wo"])
    a = {k[7:]: np.asarray(v) for k, v in I.items() if k.startswith("L0_ffn_")}
    o["pk2"] = cat(ch(a["expert_w"].transpose(1, 0, 2).reshape(256, 2048)), ch(a["router_w"]), every(a["router_b"]))
    o["pk2e"] = a["expert_b"]
    a = {k[8:]: np.asarray(v) for k, v in I.items() if k.startswith("L1_attn_")}
    o["pk3"] = cat(ch(a["Wqkv"].T), ch(a["Wproj"].T))
    o["pk3r"] = every(np.concatenate([a["bqkv"], a["bproj"]]))
    a = {k[9:]: np.asarray(v) for k, v in I.items() if k.startswith("L1_xattn_")}
    o["pk4"] = cat(seg(a["Wq"].T, a["Wk"].T, a["Wv"].T), ch(a["Wo"].T))
    o["pk4r"] = every(cat(seg_row(a["bq"], a["bk"], a["bv"]), a["bo"].reshape(1, 256)))
    a = {k[7:]: np.asarray(v) for k, v in I.items() if k.startswith("L1_ffn_")}
    o["pk5"] = cat(ch(a["w_gate"].T), ch(a["w_up"].T), ch(a["w_down"].T))
    a = {k[8:]: np.asarray(v) for k, v in I.items() if k.startswith("L2_attn_")}
    o["pk6"] = cat(ch(a["in_proj_w"]), ch(np.concatenate([a["x_proj_w"][:, 0:16], np.zeros((512, 16), np.float32), a["x_proj_w"][:, 16:48]], 1)), ch(a["out_proj_w"]), ch(a["ff_w1"]), pad_rows(a["dt_proj_w"]), ch(a["conv_w"]),
                   cols(a["conv_b"]), cols(a["dt_proj_b"]), ch(a["A_log"]), cols(a["D"]), cols(a["ln_g"]), cols(a["ln_b"]), cols(a["ff_b1"]),
                   every(a["ff_b2"]))
    o["pk6b"] = ch(a["ff_w2"])
    a = {k[9:]: np.asarray(v) for k, v in I.items() if k.startswith("L2_xattn_")}
    o["pk7"] = cat(ch(a["W_qv"]), cols(a["w_sim"]))
    o["pk7r"] = every(np.concatenate([a["b_qv"], a["b_sim"]]))
    a = {k[7:]: np.asarray(v) for k, v in I.items() if k.startswith("L2_ffn_")}
    o["pk8"] = cat(seg(a["wq"].T, a["wk"].T, a["wv"].T), ch(a["wo"].T), cols(a["ln1_w"]), cols(a["ln2_w"]), ch(a["gate_w"].T))
    o["pk8e"] = np.stack([cat(ch(a["w1"][e].T), ch(a["w3"][e].T), ch(a["w2"][e].T)) for e in range(8)])
    a = {k[8:]: np.asarray(v) for k, v in I.items() if k.startswith("L3_attn_")}
    o["pk9"] = cat(a["W_DQ"], np.ascontiguousarray(a["W_UQ"].T), ch(a["W_DKV"]), ch(a["W_UKV"].T), pad_rows(a["W_KR"]), pad_rows(a["W_QR"]),
                   pad_rows(a["W_O"].T), every(a["q_norm_w"]), every(a["k_norm_w"]))
    a = {k[9:]: np.asarray(v) for k, v in I.items() if k.startswith("L3_xattn_")}
    o["pk10"] = cat(seg(a["Wq"].T, a["Wk"].T, a["Wv"].T), ch(a["Wo"].T))
    o["pk10r"] = every(a["bo"])
    a = {k[7:]: np.asarray(v) for k, v in I.items() if k.startswith("L3_ffn_")}
    o["pk11"] = cat(seg(a["wq"], a["wk"], a["wv"]), ch(a["wo"]), cols(a["ln1_g"]), cols(a["ln1_b"]), cols(a["ln2_g"]), cols(a["ln2_b"]),
                    ch(a["wr"]))
    o["pk11r"] = every(cat(seg_row(a["bq"], a["bk"], a["bv"]), a["bo"].reshape(1, 256)))
    o["pk11e"] = np.stack([cat(ch(a["w1"][e]), cols(a["b1"][e]), ch(a["w2"][e]), every(a["b2"][e])) for e in range(8)])
    return {k: np.ascontiguousarray(v) for k, v in o.items()}


def kernel(**inputs):
    import concourse.bacc as _bacc
    from concourse import mybir as _mybir
    from concourse.bass_utils import run_bass_kernel_spmd as _run

    nc = _bacc.Bacc("TRN2", target_bir_lowering=False, num_devices=1)
    arrays = layout(inputs)
    ins = {}
    for name, a in arrays.items():
        ins[name] = nc.dram_tensor(f"in_{name}", a.shape, _mybir.dt.from_np(a.dtype), kind="ExternalInput").ap()
    out = nc.dram_tensor("out_0", (2, 1024, 256), _mybir.dt.float32, kind="ExternalOutput").ap()
    build(nc, ins, out, range(12))
    r = _run(nc, [{f"in_{k}": v for k, v in arrays.items()}], core_ids=[0])
    return r.results[0]["out_0"]
```
